# Optimizing a Trainium2 kernel written in Bass

```python
import numpy as np
import jax
import jax.numpy as jnp

def _softmax(x, axis=-1):
    return jax.nn.softmax(x, axis=axis)

def _gelu(x):
    return jax.nn.gelu(x, approximate=True)

def _silu(x):
    return jax.nn.silu(x)

def _sigmoid(x):
    return jax.nn.sigmoid(x)

def _layernorm(x, axis=-1, eps=1e-05):
    m = jnp.mean(x, axis=axis, keepdims=True)
    v = jnp.var(x, axis=axis, keepdims=True)
    return (x - m) / jnp.sqrt(v + eps)

def _scatter_add(tgt, idx, src, axis=0):
    return tgt.at[idx].add(src)

def _segment_sum(src, seg, n):
    return jax.ops.segment_sum(src, seg, n)
kernel_name = 'mk_macaron_d2_jaxref_r8_92b9a9'

def setup_inputs(seed: int=0):
    np.random.seed(seed)
    _w = jnp.asarray

    def _L0_attn_setup():
        import jax, jax.numpy as jnp
        import numpy as np
        B, N, D = (2, 512, 128)
        DS = 128
        H = 512
        EPS = 1e-05

        def _layernorm(x, w, b):
            mu = jnp.mean(x, axis=-1, keepdims=True)
            var = jnp.mean((x - mu) ** 2, axis=-1, keepdims=True)
            return (x - mu) * jax.lax.rsqrt(var + EPS) * w + b

        def _selective_scan(deltaA, deltaB_u):

            def step(h, inp):
                dA, dBu = inp
                h = dA * h + dBu
                return (h, h)
            h0 = jnp.zeros((deltaB_u.shape[0], deltaB_u.shape[2]), deltaB_u.dtype)
            _, ys = jax.lax.scan(step, h0, (jnp.swapaxes(deltaA, 0, 1), jnp.swapaxes(deltaB_u, 0, 1)))
            return jnp.swapaxes(ys, 0, 1)

        def _forward(x, norm1_w, norm1_b, gate_w, gate_b, state_w, state_b, out_w, out_b, norm2_w, norm2_b, mlp_w1, mlp_b1, mlp_w2, mlp_b2):
            xn = _layernorm(x, norm1_w, norm1_b)
            g = xn @ gate_w + gate_b
            gate, gate_gate = jnp.split(g, 2, axis=-1)
            gate = jax.nn.silu(gate)
            gate_gate = jax.nn.silu(gate_gate)
            u = xn * gate @ state_w + state_b
            Bm = gate_gate @ state_w + state_b
            delta = jax.nn.softplus(jnp.mean(xn @ state_w + state_b, axis=-1, keepdims=True))
            deltaA = jnp.exp(-delta)
            deltaB_u = delta * Bm * u
            y = _selective_scan(deltaA, deltaB_u)
            ssm_out = y @ out_w + out_b
            x = x + ssm_out
            x2 = _layernorm(x, norm2_w, norm2_b)
            mlp = jax.nn.gelu(x2 @ mlp_w1 + mlp_b1, approximate=False) @ mlp_w2 + mlp_b2
            return x + mlp
        key = jax.random.key(seed)
        ks = jax.random.split(key, 12)
        s = 0.02
        p = lambda k, shape: jax.random.normal(k, shape, jnp.float32) * s
        return {'x': jax.random.normal(ks[0], (B, N, D), jnp.float32), 'norm1_w': jnp.ones((D,), jnp.float32), 'norm1_b': jnp.zeros((D,), jnp.float32), 'gate_w': p(ks[1], (D, 2 * D)), 'gate_b': p(ks[2], (2 * D,)), 'state_w': p(ks[3], (D, DS)), 'state_b': p(ks[4], (DS,)), 'out_w': p(ks[5], (DS, D)), 'out_b': p(ks[6], (D,)), 'norm2_w': jnp.ones((D,), jnp.float32), 'norm2_b': jnp.zeros((D,), jnp.float32), 'mlp_w1': p(ks[7], (D, H)), 'mlp_b1': p(ks[8], (H,)), 'mlp_w2': p(ks[9], (H, D)), 'mlp_b2': p(ks[10], (D,))}
    _L0_attn_in = _L0_attn_setup()

    def _L0_ffn_setup():
        import jax, jax.numpy as jnp
        import numpy as np
        NUM_EXPERTS = 8
        TOP_K = 2
        D = 128
        H = 4 * D
        B, S = (4, 256)
        key = jax.random.key(seed)
        ks = jax.random.split(key, 8)
        s = 0.02
        return {'x': jax.random.normal(ks[0], (B, S, D), dtype=jnp.float32), 'gate_w': jax.random.normal(ks[1], (NUM_EXPERTS, D), dtype=jnp.float32) * s, 'gate_b': jnp.zeros((NUM_EXPERTS,), dtype=jnp.float32), 'w1': jax.random.normal(ks[2], (NUM_EXPERTS, D, H), dtype=jnp.float32) * s, 'b1': jnp.zeros((NUM_EXPERTS, H), dtype=jnp.float32), 'w2': jax.random.normal(ks[3], (NUM_EXPERTS, H, D), dtype=jnp.float32) * s, 'b2': jnp.zeros((NUM_EXPERTS, D), dtype=jnp.float32)}
    _L0_ffn_in = _L0_ffn_setup()

    def _L1_attn_setup():
        import jax, jax.numpy as jnp
        import numpy as np
        L = 2
        D = 128
        H = 8
        DK = D // H
        DV = D // H
        T = 256
        B = 4
        INTER = 352
        EPS = 1e-06

        def rmsnorm(x, w):
            return x * jax.lax.rsqrt(jnp.mean(x * x, axis=-1, keepdims=True) + EPS) * w

        def l2norm(x):
            return x * jax.lax.rsqrt(jnp.sum(x * x, axis=-1, keepdims=True) + EPS)

        def delta_attn(x, Wq, Wk, Wv, Wb, Wo, onorm_w):
            b, t, _ = x.shape
            q = jax.nn.silu((x @ Wq).reshape(b, t, H, DK))
            k = jax.nn.silu((x @ Wk).reshape(b, t, H, DK))
            q = l2norm(q)
            k = l2norm(k)
            v = jax.nn.silu((x @ Wv).reshape(b, t, H, DV))
            beta = jax.nn.sigmoid(x @ Wb) * 2.0
            qt = q.transpose(1, 0, 2, 3)
            kt = k.transpose(1, 0, 2, 3)
            vt = v.transpose(1, 0, 2, 3)
            bt = beta.transpose(1, 0, 2)

            def step(S, inps):
                qi, ki, vi, bi = inps
                pred = jnp.einsum('bhkv,bhk->bhv', S, ki)
                S = S + bi[..., None, None] * ki[..., :, None] * (vi - pred)[..., None, :]
                o = jnp.einsum('bhkv,bhk->bhv', S, qi)
                return (S, o)
            S0 = jnp.zeros((b, H, DK, DV), x.dtype)
            _, o = jax.lax.scan(step, S0, (qt, kt, vt, bt))
            o = rmsnorm(o, onorm_w)
            o = o.transpose(1, 0, 2, 3).reshape(b, t, H * DV)
            return o @ Wo
        key = jax.random.key(seed)
        ks = jax.random.split(key, 13)
        s = 0.02
        f32 = jnp.float32
        return {'input_embeds': jax.random.normal(ks[0], (T, B, D), f32), 'Wq': jax.random.normal(ks[1], (L, D, D), f32) * s, 'Wk': jax.random.normal(ks[2], (L, D, D), f32) * s, 'Wv': jax.random.normal(ks[3], (L, D, D), f32) * s, 'Wb': jax.random.normal(ks[4], (L, D, H), f32) * s, 'Wo': jax.random.normal(ks[5], (L, D, D), f32) * s, 'onorm_w': jnp.ones((L, DV), f32) + jax.random.normal(ks[6], (L, DV), f32) * 0.02, 'norm1_w': jnp.ones((L, D), f32) + jax.random.normal(ks[7], (L, D), f32) * 0.02, 'norm2_w': jnp.ones((L, D), f32) + jax.random.normal(ks[8], (L, D), f32) * 0.02, 'Wg': jax.random.normal(ks[9], (L, D, 2 * INTER), f32) * s, 'Wd': jax.random.normal(ks[10], (L, INTER, D), f32) * s, 'final_norm_w': jnp.ones((D,), f32) + jax.random.normal(ks[11], (D,), f32) * 0.02}
    _L1_attn_in = _L1_attn_setup()

    def _L1_ffn_setup():
        import jax, jax.numpy as jnp
        import numpy as np
        B, SEQ, DIM = (2, 512, 128)
        E, S = (8, 64)
        HID = 4 * DIM
        SCALE = DIM ** 0.5

        def rmsnorm(x, gamma):
            n = jnp.linalg.norm(x, axis=-1, keepdims=True)
            return x / jnp.maximum(n, 1e-12) * SCALE * gamma
        key = jax.random.key(seed)
        ks = jax.random.split(key, 4)
        w_init = lambda k, shape: jax.random.normal(k, shape, dtype=jnp.float32) * 0.02
        return {'x': jax.random.normal(ks[0], (B, SEQ, DIM), dtype=jnp.float32), 'norm_gamma': jnp.ones((DIM,), jnp.float32), 'slot_norm_gamma': jnp.ones((DIM,), jnp.float32), 'slot_embeds': jax.random.normal(ks[1], (E, S, DIM), dtype=jnp.float32), 'w1': w_init(ks[2], (E, DIM, HID)), 'b1': jnp.zeros((E, HID), jnp.float32), 'w2': w_init(ks[3], (E, HID, DIM)), 'b2': jnp.zeros((E, DIM), jnp.float32)}
    _L1_ffn_in = _L1_ffn_setup()
    _d = {'L0_attn_x': _L0_attn_in['x'], 'L0_attn_norm1_w': _L0_attn_in['norm1_w'], 'L0_attn_norm1_b': _L0_attn_in['norm1_b'], 'L0_attn_gate_w': _L0_attn_in['gate_w'], 'L0_attn_gate_b': _L0_attn_in['gate_b'], 'L0_attn_state_w': _L0_attn_in['state_w'], 'L0_attn_state_b': _L0_attn_in['state_b'], 'L0_attn_out_w': _L0_attn_in['out_w'], 'L0_attn_out_b': _L0_attn_in['out_b'], 'L0_attn_norm2_w': _L0_attn_in['norm2_w'], 'L0_attn_norm2_b': _L0_attn_in['norm2_b'], 'L0_attn_mlp_w1': _L0_attn_in['mlp_w1'], 'L0_attn_mlp_b1': _L0_attn_in['mlp_b1'], 'L0_attn_mlp_w2': _L0_attn_in['mlp_w2'], 'L0_attn_mlp_b2': _L0_attn_in['mlp_b2'], 'L0_ffn_gate_w': _L0_ffn_in['gate_w'], 'L0_ffn_gate_b': _L0_ffn_in['gate_b'], 'L0_ffn_w1': _L0_ffn_in['w1'], 'L0_ffn_b1': _L0_ffn_in['b1'], 'L0_ffn_w2': _L0_ffn_in['w2'], 'L0_ffn_b2': _L0_ffn_in['b2'], 'L1_attn_Wq': _L1_attn_in['Wq'], 'L1_attn_Wk': _L1_attn_in['Wk'], 'L1_attn_Wv': _L1_attn_in['Wv'], 'L1_attn_Wb': _L1_attn_in['Wb'], 'L1_attn_Wo': _L1_attn_in['Wo'], 'L1_attn_onorm_w': _L1_attn_in['onorm_w'], 'L1_attn_norm1_w': _L1_attn_in['norm1_w'], 'L1_attn_norm2_w': _L1_attn_in['norm2_w'], 'L1_attn_Wg': _L1_attn_in['Wg'], 'L1_attn_Wd': _L1_attn_in['Wd'], 'L1_attn_final_norm_w': _L1_attn_in['final_norm_w'], 'L1_ffn_norm_gamma': _L1_ffn_in['norm_gamma'], 'L1_ffn_slot_norm_gamma': _L1_ffn_in['slot_norm_gamma'], 'L1_ffn_slot_embeds': _L1_ffn_in['slot_embeds'], 'L1_ffn_w1': _L1_ffn_in['w1'], 'L1_ffn_b1': _L1_ffn_in['b1'], 'L1_ffn_w2': _L1_ffn_in['w2'], 'L1_ffn_b2': _L1_ffn_in['b2']}
    _x0 = _d['L0_attn_x']
    _d['L0_attn_x'] = jax.random.normal(jax.random.fold_in(jax.random.key(seed), 1), (4, 512, 128), dtype=_x0.dtype)
    del _x0
    return _d

def reference(L0_attn_x, L0_attn_norm1_w, L0_attn_norm1_b, L0_attn_gate_w, L0_attn_gate_b, L0_attn_state_w, L0_attn_state_b, L0_attn_out_w, L0_attn_out_b, L0_attn_norm2_w, L0_attn_norm2_b, L0_attn_mlp_w1, L0_attn_mlp_b1, L0_attn_mlp_w2, L0_attn_mlp_b2, L0_ffn_gate_w, L0_ffn_gate_b, L0_ffn_w1, L0_ffn_b1, L0_ffn_w2, L0_ffn_b2, L1_attn_Wq, L1_attn_Wk, L1_attn_Wv, L1_attn_Wb, L1_attn_Wo, L1_attn_onorm_w, L1_attn_norm1_w, L1_attn_norm2_w, L1_attn_Wg, L1_attn_Wd, L1_attn_final_norm_w, L1_ffn_norm_gamma, L1_ffn_slot_norm_gamma, L1_ffn_slot_embeds, L1_ffn_w1, L1_ffn_b1, L1_ffn_w2, L1_ffn_b2):

    def _L0_attn_ref(x, norm1_w, norm1_b, gate_w, gate_b, state_w, state_b, out_w, out_b, norm2_w, norm2_b, mlp_w1, mlp_b1, mlp_w2, mlp_b2):
        import jax, jax.numpy as jnp
        import numpy as np
        B, N, D = (2, 512, 128)
        DS = 128
        H = 512
        EPS = 1e-05

        def _layernorm(x, w, b):
            mu = jnp.mean(x, axis=-1, keepdims=True)
            var = jnp.mean((x - mu) ** 2, axis=-1, keepdims=True)
            return (x - mu) * jax.lax.rsqrt(var + EPS) * w + b

        def _selective_scan(deltaA, deltaB_u):

            def step(h, inp):
                dA, dBu = inp
                h = dA * h + dBu
                return (h, h)
            h0 = jnp.zeros((deltaB_u.shape[0], deltaB_u.shape[2]), deltaB_u.dtype)
            _, ys = jax.lax.scan(step, h0, (jnp.swapaxes(deltaA, 0, 1), jnp.swapaxes(deltaB_u, 0, 1)))
            return jnp.swapaxes(ys, 0, 1)

        def _forward(x, norm1_w, norm1_b, gate_w, gate_b, state_w, state_b, out_w, out_b, norm2_w, norm2_b, mlp_w1, mlp_b1, mlp_w2, mlp_b2):
            xn = _layernorm(x, norm1_w, norm1_b)
            g = xn @ gate_w + gate_b
            gate, gate_gate = jnp.split(g, 2, axis=-1)
            gate = jax.nn.silu(gate)
            gate_gate = jax.nn.silu(gate_gate)
            u = xn * gate @ state_w + state_b
            Bm = gate_gate @ state_w + state_b
            delta = jax.nn.softplus(jnp.mean(xn @ state_w + state_b, axis=-1, keepdims=True))
            deltaA = jnp.exp(-delta)
            deltaB_u = delta * Bm * u
            y = _selective_scan(deltaA, deltaB_u)
            ssm_out = y @ out_w + out_b
            x = x + ssm_out
            x2 = _layernorm(x, norm2_w, norm2_b)
            mlp = jax.nn.gelu(x2 @ mlp_w1 + mlp_b1, approximate=False) @ mlp_w2 + mlp_b2
            return x + mlp
        return _forward(x, norm1_w, norm1_b, gate_w, gate_b, state_w, state_b, out_w, out_b, norm2_w, norm2_b, mlp_w1, mlp_b1, mlp_w2, mlp_b2)

    def _L0_ffn_ref(x, gate_w, gate_b, w1, b1, w2, b2):
        import jax, jax.numpy as jnp
        import numpy as np
        NUM_EXPERTS = 8
        TOP_K = 2
        D = 128
        H = 4 * D
        B, S = (4, 256)
        orig_shape = x.shape
        xf = x.reshape(-1, orig_shape[-1])
        gates = xf @ gate_w.T + gate_b
        weights, indices = jax.lax.top_k(gates, TOP_K)
        weights = jax.nn.softmax(weights, axis=-1)
        out = jnp.zeros_like(xf)
        for e in range(NUM_EXPERTS):
            w_e = jnp.sum(weights * (indices == e), axis=-1, keepdims=True)
            h = jax.nn.gelu(xf @ w1[e] + b1[e], approximate=False)
            out = out + w_e * (h @ w2[e] + b2[e])
        return out.reshape(orig_shape)

    def _L1_attn_ref(input_embeds, Wq, Wk, Wv, Wb, Wo, onorm_w, norm1_w, norm2_w, Wg, Wd, final_norm_w):
        import jax, jax.numpy as jnp
        import numpy as np
        L = 2
        D = 128
        H = 8
        DK = D // H
        DV = D // H
        T = 256
        B = 4
        INTER = 352
        EPS = 1e-06

        def rmsnorm(x, w):
            return x * jax.lax.rsqrt(jnp.mean(x * x, axis=-1, keepdims=True) + EPS) * w

        def l2norm(x):
            return x * jax.lax.rsqrt(jnp.sum(x * x, axis=-1, keepdims=True) + EPS)

        def delta_attn(x, Wq, Wk, Wv, Wb, Wo, onorm_w):
            b, t, _ = x.shape
            q = jax.nn.silu((x @ Wq).reshape(b, t, H, DK))
            k = jax.nn.silu((x @ Wk).reshape(b, t, H, DK))
            q = l2norm(q)
            k = l2norm(k)
            v = jax.nn.silu((x @ Wv).reshape(b, t, H, DV))
            beta = jax.nn.sigmoid(x @ Wb) * 2.0
            qt = q.transpose(1, 0, 2, 3)
            kt = k.transpose(1, 0, 2, 3)
            vt = v.transpose(1, 0, 2, 3)
            bt = beta.transpose(1, 0, 2)

            def step(S, inps):
                qi, ki, vi, bi = inps
                pred = jnp.einsum('bhkv,bhk->bhv', S, ki)
                S = S + bi[..., None, None] * ki[..., :, None] * (vi - pred)[..., None, :]
                o = jnp.einsum('bhkv,bhk->bhv', S, qi)
                return (S, o)
            S0 = jnp.zeros((b, H, DK, DV), x.dtype)
            _, o = jax.lax.scan(step, S0, (qt, kt, vt, bt))
            o = rmsnorm(o, onorm_w)
            o = o.transpose(1, 0, 2, 3).reshape(b, t, H * DV)
            return o @ Wo
        x = input_embeds.transpose(1, 0, 2)
        for l in range(L):
            h = rmsnorm(x, norm1_w[l])
            x = x + delta_attn(h, Wq[l], Wk[l], Wv[l], Wb[l], Wo[l], onorm_w[l])
            h = rmsnorm(x, norm2_w[l])
            gy = h @ Wg[l]
            g, y = jnp.split(gy, 2, axis=-1)
            x = x + jax.nn.silu(g) * y @ Wd[l]
        x = rmsnorm(x, final_norm_w)
        return x.transpose(1, 0, 2)

    def _L1_ffn_ref(x, norm_gamma, slot_norm_gamma, slot_embeds, w1, b1, w2, b2):
        import jax, jax.numpy as jnp
        import numpy as np
        B, SEQ, DIM = (2, 512, 128)
        E, S = (8, 64)
        HID = 4 * DIM
        SCALE = DIM ** 0.5

        def rmsnorm(x, gamma):
            n = jnp.linalg.norm(x, axis=-1, keepdims=True)
            return x / jnp.maximum(n, 1e-12) * SCALE * gamma
        xn = rmsnorm(x, norm_gamma)
        sn = rmsnorm(slot_embeds, slot_norm_gamma)
        logits = jnp.einsum('bnd,esd->bnes', xn, sn)
        dispatch = jax.nn.softmax(logits, axis=1)
        b, n, e, s = logits.shape
        combine = jax.nn.softmax(logits.reshape(b, n, e * s), axis=-1)
        slots = jnp.einsum('bnd,bnes->besd', xn, dispatch)
        h = jnp.einsum('besd,edh->besh', slots, w1) + b1[None, :, None, :]
        h = jax.nn.gelu(h, approximate=False)
        eo = jnp.einsum('besh,ehd->besd', h, w2) + b2[None, :, None, :]
        eo = eo.reshape(b, e * s, DIM)
        out = jnp.einsum('bmd,bnm->bnd', eo, combine)
        return out
    x = L0_attn_x
    x = x + 0.5 * _L0_ffn_ref(_layernorm(x, axis=-1), L0_ffn_gate_w, L0_ffn_gate_b, L0_ffn_w1, L0_ffn_b1, L0_ffn_w2, L0_ffn_b2)
    x = x + _L0_attn_ref(_layernorm(x, axis=-1), L0_attn_norm1_w, L0_attn_norm1_b, L0_attn_gate_w, L0_attn_gate_b, L0_attn_state_w, L0_attn_state_b, L0_attn_out_w, L0_attn_out_b, L0_attn_norm2_w, L0_attn_norm2_b, L0_attn_mlp_w1, L0_attn_mlp_b1, L0_attn_mlp_w2, L0_attn_mlp_b2)
    x = x + 0.5 * _L0_ffn_ref(_layernorm(x, axis=-1), L0_ffn_gate_w, L0_ffn_gate_b, L0_ffn_w1, L0_ffn_b1, L0_ffn_w2, L0_ffn_b2)
    x = x + 0.5 * _L1_ffn_ref(_layernorm(x, axis=-1), L1_ffn_norm_gamma, L1_ffn_slot_norm_gamma, L1_ffn_slot_embeds, L1_ffn_w1, L1_ffn_b1, L1_ffn_w2, L1_ffn_b2)
    x = x + _L1_attn_ref(_layernorm(x, axis=-1), L1_attn_Wq, L1_attn_Wk, L1_attn_Wv, L1_attn_Wb, L1_attn_Wo, L1_attn_onorm_w, L1_attn_norm1_w, L1_attn_norm2_w, L1_attn_Wg, L1_attn_Wd, L1_attn_final_norm_w)
    x = x + 0.5 * _L1_ffn_ref(_layernorm(x, axis=-1), L1_ffn_norm_gamma, L1_ffn_slot_norm_gamma, L1_ffn_slot_embeds, L1_ffn_w1, L1_ffn_b1, L1_ffn_w2, L1_ffn_b2)
    return x

_drawn_inputs = setup_inputs


def setup_inputs(seed=0):
    import zlib

    import numpy as np

    out = dict(_drawn_inputs(seed))
    spreads = {'L0_attn_norm1_w': (1.0, 0.6),
     'L0_attn_norm1_b': (0.0, 0.8),
     'L0_attn_norm2_w': (1.0, 0.6),
     'L0_attn_norm2_b': (0.0, 2.0),
     'L0_ffn_gate_b': (0.0, 0.1),
     'L0_ffn_b1': (0.0, 0.585),
     'L0_ffn_b2': (0.0, 0.1),
     'L1_ffn_norm_gamma': (1.0, 0.6),
     'L1_ffn_slot_norm_gamma': (1.0, 0.6),
     'L1_ffn_b1': (0.0, 2.0),
     'L1_ffn_b2': (0.0, 0.8)}
    factors = {'L0_attn_gate_w': 8.0,
     'L0_attn_gate_b': 8.0,
     'L0_attn_state_w': 8.0,
     'L0_attn_state_b': 8.0,
     'L0_attn_out_w': 8.0,
     'L0_attn_out_b': 28.412,
     'L0_attn_mlp_b1': 64.0,
     'L0_attn_mlp_b2': 36.824,
     'L1_attn_Wb': 8.0,
     'L1_attn_onorm_w': 52.239,
     'L1_attn_norm1_w': 7.585,
     'L1_attn_norm2_w': 46.317,
     'L1_attn_Wg': 8.0,
     'L1_attn_Wd': 8.0,
     'L1_attn_final_norm_w': 177.696,
     'L1_ffn_w1': 11.737,
     'L0_attn_mlp_w1': 5.534,
     'L0_attn_mlp_w2': 5.371,
     'L1_ffn_slot_embeds': 3.411,
     'L1_ffn_w2': 3.27}
    for name, (base, spread) in spreads.items():
        noise = np.random.default_rng([zlib.crc32(name.encode()), seed]).standard_normal(out[name].shape)
        drawn = base * np.exp(spread * noise) if base else spread * noise
        out[name] = jnp.asarray(drawn.astype(out[name].dtype))
    for name, factor in factors.items():
        out[name] = (out[name] * factor).astype(out[name].dtype)
    return out
```

```python
from contextlib import ExitStack

import concourse.bass as bass
from concourse import mybir

STAGES = 6
P = 128
T = 16
C = 4
JT = 4
CH = JT * P
E = 8
S_PER = 64
NB = C * S_PER
SCALE = float(P) ** 0.5
H = 8
DK = P // H
LAYERS = 2
FF = 352
FB = [(0, 128), (128, 128), (256, 96)]
HK = 4

F32 = mybir.dt.float32
F32R = mybir.dt.float32r
I32 = mybir.dt.int32
ALU = mybir.AluOpType
ACT = mybir.ActivationFunctionType
AX_X = mybir.AxisListType.X
RSQRT_MAGIC = float(0x5F3759DF)


def program(nc, A, out):
    with ExitStack() as ctx:
        def sb(name, shape, dt=F32):
            return ctx.enter_context(nc.sbuf_tensor(name, shape, dt))

        def sem(name):
            return ctx.enter_context(nc.semaphore(name))

        bank = [ctx.enter_context(nc.psum_tensor(f"bank{i}", [P, CH], F32)) for i in range(8)]
        ident = sb("ident", [P, P])
        X = sb("X", [P, T, P])
        XH = sb("XH", [P, T, P])
        stats = sb("stats", [P, T, 6])
        mv = sb("mv", [P, T, 2])
        rs = sb("rs", [P, 8, T])
        xTh = sb("xTh", [P, C, CH], F32R)
        xTl = sb("xTl", [P, C, CH], F32R)
        arena = sb("arena", [P, 40, CH])
        hh = sb("hh", [P, 2, HK, CH], F32R)
        hl = sb("hl", [P, 2, HK, CH], F32R)
        wraw = [sb(f"wraw{p}", [P, 2, CH]) for p in range(2)]
        wh = [sb(f"wh{p}", [P, 2, CH], F32R) for p in range(2)]
        wl = [sb(f"wl{p}", [P, 2, CH], F32R) for p in range(2)]

        U = sb("U", [P, T, P])

        COLS = {}
        n_cols = 0
        for name, ref, k in (
            ("n1w", "L0_attn_norm1_w", 1), ("n1b", "L0_attn_norm1_b", 1), ("gate_b", "L0_attn_gate_b", 2),
            ("state_b", "L0_attn_state_b", 1), ("n2w", "L0_attn_norm2_w", 1), ("n2b", "L0_attn_norm2_b", 1),
            ("mlp_b1", "L0_attn_mlp_b1", HK), ("mlp_b2", "L0_attn_mlp_b2", 1), ("gamma", "L1_ffn_norm_gamma", 1),
            ("slot_gamma", "L1_ffn_slot_norm_gamma", 1), ("r1w", "L1_attn_norm1_w", 2), ("r2w", "L1_attn_norm2_w", 2),
            ("b1_0", "L0_ffn_b1", E * HK), ("b2_0", "L0_ffn_b2", E), ("b1_1", "L1_ffn_b1", E * HK),
            ("b2_1", "L1_ffn_b2", E), ("onorm", None, 2),
        ):
            COLS[name] = (n_cols, k, ref)
            n_cols += k
        vrows = sb("vrows", [n_cols, P])
        vcols = sb("vcols", [P, n_cols])

        def col(name, k=0):
            at = COLS[name][0] + k
            return vcols[:, at:at + 1]

        def cols_of(name):
            at, k, _ = COLS[name]
            return vcols[:, at:at + k]

        gate_w = sb("gate_w", [P, 2 * P])
        state_w = sb("state_w", [P, P])
        out_w = sb("out_w", [P, P])
        outb_row = sb("outb_row", [P, P])
        stateb_row = sb("stateb_row", [P, P])
        mlp_w1 = sb("mlp_w1", [P, CH])
        mlp_w2 = sb("mlp_w2", [P, HK, P])
        sbar = sb("sbar", [P, 2])

        qkvb = sb("qkvb", [P, LAYERS, 3 * P + H])
        wo = sb("wo", [P, LAYERS, P])
        wg = sb("wg", [P, LAYERS, 2 * FF])
        wd = sb("wd", [P, LAYERS, 3, P])
        final_row = sb("final_row", [P, P])

        snT = sb("snT", [P, CH])
        slotsT = U[:].rearrange("p t d -> p (t d)").rearrange("p (e b s) -> p e b s", e=E, b=C)
        nmax = sb("nmax", [P, C, 8])
        sums = sb("sums", [P, C, 8])

        tri = sb("tri", [P, E, E])
        gwraw = sb("gwraw", [E, P])
        gwh = sb("gwh", [P, E], F32R)
        gwl = sb("gwl", [P, E], F32R)
        gb_row = sb("gb_row", [P, E])
        b1col = sb("b1col", [P, 2, HK])
        G = sb("G", [P, T, E])
        WE = sb("WE", [P, E, T])
        gsm = sb("gsm", [P, 4, T, E])
        wcol = sb("wcol", [P, 2, T])

        ybank = (bank[5], bank[7])
        acc = arena[:, 0:4, :]
        hf = arena[:, 4:12, :]
        wbs = arena[:, 12:14, :]
        tmp = arena[:, 14:16, :]

        b1T, b2T = cols_of("b1_0"), cols_of("b2_0")

        s_x = sem("s_x")
        s_w0 = sem("s_w0")
        s_const = sem("s_const")
        s_zero = sem("s_zero")
        s_small = sem("s_small")
        s_out = sem("s_out")
        x_ready = sem("x_ready")
        dve_chain = sem("dve_chain")
        pool_chain = sem("pool_chain")
        b_turned = sem("b_turned")
        b_copied = sem("b_copied")

        chain_at = {"dve": 0, "pool": 0}

        def link(ins):
            chain_at["dve"] += 1
            ins.then_inc(dve_chain, 1)
            nc.vector.wait_ge(dve_chain, chain_at["dve"])

        def moe_sems(n):
            names = ("xh_ready xt_turned xt_hi xt_lo gates_done logits_ready exp_ready wcol_ready w_split g1_done "
                     "hf_ready hh_ready hl_dve hl_pool wb_done wb_copied g2_done y_ready acc_done "
                     "w_hi acc_turned wload0 wload1 b1_ready").split()
            return {k: sem(f"{k}_{n}") for k in names}

        M = [moe_sems("moe0"), moe_sems("moe1")]
        B = {k: sem(k + "_ssm") for k in (
            "xh_ready xt_turned xt_ready z_done z_abs z_exp z_ln delta_ready decay_ready bc_done bc_copied g_done silu_ready "
            "xg_ready ub_done scan_ready u_b_ready ssm_done x1_ready xh2_ready x2_turned x2_ready g1_done hf_ready y_done "
            "y_copied yt_done xu_ready").split()}

        def dve_rsqrt(y, v, t):
            link(nc.vector.tensor_scalar(t.bitcast(I32), v.bitcast(I32), 1, None, ALU.logical_shift_right))
            link(nc.vector.tensor_scalar(y.bitcast(I32), t.bitcast(I32), -1.0, RSQRT_MAGIC, ALU.mult, ALU.add))
            for _ in range(4):
                link(nc.vector.scalar_tensor_tensor(out=t, in0=y, scalar=-0.5, in1=y, op0=ALU.mult, op1=ALU.mult))
                link(nc.vector.tensor_tensor(t, t, v, ALU.mult))
                link(nc.vector.scalar_tensor_tensor(out=y, in0=t, scalar=1.5, in1=y, op0=ALU.add, op1=ALU.mult))

        def dve_stats(src, done, at):
            for t in range(T):
                if t % JT == 0 and at is not None:
                    nc.vector.wait_ge(done, at + t // JT + 1)
                last = nc.vector.bn_stats(stats[:, t, :], src[:, t, :])
            link(last)
            for t in range(T):
                last = nc.vector.bn_aggr(mv[:, t, :], stats[:, t, :])
            link(last)

        def row(k):
            return rs[:, k, :]

        def moe_dve(S, k):
            if k == 0:
                nc.vector.wait_ge(s_x, 16 * C)
            dve_stats(X, x_ready, None if k == 0 else C)
            link(nc.vector.tensor_scalar(row(1), mv[:, :, 1], 1e-5, None, ALU.add))
            dve_rsqrt(row(0), row(1), row(2))
            for t in range(T):
                nc.vector.tensor_scalar(XH[:, t, :], X[:, t, :], mv[:, t, 0:1], rs[:, 0, t:t + 1],
                                        ALU.subtract, ALU.mult).then_inc(S["xh_ready"], 1)
            nc.vector.tensor_copy(b1col[:, 0, :], b1T[:, 0:HK]).then_inc(S["b1_ready"], 1)
            nc.vector.wait_ge(S["wload0"], 32)
            for which in range(2):
                nc.vector.tensor_copy(wh[0][:, which, :], wraw[0][:, which, :]).then_inc(S["w_hi"], 1)
            for c in range(C):
                nc.vector.wait_ge(S["xt_hi"], c + 1)
                nc.vector.tensor_tensor(xTl[:, c, :], bank[c][:], xTh[:, c, :].bitcast(F32),
                                        ALU.subtract).then_inc(S["xt_lo"], 1)
            nc.vector.wait_ge(S["gates_done"], 1)
            glog = bank[6][:, 0:T * E].rearrange("p (t e) -> p t e", e=E)
            link(nc.vector.tensor_tensor(G[:], glog, gb_row[:].unsqueeze(1).to_broadcast([P, T, E]), ALU.add))
            link(nc.vector.tensor_reduce(row(3), G[:], AX_X, ALU.max))
            nc.vector.tensor_tensor(gsm[:, 0], G[:], row(3).unsqueeze(2).to_broadcast([P, T, E]),
                                    ALU.subtract).then_inc(S["logits_ready"], 1)
            for t0 in range(0, T, JT):
                g = G[:, t0:t0 + JT, :]
                gj = g.unsqueeze(2).to_broadcast([P, JT, E, E])
                ge_ = g.unsqueeze(3).to_broadcast([P, JT, E, E])
                before = arena[:, 16, 0:JT * E * E].rearrange("p (t e j) -> p t e j", e=E, j=E)
                equal = arena[:, 17, 0:JT * E * E].rearrange("p (t e j) -> p t e j", e=E, j=E)
                nc.vector.tensor_tensor(before, gj, ge_, ALU.is_gt)
                link(nc.vector.tensor_tensor(equal, gj, ge_, ALU.is_equal))
                link(nc.vector.tensor_tensor(equal, equal, tri[:].unsqueeze(1).to_broadcast([P, JT, E, E]), ALU.mult))
                link(nc.vector.tensor_tensor(before, before, equal, ALU.add))
                link(nc.vector.tensor_reduce(gsm[:, 1, t0:t0 + JT, :], before, AX_X, ALU.add))
            link(nc.vector.tensor_scalar(gsm[:, 1], gsm[:, 1], 2.0, None, ALU.is_lt))
            nc.vector.wait_ge(S["exp_ready"], 1)
            link(nc.vector.tensor_tensor(gsm[:, 1], gsm[:, 1], gsm[:, 2], ALU.mult))
            link(nc.vector.tensor_reduce(row(4), gsm[:, 1], AX_X, ALU.add))
            link(nc.vector.reciprocal(row(5), row(4)))
            link(nc.vector.tensor_tensor(WE[:].rearrange("p e t -> p t e"), gsm[:, 1],
                                         row(5).unsqueeze(2).to_broadcast([P, T, E]), ALU.mult))
            nc.vector.tensor_copy(wcol[:, 0, :], WE[:, 0, :]).then_inc(S["wcol_ready"], 1)

            nc.vector.sem_inc(S["hh_ready"], 5)
            nc.vector.sem_inc(S["hl_dve"], 3)
            nc.vector.sem_inc(S["y_ready"], 2)

            def split_hidden(s, q):
                nc.vector.wait_ge(S["g2_done"], s + 1)
                for m in range(HK):
                    nc.vector.wait_ge(S["hf_ready"], s * 4 + (m + 1))
                    nc.vector.tensor_copy(hh[:, q, m, :], hf[:, q * 4 + m, :]).then_inc(S["hh_ready"], 1)
                    if m < 2:
                        nc.vector.wait_ge(S["hh_ready"], s * 4 + (m + 6))
                        nc.vector.tensor_tensor(hl[:, q, m, :], hf[:, q * 4 + m, :], hh[:, q, m, :].bitcast(F32),
                                                ALU.subtract).then_inc(S["hl_dve"], 1)

            def body(i, last):
                for p in range(2):
                    for c in range(C):
                        q = c % 2
                        s = i * 8 + (4 * p + c)
                        more = not (last and p == 1)
                        if more or c < C - 1:
                            split_hidden(s + 1, 1 - q)
                        if c == 1 and more:
                            nc.vector.wait_ge(S["wload0"] if p else S["wload1"], i * 32 + (64 if p else 32))
                            nc.vector.wait_ge(S["g2_done"], i * 8 + (4 * p + 2))
                            for which in range(2):
                                nc.vector.tensor_copy(wh[1 - p][:, which, :], wraw[1 - p][:, which, :]
                                                      ).then_inc(S["w_hi"], 1)
                        if c == 2 and more:
                            n = i * 2 + (p + 1)
                            nc.vector.wait_ge(S["hf_ready"], i * 32 + (16 * p + 1))
                            nc.vector.tensor_scalar(wcol[:, 1 - p, :], WE[:, bass.ds(n, 1), :].squeeze(1), 1.0, None,
                                                    ALU.mult).then_inc(S["wcol_ready"], 1)
                            nc.vector.tensor_scalar(b1col[:, 1 - p, :], b1T[:, bass.ds(n * HK, HK)], 1.0, None,
                                                    ALU.mult).then_inc(S["b1_ready"], 1)
                        nc.vector.wait_ge(S["g2_done"], s + 3)
                        nc.vector.wait_ge(S["wb_copied"], s + 2)
                        nc.vector.wait_ge(S["acc_done"], s + 1)
                        nc.vector.scalar_tensor_tensor(
                            out=tmp[:, q, :], in0=ybank[q][:], scalar=b2T[:, bass.ds(i * 2 + p, 1)],
                            in1=wbs[:, q, :], op0=ALU.add, op1=ALU.mult).then_inc(S["y_ready"], 1)

            split_hidden(0, 0)
            with nc.vector.Fori(0, E // 2 - 1) as i:
                body(i, False)
            body(E // 2 - 1, True)
            for c in range(C):
                nc.vector.wait_ge(S["acc_turned"], c + 1)
                nc.vector.scalar_tensor_tensor(
                    out=X[:, JT * c:JT * c + JT, :], in0=bank[c][:].rearrange("p (t d) -> p t d", d=P),
                    scalar=0.5, in1=X[:, JT * c:JT * c + JT, :], op0=ALU.mult, op1=ALU.add).then_inc(x_ready, 1)

        def moe_act(S, k):
            for c in range(C):
                nc.scalar.wait_ge(S["xt_turned"], c + 1)
                nc.scalar.activation(xTh[:, c, :], bank[c][:], ACT.Copy).then_inc(S["xt_hi"], 1)
            nc.scalar.wait_ge(S["logits_ready"], 1)
            nc.scalar.activation(gsm[:, 2], gsm[:, 0], ACT.Exp).then_inc(S["exp_ready"], 1)
            nc.scalar.sem_inc(S["wb_copied"], 1)
            with nc.scalar.Fori(0, E // 2) as i:
                for p in range(2):
                    nc.scalar.wait_ge(S["b1_ready"], i * 2 + (p + 1))
                    for c in range(C):
                        q = c % 2
                        s = i * 8 + (4 * p + c)
                        nc.scalar.wait_ge(S["hh_ready"], s * 4 + 1)
                        nc.scalar.wait_ge(S["hl_dve"], s * 2 + 1)
                        nc.scalar.wait_ge(S["hl_pool"], s * 2 + 1)
                        for m in range(HK):
                            nc.scalar.wait_ge(S["g1_done"], s * 4 + (m + 1))
                            nc.scalar.activation(hf[:, q * 4 + m, :], bank[m][:], ACT.Gelu,
                                                 bias=b1col[:, p, m:m + 1]).then_inc(S["hf_ready"], 1)
                        nc.scalar.wait_ge(S["wb_done"], s + 1)
                        nc.scalar.wait_ge(S["y_ready"], s + 1)
                        nc.scalar.activation(wbs[:, q, :], bank[4][:], ACT.Copy).then_inc(S["wb_copied"], 1)

        def moe_pool(S, k):
            if k:
                nc.gpsimd.wait_ge(x_ready, 2 * C)
            nc.gpsimd.memset(acc, 0.0).then_inc(S["acc_done"], 2)
            nc.gpsimd.sem_inc(S["hl_pool"], 3)

            def split(p, which, e):
                src = wraw[p][:, which, :]
                nc.gpsimd.wait_ge(S["w_hi"], e * 2 + (which + 1))
                nc.gpsimd.tensor_tensor(wl[p][:, which, :], src, wh[p][:, which, :].bitcast(F32),
                                        ALU.subtract).then_inc(S["w_split"], 1)

            split(0, 0, 0)
            split(0, 1, 0)

            def low_hidden(s, q):
                for m in (2, 3):
                    if m == 2:
                        nc.gpsimd.wait_ge(S["g2_done"], s + 1)
                    nc.gpsimd.wait_ge(S["hh_ready"], s * 4 + (m + 6))
                    nc.gpsimd.tensor_tensor(hl[:, q, m, :], hf[:, q * 4 + m, :], hh[:, q, m, :].bitcast(F32),
                                            ALU.subtract).then_inc(S["hl_pool"], 1)

            def body(i, last):
                for p in range(2):
                    for c in range(C):
                        q = c % 2
                        s = i * 8 + (4 * p + c)
                        more = not (last and p == 1)
                        if more or c < C - 1:
                            low_hidden(s + 1, 1 - q)
                        if more and c in (1, 2):
                            split(1 - p, c - 1, i * 2 + (p + 1))
                        nc.gpsimd.wait_ge(S["y_ready"], s + 3)
                        nc.gpsimd.wait_ge(S["acc_done"], s + 2)
                        nc.gpsimd.tensor_tensor(acc[:, c, :], acc[:, c, :], tmp[:, q, :], ALU.add
                                                ).then_inc(S["acc_done"], 1)

            low_hidden(0, 0)
            with nc.gpsimd.Fori(0, E // 2 - 1) as i:
                body(i, False)
            body(E // 2 - 1, True)

        def mm3(o, ah, al, bh, bl, start, stop):
            nc.tensor.matmul(o, ah, bh, start=start, stop=False)
            nc.tensor.matmul(o, ah, bl, start=False, stop=False)
            return nc.tensor.matmul(o, al, bh, start=False, stop=stop)

        def moe_pe(S, k):
            nc.tensor.sem_inc(S["g2_done"], 2)
            for c in range(C):
                for j in range(JT):
                    t = JT * c + j
                    nc.tensor.wait_ge(S["xh_ready"], t + 1)
                    if t == 0 and k == 0:
                        nc.tensor.wait_ge(s_const, 1)
                    ins = nc.tensor.transpose(bank[c][:, j * P:(j + 1) * P], XH[:, t, :], ident[:])
                ins.then_inc(S["xt_turned"], 1)
            if k == 0:
                nc.tensor.wait_ge(b_copied, 3)
            nc.tensor.wait_ge(S["xt_hi"], C)
            nc.tensor.wait_ge(S["xt_lo"], C)
            for t in range(T):
                c, j = divmod(t, JT)
                ins = mm3(bank[6][:, t * E:(t + 1) * E], xTh[:, c, j * P:(j + 1) * P], xTl[:, c, j * P:(j + 1) * P],
                          gwh[:], gwl[:], True, True)
            ins.then_inc(S["gates_done"], 1)

            def g1(p, c, s, at_s):
                nc.tensor.wait_ge(S["w_split"], at_s)
                for m in range(HK):
                    nc.tensor.wait_ge(S["hf_ready"], s * 4 + (m - 3))
                    cols = slice(m * P, (m + 1) * P)
                    mm3(bank[m][:], wh[p][:, 0, cols], wl[p][:, 0, cols], xTh[:, c, :], xTl[:, c, :],
                        True, True).then_inc(S["g1_done"], 1)

            def step(i, p, c, more):
                q = c % 2
                s = i * 8 + (4 * p + c)
                nc.tensor.wait_ge(S["wcol_ready"], i * 2 + (p + 1))
                nc.tensor.wait_ge(S["wb_copied"], s + 1)
                for j in range(JT):
                    ins = nc.tensor.transpose(bank[4][:, j * P:(j + 1) * P],
                                              wcol[:, p, JT * c + j:JT * c + j + 1].to_broadcast([P, P]), ident[:])
                ins.then_inc(S["wb_done"], 1)
                if more:
                    p2, c2 = (p, c + 1) if c < C - 1 else (1 - p, 0)
                    e2 = i * 2 + (p + (1 if c == C - 1 else 0))
                    g1(p2, c2, s + 1, e2 * 2 + 2)
                nc.tensor.wait_ge(S["y_ready"], s + 1)
                for m in range(HK):
                    nc.tensor.wait_ge(S["hh_ready"], s * 4 + (m + 6))
                    if m < 2:
                        nc.tensor.wait_ge(S["hl_dve"], s * 2 + (m + 4))
                    else:
                        nc.tensor.wait_ge(S["hl_pool"], s * 2 + (m + 2))
                    cols = slice(m * P, (m + 1) * P)
                    ins = mm3(ybank[q][:], wh[p][:, 1, cols], wl[p][:, 1, cols], hh[:, q, m, :], hl[:, q, m, :],
                              m == 0, m == HK - 1)
                ins.then_inc(S["g2_done"], 1)

            nc.tensor.wait_ge(S["w_split"], 2)
            for m in range(HK):
                cols = slice(m * P, (m + 1) * P)
                mm3(bank[m][:], wh[0][:, 0, cols], wl[0][:, 0, cols], xTh[:, 0, :], xTl[:, 0, :],
                    True, True).then_inc(S["g1_done"], 1)
            with nc.tensor.Fori(0, E // 2 - 1) as i:
                for p in range(2):
                    for c in range(C):
                        step(i, p, c, True)
            for p in range(2):
                for c in range(C):
                    step(E // 2 - 1, p, c, not (p == 1 and c == C - 1))
            for c in range(C):
                nc.tensor.wait_ge(S["acc_done"], 2 + 4 * (E - 1) + c + 1)
                for j in range(JT):
                    ins = nc.tensor.transpose(bank[c][:, j * P:(j + 1) * P], acc[:, c, j * P:(j + 1) * P], ident[:])
                ins.then_inc(S["acc_turned"], 1)

        def moe_sp(S, k):
            w1, w2 = A["L0_ffn_w1"], A["L0_ffn_w2"].rearrange("e (m h) d -> e h m d", h=P)

            def load(e, p, wl_sem):
                nc.sync.dma_start(wraw[p][:, 0, :], w1[e, :, :] if isinstance(e, int) else
                                  w1[bass.ds(e, 1), :, :].squeeze(0)).then_inc(wl_sem, 16)
                dst = wraw[p][:, 1, :].rearrange("p (m d) -> p m d", d=P)
                nc.sync.dma_start(dst, w2[e, :, :, :] if isinstance(e, int) else
                                  w2[bass.ds(e, 1), :, :, :].squeeze(0)).then_inc(wl_sem, 16)

            if k:
                nc.sync.wait_ge(M[0]["w_split"], 2 * E)
            load(0, 0, S["wload0"])
            load(1, 1, S["wload1"])
            with nc.sync.Fori(0, E // 2 - 1) as i:
                nc.sync.wait_ge(S["w_split"], i * 4 + 2)
                load(i * 2 + 2, 0, S["wload0"])
                nc.sync.wait_ge(S["w_split"], i * 4 + 4)
                load(i * 2 + 3, 1, S["wload1"])

        xT = arena[:, 0:4, :]
        gate = arena[:, 4:8, :]
        gate2 = arena[:, 8:12, :]
        delta_b = arena[:, 12:16, :]
        decay_b = arena[:, 16:20, :]
        states = arena[:, 20:24, :]
        hid = arena[:, 24:32, :]
        yfm = arena[:, 32:34, :]
        dBu = arena[:, 34:36, :]
        zs = rs[:, 3:8, :]

        def ssm_dve():
            dve_stats(X, x_ready, 0)
            link(nc.vector.tensor_scalar(row(1), mv[:, :, 1], 1e-5, None, ALU.add))
            dve_rsqrt(row(0), row(1), row(2))
            for t in range(T):
                last = nc.vector.tensor_scalar(U[:, t, :], X[:, t, :], mv[:, t, 0:1], rs[:, 0, t:t + 1],
                                               ALU.subtract, ALU.mult)
            link(nc.vector.tensor_tensor(row(1), row(0), row(0), ALU.mult))
            link(nc.vector.tensor_tensor(row(1), row(1), mv[:, :, 1], ALU.mult))
            link(nc.vector.tensor_scalar(row(1), row(1), 1e-5, None, ALU.add))
            dve_rsqrt(row(0), row(1), row(2))
            for t in range(T):
                nc.vector.tensor_scalar(XH[:, t, :], U[:, t, :], rs[:, 0, t:t + 1], None,
                                        ALU.mult).then_inc(B["xh_ready"], 1)
            nc.vector.wait_ge(s_w0, 16 * 7)
            nc.vector.reduce_sum(sbar[:, 0:1], state_w[:], AX_X)
            link(nc.vector.reduce_sum(sbar[:, 1:2], stateb_row[:], AX_X))
            nc.vector.tensor_scalar(sbar[:, 1:2], sbar[:, 1:2], 1.0 / P, None, ALU.mult).then_inc(B["z_done"], 1)
            nc.vector.wait_ge(B["z_done"], 2)
            link(nc.vector.tensor_scalar(zs[:, 0], bank[7][:, 0:T], 1.0 / P, sbar[:, 1:2], ALU.mult, ALU.add))
            link(nc.vector.tensor_scalar(zs[:, 1], zs[:, 0], -1.0, None, ALU.mult))
            nc.vector.tensor_tensor(zs[:, 1], zs[:, 1], zs[:, 0], ALU.max).then_inc(B["z_abs"], 1)
            nc.vector.wait_ge(B["z_exp"], 1)
            w_, one = row(0), row(1)
            link(nc.vector.tensor_scalar(w_, zs[:, 2], 1.0, None, ALU.add))
            link(nc.vector.tensor_scalar(one, w_, 1.0, None, ALU.is_equal))
            link(nc.vector.scalar_tensor_tensor(out=w_, in0=w_, scalar=-1.0, in1=one, op0=ALU.add, op1=ALU.add))
            link(nc.vector.reciprocal(w_, w_))
            link(nc.vector.tensor_tensor(w_, w_, zs[:, 2], ALU.mult))
            nc.vector.wait_ge(B["z_ln"], 1)
            link(nc.vector.tensor_tensor(one, one, zs[:, 3], ALU.add))
            link(nc.vector.tensor_tensor(one, one, w_, ALU.mult))
            nc.vector.scalar_tensor_tensor(out=zs[:, 3], in0=zs[:, 0], scalar=0.0, in1=one, op0=ALU.max,
                                           op1=ALU.add).then_inc(B["delta_ready"], 1)
            for c in range(C):
                nc.vector.wait_ge(B["silu_ready"], 2 * c + 2)
                nc.vector.tensor_tensor(gate[:, c, :], gate[:, c, :], xT[:, c, :], ALU.mult).then_inc(B["xg_ready"], 1)
            for c in range(C):
                nc.vector.wait_ge(B["ub_done"], c + 1)
                nc.vector.wait_ge(B["bc_copied"], 2 * c + 2)
                link(nc.vector.scalar_tensor_tensor(out=dBu[:, 0, :], in0=bank[7][:], scalar=col("state_b"),
                                                    in1=delta_b[:, c, :], op0=ALU.add, op1=ALU.mult))
                link(nc.vector.scalar_tensor_tensor(out=dBu[:, 1, :], in0=bank[3][:], scalar=col("state_b"),
                                                    in1=dBu[:, 0, :], op0=ALU.add, op1=ALU.mult))
                nc.vector.tensor_tensor_scan(states[:, c, :], decay_b[:, c, :], dBu[:, 1, :], 0.0, ALU.mult,
                                             ALU.add).then_inc(B["scan_ready"], 1)
            for c in range(C):
                nc.vector.wait_ge(B["ssm_done"], c + 1)
                nc.vector.wait_ge(B["u_b_ready"], c + 1)
                sl = slice(JT * c, JT * c + JT)
                link(nc.vector.tensor_tensor(U[:, sl, :], U[:, sl, :],
                                             bank[4 + c % 2][:].rearrange("p (t d) -> p t d", d=P), ALU.add))
                for t in range(JT * c, JT * c + JT):
                    last = nc.vector.bn_stats(stats[:, t, :], U[:, t, :])
                last.then_inc(B["x1_ready"], 1)
            nc.vector.wait_ge(B["x1_ready"], C)
            for t in range(T):
                last = nc.vector.bn_aggr(mv[:, t, :], stats[:, t, :])
            link(last)
            link(nc.vector.tensor_scalar(row(1), mv[:, :, 1], 1e-5, None, ALU.add))
            dve_rsqrt(row(0), row(1), row(2))
            for t in range(T):
                nc.vector.tensor_scalar(XH[:, t, :], U[:, t, :], mv[:, t, 0:1], rs[:, 0, t:t + 1],
                                        ALU.subtract, ALU.mult).then_inc(B["xh2_ready"], 1)
            for c in range(C):
                sl = slice(JT * c, JT * c + JT)
                nc.vector.wait_ge(B["yt_done"], c + 1)
                nc.vector.wait_ge(B["xu_ready"], c + 1)
                nc.vector.tensor_tensor(X[:, sl, :], X[:, sl, :], bank[7][:].rearrange("p (t d) -> p t d", d=P),
                                        ALU.add).then_inc(x_ready, 1)

        def ssm_act():
            for c in range(C):
                nc.scalar.wait_ge(B["xt_turned"], c + 1)
                nc.scalar.activation(xT[:, c, :], bank[c][:], ACT.Identity, bias=col("n1b"),
                                     scale=col("n1w")).then_inc(B["xt_ready"], 1)
            nc.scalar.wait_ge(B["z_abs"], 1)
            nc.scalar.activation(zs[:, 2], zs[:, 1], ACT.Exp, scale=-1.0).then_inc(B["z_exp"], 1)
            nc.scalar.wait_ge(B["z_exp"], 1)
            nc.scalar.activation(zs[:, 3], zs[:, 2], ACT.Ln, bias=1.0).then_inc(B["z_ln"], 1)
            nc.scalar.wait_ge(B["delta_ready"], 1)
            nc.scalar.activation(zs[:, 4], zs[:, 3], ACT.Exp, scale=-1.0).then_inc(B["decay_ready"], 1)
            for c in range(C):
                pair = (4, 5) if c % 2 == 0 else (6, 0)
                for g, dst in ((0, gate), (1, gate2)):
                    nc.scalar.wait_ge(B["g_done"], 2 * c + g + 1)
                    nc.scalar.activation(dst[:, c, :], bank[pair[g]][:], ACT.Silu,
                                         bias=col("gate_b", g)).then_inc(B["silu_ready"], 1)
            for c in range(C):
                for g, dst in ((0, delta_b), (1, decay_b)):
                    nc.scalar.wait_ge(B["bc_done"], 2 * c + g + 1)
                    nc.scalar.activation(dst[:, c, :], bank[1 + g][:], ACT.Copy).then_inc(B["bc_copied"], 1)
            for c in range(C):
                nc.scalar.wait_ge(B["x2_turned"], c + 1)
                nc.scalar.activation(xT[:, c, :], bank[6][:] if c % 2 == 0 else bank[0][:], ACT.Identity,
                                     bias=col("n2b"), scale=col("n2w")).then_inc(B["x2_ready"], 1)
            for c in range(C + 1):
                if c < C:
                    if c >= 2:
                        nc.scalar.wait_ge(B["y_done"], c - 1)
                    for m in range(HK):
                        nc.scalar.wait_ge(B["g1_done"], HK * c + m + 1)
                        nc.scalar.activation(hid[:, (c % 2) * HK + m, :], bank[1 + m][:], ACT.Gelu,
                                             bias=col("mlp_b1", m)).then_inc(B["hf_ready"], 1)
                if c >= 1:
                    nc.scalar.wait_ge(B["y_done"], c)
                    if c >= 3:
                        nc.scalar.wait_ge(B["yt_done"], c - 2)
                    nc.scalar.activation(yfm[:, (c - 1) % 2, :], bank[5 + (c - 1) % 2][:], ACT.Identity,
                                         bias=col("mlp_b2")).then_inc(B["y_copied"], 1)

        def ssm_pool():
            nc.gpsimd.wait_ge(s_w0, 16 * 7)
            for c in range(C):
                sl = slice(JT * c, JT * c + JT)
                nc.gpsimd.wait_ge(B["xh_ready"], JT * c + JT)
                nc.gpsimd.tensor_tensor(U[:, sl, :], U[:, sl, :], outb_row[:].unsqueeze(1).to_broadcast([P, JT, P]),
                                        ALU.add).then_inc(B["u_b_ready"], 1)
            for c in range(C):
                sl = slice(JT * c, JT * c + JT)
                nc.gpsimd.wait_ge(B["x1_ready"], c + 1)
                nc.gpsimd.tensor_tensor(X[:, sl, :], X[:, sl, :], U[:, sl, :], ALU.add).then_inc(B["xu_ready"], 1)

        def ssm_pe():
            for c in range(C):
                for j in range(JT):
                    nc.tensor.wait_ge(B["xh_ready"], JT * c + j + 1)
                    ins = nc.tensor.transpose(bank[c][:, j * P:(j + 1) * P], XH[:, JT * c + j, :], ident[:])
                ins.then_inc(B["xt_turned"], 1)
            nc.tensor.wait_ge(B["z_done"], 1)
            for t in range(T):
                c, j = divmod(t, JT)
                nc.tensor.wait_ge(B["xt_ready"], c + 1)
                ins = nc.tensor.matmul(bank[7][:, t:t + 1], xT[:, c, j * P:(j + 1) * P], sbar[:, 0:1],
                                       start=True, stop=True)
            ins.then_inc(B["z_done"], 1)
            for c in range(C):
                pair = (4, 5) if c % 2 == 0 else (6, 0)
                if c >= 2:
                    nc.tensor.wait_ge(B["silu_ready"], 2 * (c - 1))
                for g in range(2):
                    nc.tensor.matmul(bank[pair[g]][:], gate_w[:, g * P:(g + 1) * P], xT[:, c, :], start=True,
                                     stop=True).then_inc(B["g_done"], 1)
            nc.tensor.wait_ge(B["decay_ready"], 1)
            for c in range(C):
                for g, k in ((0, 3), (1, 4)):
                    if c >= 1:
                        nc.tensor.wait_ge(B["bc_copied"], 2 * c - 1 + g)
                    for j in range(JT):
                        t = JT * c + j
                        ins = nc.tensor.transpose(bank[1 + g][:, j * P:(j + 1) * P],
                                                  zs[:, k, t:t + 1].to_broadcast([P, P]), ident[:])
                    ins.then_inc(B["bc_done"], 1)
                nc.tensor.wait_ge(B["xg_ready"], c + 1)
                if c >= 1:
                    nc.tensor.wait_ge(B["scan_ready"], c)
                nc.tensor.matmul(bank[7][:], state_w[:], gate2[:, c, :], start=True, stop=True)
                nc.tensor.matmul(bank[3][:], state_w[:], gate[:, c, :], start=True, stop=True).then_inc(B["ub_done"], 1)
            for c in range(C):
                nc.tensor.wait_ge(B["scan_ready"], c + 1)
                if c >= 2:
                    nc.tensor.wait_ge(B["x1_ready"], c - 1)
                for j in range(JT):
                    ins = nc.tensor.matmul(bank[4 + c % 2][:, j * P:(j + 1) * P], states[:, c, j * P:(j + 1) * P],
                                           out_w[:], start=True, stop=True)
                ins.then_inc(B["ssm_done"], 1)
            for c in range(C):
                if c >= 2:
                    nc.tensor.wait_ge(B["x2_ready"], c - 1)
                for j in range(JT):
                    nc.tensor.wait_ge(B["xh2_ready"], JT * c + j + 1)
                    ins = nc.tensor.transpose((bank[6] if c % 2 == 0 else bank[0])[:, j * P:(j + 1) * P],
                                              XH[:, JT * c + j, :], ident[:])
                ins.then_inc(B["x2_turned"], 1)
            for c in range(C + 2):
                if c < C:
                    nc.tensor.wait_ge(B["x2_ready"], C if c else 1)
                    for m in range(HK):
                        if c >= 1:
                            nc.tensor.wait_ge(B["hf_ready"], HK * (c - 1) + m + 1)
                        nc.tensor.matmul(bank[1 + m][:], mlp_w1[:, m * P:(m + 1) * P], xT[:, c, :], start=True,
                                         stop=True).then_inc(B["g1_done"], 1)
                if 1 <= c <= C:
                    if c >= 3:
                        nc.tensor.wait_ge(B["y_copied"], c - 2)
                    for m in range(HK):
                        nc.tensor.wait_ge(B["hf_ready"], HK * (c - 1) + m + 1)
                        ins = nc.tensor.matmul(bank[5 + (c - 1) % 2][:], mlp_w2[:, m, :],
                                               hid[:, ((c - 1) % 2) * HK + m, :], start=(m == 0), stop=(m == HK - 1))
                    ins.then_inc(B["y_done"], 1)
                if c >= 2:
                    nc.tensor.wait_ge(B["y_copied"], c - 1)
                    if c >= 3:
                        nc.tensor.wait_ge(x_ready, C + c - 2)
                    for j in range(JT):
                        ins = nc.tensor.transpose(bank[7][:, j * P:(j + 1) * P],
                                                  yfm[:, (c - 2) % 2, j * P:(j + 1) * P], ident[:])
                    ins.then_inc(B["yt_done"], 1)

        comb = arena[:, 4:12, :]
        disp = arena[:, 12:20, :]
        dispT = arena[:, 20:24, :]
        combT = arena[:, 24:40, :]
        hid_s = arena[:, 4:8, :].rearrange("p (q h) (b n) -> p q (h b) n", q=2, b=2)
        eoT = arena[:, 8:12, :]
        eo = arena[:, 12:16, :].rearrange("p c (s d) -> p c s d", d=P)

        def soft_sems(n):
            names = ("xh_ready xt_turned xt_ready lg_done nm_ready exp_done dt_ready tr_done ct_ready d_ready "
                     "slots_done slots_ready wload0 wload1 g1_done hf_ready y_done eot_ready eo_turned eo_ready out_done").split()
            return {k: sem(f"{k}_{n}") for k in names}

        F = [soft_sems("soft0"), soft_sems("soft1")]
        slots_ld = sem("slots_ld")
        sn_ready = sem("sn_ready")
        sn_turned = sem("sn_turned")
        sn_copied = sem("sn_copied")

        def slots_dve():
            se = U[:, 0:JT, :]
            nc.vector.wait_ge(slots_ld, 16)
            for t in range(JT):
                last = nc.vector.bn_stats(stats[:, t, :], se[:, t, :])
            link(last)
            for t in range(JT):
                last = nc.vector.bn_aggr(mv[:, t, :], stats[:, t, :])
            link(last)
            r = [rs[:, k, 0:JT] for k in range(3)]
            link(nc.vector.tensor_tensor(r[1], mv[:, 0:JT, 0], mv[:, 0:JT, 0], ALU.mult))
            link(nc.vector.tensor_tensor(r[1], r[1], mv[:, 0:JT, 1], ALU.add))
            link(nc.vector.tensor_scalar(r[1], r[1], float(P), 1e-30, ALU.mult, ALU.max))
            dve_rsqrt(r[0], r[1], r[2])
            link(nc.vector.tensor_scalar(r[0], r[0], 1e12, SCALE, ALU.min, ALU.mult))
            for t in range(JT):
                nc.vector.tensor_scalar(U[:, JT + t, :], se[:, t, :], rs[:, 0, t:t + 1], None,
                                        ALU.mult).then_inc(sn_ready, 1)

        def slots_pe():
            nc.tensor.wait_ge(sn_ready, JT)
            for t in range(JT):
                ins = nc.tensor.transpose(bank[7][:, t * P:(t + 1) * P], U[:, JT + t, :], ident[:])
            ins.then_inc(sn_turned, 1)

        def slots_act():
            nc.scalar.wait_ge(b_copied, 1)
            nc.scalar.wait_ge(sn_turned, 1)
            nc.scalar.activation(snT[:], bank[7][:], ACT.Copy, scale=col("slot_gamma")).then_inc(sn_copied, 1)

        def soft_dve(S, at, whole):
            if whole:
                nc.vector.wait_ge(x_ready, at + C)
            dve_stats(X, x_ready, None if whole else at)
            link(nc.vector.tensor_scalar(row(1), mv[:, :, 1], 1e-5, None, ALU.add))
            dve_rsqrt(row(0), row(1), row(2))
            link(nc.vector.tensor_tensor(row(3), row(0), row(0), ALU.mult))
            link(nc.vector.tensor_tensor(row(3), row(3), mv[:, :, 1], ALU.mult))
            link(nc.vector.tensor_scalar(row(3), row(3), float(P), 1e-30, ALU.mult, ALU.max))
            dve_rsqrt(row(1), row(3), row(2))
            link(nc.vector.tensor_scalar(row(1), row(1), 1e12, SCALE, ALU.min, ALU.mult))
            link(nc.vector.tensor_tensor(row(0), row(0), row(1), ALU.mult))
            for t in range(T):
                nc.vector.tensor_scalar(XH[:, t, :], X[:, t, :], mv[:, t, 0:1], rs[:, 0, t:t + 1],
                                        ALU.subtract, ALU.mult).then_inc(S["xh_ready"], 1)

            def maxima(b):
                for k in range(8):
                    nc.vector.wait_ge(S["lg_done"], 8 * b + k + 1)
                    nc.vector.tensor_reduce(nmax[:, b, k:k + 1], bank[k % 4][:], AX_X, ALU.max,
                                            negate=True).then_inc(S["nm_ready"], 1)

            def scale_dispatch(b):
                nc.vector.wait_ge(S["exp_done"], 8 * b + 8)
                link(nc.vector.reciprocal(sums[:, b, 4:8], sums[:, b, 4:8]))
                for st in range(4):
                    d = disp[:, 4 * (b % 2) + st, :]
                    nc.vector.tensor_scalar(d, d, sums[:, b, 4 + st:5 + st], None, ALU.mult).then_inc(S["dt_ready"], 1)

            maxima(0)
            scale_dispatch(0)
            for b in range(C):
                if b < C - 1:
                    maxima(b + 1)
                for st in range(4):
                    nc.vector.wait_ge(S["tr_done"], 8 * b + st + 1)
                    nc.vector.tensor_copy(combT[:, 4 * b + st, :], bank[4 + st % 2][:]).then_inc(S["ct_ready"], 1)
                if b < C - 1:
                    scale_dispatch(b + 1)
            link(nc.vector.reciprocal(sums[:, :, 0:4], sums[:, :, 0:4]))
            link(nc.vector.tensor_scalar(sums[:, :, 0:4], sums[:, :, 0:4], 0.5, None, ALU.mult))
            for e in range(E):
                nc.vector.wait_ge(S["y_done"], e + 1)
                dst = eoT[:, :, e * S_PER:(e + 1) * S_PER]
                nc.vector.tensor_scalar(dst, bank[4 + e % 2][:, 0:NB].rearrange("p (b s) -> p b s", b=C),
                                        cols_of("b2_1")[:, e:e + 1], None, ALU.add).then_inc(S["eot_ready"], 1)
            for c in range(C):
                nc.vector.wait_ge(S["out_done"], c + 1)
                for j in range(JT):
                    t = JT * c + j
                    ins = nc.vector.scalar_tensor_tensor(
                        out=X[:, t, :], in0=bank[c][:, j * P:(j + 1) * P], scalar=sums[:, c, j:j + 1],
                        in1=X[:, t, :], op0=ALU.mult, op1=ALU.add)
                ins.then_inc(x_ready, 1)

        def soft_act(S):
            for c in range(C):
                nc.scalar.wait_ge(S["xt_turned"], c + 1)
                nc.scalar.activation(xT[:, c, :], bank[c][:], ACT.Copy, scale=col("gamma")).then_inc(S["xt_ready"], 1)

            def exps(b):
                for k in range(8):
                    nc.scalar.wait_ge(S["nm_ready"], 8 * b + k + 1)
                    if b >= 2:
                        nc.scalar.wait_ge(S["tr_done"], 8 * (b - 2) + (4 if k < 4 else 8))
                    dst = (comb if k < 4 else disp)[:, 4 * (b % 2) + k % 4, :]
                    nc.scalar.activation(dst, bank[k % 4][:], ACT.Exp, bias=nmax[:, b, k:k + 1],
                                         accum_out=sums[:, b, k:k + 1]).then_inc(S["exp_done"], 1)

            exps(0)
            for b in range(C):
                if b < C - 1:
                    exps(b + 1)
                for nt in range(JT):
                    nc.scalar.wait_ge(S["tr_done"], 8 * b + 4 + nt + 1)
                    if b >= 1:
                        nc.scalar.wait_ge(S["slots_done"], b)
                    nc.scalar.activation(dispT[:, nt, :], bank[4 + nt % 2][:], ACT.Copy).then_inc(S["d_ready"], 1)
                nc.scalar.wait_ge(S["slots_done"], b + 1)
                nc.scalar.activation(slotsT[:, :, b, :], bank[6][:].rearrange("p (e s) -> p e s", e=E), ACT.Copy,
                                     scale=col("gamma")).then_inc(S["slots_ready"], 1)
            for e in range(E):
                if e >= 2:
                    nc.scalar.wait_ge(S["y_done"], e - 1)
                for m in range(HK):
                    nc.scalar.wait_ge(S["g1_done"], HK * e + m + 1)
                    nc.scalar.activation(hid_s[:, e % 2, m, :], bank[m][:, 0:NB],
                                         ACT.Gelu, bias=cols_of("b1_1")[:, HK * e + m:HK * e + m + 1]).then_inc(S["hf_ready"], 1)
            for c in range(C):
                nc.scalar.wait_ge(S["eo_turned"], c + 1)
                nc.scalar.activation(eo[:, c, :, :], bank[6 + c % 2][:].rearrange("p (s d) -> p s d", d=P),
                                     ACT.Copy).then_inc(S["eo_ready"], 1)

        def soft_pe(S):
            for c in range(C):
                for j in range(JT):
                    nc.tensor.wait_ge(S["xh_ready"], JT * c + j + 1)
                    ins = nc.tensor.transpose(bank[c][:, j * P:(j + 1) * P], XH[:, JT * c + j, :], ident[:])
                ins.then_inc(S["xt_turned"], 1)
            nc.tensor.wait_ge(sn_copied, 1)

            def logits(b):
                nc.tensor.wait_ge(S["xt_ready"], C)
                for k in range(8):
                    n = 8 * b + k
                    if n >= 4:
                        nc.tensor.wait_ge(S["exp_done"], n - 3)
                    blk = slice((k % 4) * P, (k % 4 + 1) * P)
                    if k < 4:
                        ins = nc.tensor.matmul(bank[k][:], xT[:, b, blk], snT[:], start=True, stop=True)
                    else:
                        ins = nc.tensor.matmul(bank[k - 4][:], snT[:, blk], xT[:, b, :], start=True, stop=True)
                    ins.then_inc(S["lg_done"], 1)

            logits(0)
            for b in range(C):
                if b < C - 1:
                    logits(b + 1)
                for j in range(8):
                    if j < 2 and b >= 1:
                        nc.tensor.wait_ge(S["d_ready"], 4 * (b - 1) + 3 + j)
                    elif 2 <= j < 6:
                        nc.tensor.wait_ge(S["ct_ready"], 4 * b + j - 1)
                    elif j >= 6:
                        nc.tensor.wait_ge(S["d_ready"], 4 * b + j - 5)
                    if j < 4:
                        nc.tensor.wait_ge(S["exp_done"], 8 * b + 4)
                    else:
                        nc.tensor.wait_ge(S["dt_ready"], 4 * b + 4)
                    src = comb if j < 4 else disp
                    for k in range(4):
                        ins = nc.tensor.transpose(bank[4 + j % 2][:, k * P:(k + 1) * P],
                                                  src[:, 4 * (b % 2) + k, (j % 4) * P:(j % 4 + 1) * P], ident[:])
                    ins.then_inc(S["tr_done"], 1)
                if b >= 1:
                    nc.tensor.wait_ge(S["slots_ready"], b)
                for nt in range(JT):
                    nc.tensor.wait_ge(S["d_ready"], 4 * b + nt + 1)
                    ins = nc.tensor.matmul(bank[6][:], XH[:, JT * b + nt, :], dispT[:, nt, :], start=(nt == 0),
                                           stop=(nt == JT - 1))
                ins.then_inc(S["slots_done"], 1)

            def g1(e):
                nc.tensor.wait_ge(S["wload1"] if e % 2 else S["wload0"], 32 * (e // 2 + 1))
                for m in range(HK):
                    if e >= 1:
                        nc.tensor.wait_ge(S["hf_ready"], HK * (e - 1) + m + 1)
                    nc.tensor.matmul(bank[m][:, 0:NB],
                                     wraw[e % 2][:, 0, m * P:(m + 1) * P],
                                     slotsT[:, e, :, :], start=True, stop=True).then_inc(S["g1_done"], 1)

            nc.tensor.wait_ge(S["slots_ready"], C)
            nc.tensor.wait_ge(S["exp_done"], 8 * C)
            nc.tensor.wait_ge(S["ct_ready"], 4 * C)
            g1(0)
            for e in range(E):
                if e < E - 1:
                    g1(e + 1)
                if e >= 2:
                    nc.tensor.wait_ge(S["eot_ready"], e - 1)
                for m in range(HK):
                    nc.tensor.wait_ge(S["hf_ready"], HK * e + m + 1)
                    ins = nc.tensor.matmul(bank[4 + e % 2][:, 0:NB], wraw[e % 2][:, 1, m * P:(m + 1) * P],
                                           hid_s[:, e % 2, m, :], start=(m == 0), stop=(m == HK - 1))
                ins.then_inc(S["y_done"], 1)
            nc.tensor.wait_ge(S["eot_ready"], E)
            for c in range(C):
                if c >= 2:
                    nc.tensor.wait_ge(S["eo_ready"], c - 1)
                for k in range(4):
                    ins = nc.tensor.transpose(bank[6 + c % 2][:, k * P:(k + 1) * P], eoT[:, c, k * P:(k + 1) * P], ident[:])
                ins.then_inc(S["eo_turned"], 1)
            for c in range(C):
                nc.tensor.wait_ge(S["eo_ready"], c + 1)
                for nt in range(JT):
                    for k in range(4):
                        ins = nc.tensor.matmul(bank[c][:, nt * P:(nt + 1) * P], combT[:, 4 * c + k, nt * P:(nt + 1) * P],
                                               eo[:, c, k, :], start=(k == 0), stop=(k == 3))
                ins.then_inc(S["out_done"], 1)

        def soft_sp(S):
            w1, w2 = A["L1_ffn_w1"], A["L1_ffn_w2"].rearrange("e (m h) d -> e h m d", h=P)
            for e in range(E):
                wl_sem = S["wload1"] if e % 2 else S["wload0"]
                if e >= 2:
                    nc.sync.wait_ge(S["y_done"], e - 1)
                nc.sync.dma_start(wraw[e % 2][:, 0, :], w1[e]).then_inc(wl_sem, 16)
                nc.sync.dma_start(wraw[e % 2][:, 1, :].rearrange("p (m d) -> p m d", d=P), w2[e]).then_inc(wl_sem, 16)

        N5 = LAYERS * JT
        hT, oT, h2T = (arena[:, k, :] for k in range(3))
        gact = arena[:, 5:8, :]
        qkv = arena[:, 8:14, :].rearrange("p (q h) n -> p q (h n)", q=2).rearrange("p q (t r) -> p q t r", t=C)
        sq = [arena[:, a:a + 2, :].rearrange("p a n -> p (a n)").rearrange("p (g k) -> p g k", k=DK) for a in (14, 24)]
        prod = arena[:, 16:20, :].rearrange("p a n -> p (a n)").rearrange("p (x h k) -> p x h k", h=H, k=DK)
        tmp5 = arena[:, 20:23, :].rearrange("p a n -> p (a n)")[:, 0:C * P].rearrange("p (t h k) -> p t h k", h=H, k=DK)
        O5 = arena[:, 23, :].rearrange("p (t h k) -> p t h k", h=H, k=DK)
        th = sb("th", [P, 2, C, H])
        coef = sb("coef", [P, 16, H])
        small5 = sb("small5", [P, 4, C * 2 * H])
        X4 = X[:].rearrange("p (t j) d -> p t j d", j=JT)
        U4 = U[:].rearrange("p (t j) d -> p t j d", j=JT)
        XH4 = XH[:].rearrange("p (t j) d -> p t j d", j=JT)
        mv4 = mv[:].rearrange("p (t j) k -> p t j k", j=JT)
        st4 = stats[:].rearrange("p (t j) k -> p t j k", j=JT)
        KK_AT = [0, 3, 5]
        KQ_AT = [6, 10, 13, 15]
        D5 = {k: sem(k + "_delta") for k in (
            "u_ready xh_ready t1_done ht_ready qkv_done qkv_ready sq_ready o_ready ot_turned ot_ready wo_done u1_ready "
            "xh2_ready t2_done h2_ready gy_done sg_ready act_ready wd_done").split()}
        s_w1 = sem("s_w1")
        last5 = {"u": 0}

        def rms(j):
            for t in range(C):
                last = nc.vector.bn_stats(st4[:, t, j, :], U4[:, t, j, :])
            link(last)
            for t in range(C):
                last = nc.vector.bn_aggr(mv4[:, t, j, :], st4[:, t, j, :])
            link(last)
            r = [rs[:, k, 0:C] for k in range(3)]
            link(nc.vector.tensor_tensor(r[1], mv4[:, :, j, 0], mv4[:, :, j, 0], ALU.mult))
            link(nc.vector.scalar_tensor_tensor(out=r[1], in0=r[1], scalar=1e-6, in1=mv4[:, :, j, 1], op0=ALU.add,
                                                op1=ALU.add))
            dve_rsqrt(r[0], r[1], r[2])

        def delta_dve(at):
            dve_stats(X, x_ready, at)
            link(nc.vector.tensor_scalar(row(1), mv[:, :, 1], 1e-5, None, ALU.add))
            dve_rsqrt(row(0), row(1), row(2))
            for t in range(T):
                last = nc.vector.tensor_scalar(U[:, t, :], X[:, t, :], mv[:, t, 0:1], rs[:, 0, t:t + 1],
                                               ALU.subtract, ALU.mult)
            link(last)

            def norm1(n):
                j = n % JT
                rms(j)
                for t in range(C):
                    nc.vector.tensor_scalar(XH4[:, t, j, :], U4[:, t, j, :], rs[:, 0, t:t + 1], None,
                                            ALU.mult).then_inc(D5["xh_ready"], 1)

            def heads(n, k):
                return qkv[:, n % 2, :, k * P:(k + 1) * P].rearrange("p t (h k) -> p t h k", k=DK)

            def norm_qk(n):
                nc.vector.wait_ge(D5["sq_ready"], n + 1)
                ss, r, t_ = small5[:, 0, :], small5[:, 1, :], small5[:, 2, :]
                link(nc.vector.tensor_reduce(ss, sq[n % 2], AX_X, ALU.add))
                link(nc.vector.tensor_scalar(ss, ss, 1e-6, None, ALU.add))
                dve_rsqrt(r, ss, t_)
                r4 = r.rearrange("p (t g) -> p t g", t=C)
                for k in range(2):
                    nc.vector.tensor_tensor(heads(n, k), heads(n, k),
                                            r4[:, :, k * H:(k + 1) * H].unsqueeze(3).to_broadcast([P, C, H, DK]), ALU.mult)
                b = th[:, n % 2]
                link(nc.vector.tensor_scalar(b, b, 1.0, None, ALU.add))
                link(nc.vector.tensor_tensor(heads(n, 2), heads(n, 2), b.unsqueeze(3).to_broadcast([P, C, H, DK]), ALU.mult))

            def products(n):
                q, k = heads(n, 0), heads(n, 1)
                for s_ in range(C):
                    m = C - s_
                    last = nc.vector.tensor_tensor(prod[:, KQ_AT[s_]:KQ_AT[s_] + m], q[:, s_:, :, :],
                                                   k[:, s_:s_ + 1, :, :].to_broadcast([P, m, H, DK]), ALU.mult)
                    if s_ < C - 1:
                        nc.vector.tensor_tensor(prod[:, KK_AT[s_]:KK_AT[s_] + m - 1], k[:, s_ + 1:, :, :],
                                                k[:, s_:s_ + 1, :, :].to_broadcast([P, m - 1, H, DK]), ALU.mult)
                link(last)
                link(nc.vector.tensor_reduce(coef[:], prod, AX_X, ALU.add))
                for s_ in range(C - 1):
                    m = C - 1 - s_
                    a = coef[:, KK_AT[s_]:KK_AT[s_] + m]
                    last = nc.vector.tensor_tensor(a, a, th[:, n % 2, s_ + 1:, :], ALU.mult)
                link(last)

            def solve(n):
                u = heads(n, 2)

                def spread(at_, m):
                    return coef[:, at_:at_ + m].unsqueeze(3).to_broadcast([P, m, H, DK])

                if n >= 1:
                    nc.vector.wait_ge(D5["ot_turned"], n)
                for s_ in range(C):
                    m = C - s_
                    us = u[:, s_:s_ + 1]
                    if m > 1:
                        link(nc.vector.tensor_tensor(tmp5[:, 0:m - 1], spread(KK_AT[s_], m - 1),
                                                     us.to_broadcast([P, m - 1, H, DK]), ALU.mult))
                        link(nc.vector.tensor_tensor(u[:, s_ + 1:], u[:, s_ + 1:], tmp5[:, 0:m - 1], ALU.subtract))
                    dst = O5 if s_ == 0 else tmp5[:, 0:m]
                    link(nc.vector.tensor_tensor(dst, spread(KQ_AT[s_], m), us.to_broadcast([P, m, H, DK]), ALU.mult))
                    if s_ > 0:
                        link(nc.vector.tensor_tensor(O5[:, s_:], O5[:, s_:], tmp5[:, 0:m], ALU.add))
                link(nc.vector.tensor_tensor(tmp5, O5, O5, ALU.mult))
                ss, r, t_ = (small5[:, k, 0:C * H] for k in range(3))
                link(nc.vector.tensor_reduce(ss.rearrange("p (t h) -> p t h", t=C), tmp5, AX_X, ALU.add))
                link(nc.vector.tensor_scalar(ss, ss, 1.0 / DK, 1e-6, ALU.mult, ALU.add))
                dve_rsqrt(r, ss, t_)
                nc.vector.tensor_tensor(O5, O5, r.rearrange("p (t h) -> p t h", t=C).unsqueeze(3).to_broadcast([P, C, H, DK]),
                                        ALU.mult).then_inc(D5["o_ready"], 1)

            def psum4(k):
                return bank[k][:].rearrange("p (t d) -> p t d", d=P)

            def after_wo(n):
                j = n % JT
                nc.vector.wait_ge(D5["wo_done"], n + 1)
                link(nc.vector.tensor_tensor(U4[:, :, j, :], U4[:, :, j, :], psum4(4), ALU.add))
                rms(j)
                for t in range(C):
                    nc.vector.tensor_scalar(XH4[:, t, j, :], U4[:, t, j, :], rs[:, 0, t:t + 1], None,
                                            ALU.mult).then_inc(D5["xh2_ready"], 1)

            def gated(n):
                for m, (_, w) in enumerate(FB):
                    nc.vector.wait_ge(D5["sg_ready"], 3 * n + m + 1)
                    if m == 0 and n >= 1:
                        nc.vector.wait_ge(D5["wd_done"], n)
                    nc.vector.tensor_tensor(gact[0:w, m, :], bank[(6, 4, 6)[m]][0:w, :], arena[0:w, 3 + m % 2, :],
                                            ALU.mult).then_inc(D5["act_ready"], 1)

            def after_wd(n):
                j = n % JT
                nc.vector.wait_ge(D5["wd_done"], n + 1)
                nc.vector.tensor_tensor(U4[:, :, j, :], U4[:, :, j, :], psum4(7), ALU.add).then_inc(D5["u_ready"], 1)
                nc.vector.wait_ge(D5["u_ready"], n + 1)
                if n >= N5 - JT:
                    rms(j)
                    for t in range(C):
                        last = nc.vector.scalar_tensor_tensor(out=XH4[:, t, j, :], in0=U4[:, t, j, :],
                                                              scalar=rs[:, 0, t:t + 1], in1=final_row[:],
                                                              op0=ALU.mult, op1=ALU.mult)
                    link(last)
                    nc.vector.tensor_tensor(X4[:, :, j, :], X4[:, :, j, :], XH4[:, :, j, :], ALU.add).then_inc(x_ready, 1)

            norm1(0)
            for n in range(N5 + 1):
                if n + 1 < N5:
                    norm1(n + 1)
                if n < N5:
                    norm_qk(n)
                if n >= 1:
                    after_wo(n - 1)
                if n < N5:
                    products(n)
                if n >= 1:
                    gated(n - 1)
                if n < N5:
                    solve(n)
                if n >= 1:
                    after_wd(n - 1)

        def delta_act():
            def project(n):
                nc.scalar.wait_ge(D5["t1_done"], n + 1)
                nc.scalar.activation(hT, bank[0][:], ACT.Copy, scale=col("r1w", n // JT)).then_inc(D5["ht_ready"], 1)
                for t in range(C):
                    nc.scalar.wait_ge(D5["qkv_done"], C * n + t + 1)
                    src = bank[1 + t % 2]
                    if n >= 2 and t == 0:
                        nc.scalar.wait_ge(D5["o_ready"], n - 1)
                    nc.scalar.activation(qkv[:, n % 2, t, :], src[:, 0:3 * P], ACT.Silu)
                    nc.scalar.activation(th[:, n % 2, t, :], src[:, 3 * P:3 * P + H], ACT.Tanh,
                                         scale=0.5).then_inc(D5["qkv_ready"], 1)
                nc.scalar.wait_ge(D5["qkv_ready"], C * n + C)
                nc.scalar.activation(sq[n % 2].rearrange("p (t g) k -> p t (g k)", t=C), qkv[:, n % 2, :, 0:2 * P],
                                     ACT.Square).then_inc(D5["sq_ready"], 1)

            project(0)
            for n in range(N5 + 1):
                if n + 1 < N5:
                    project(n + 1)
                if n >= 1:
                    nc.scalar.wait_ge(D5["ot_turned"], n)
                    nc.scalar.activation(oT, bank[3][:], ACT.Copy, scale=col("onorm", (n - 1) // JT)).then_inc(D5["ot_ready"], 1)
                    nc.scalar.wait_ge(D5["t2_done"], n)
                    nc.scalar.activation(h2T, bank[3][:], ACT.Copy, scale=col("r2w", (n - 1) // JT)).then_inc(D5["h2_ready"], 1)
                    for m, (_, w) in enumerate(FB):
                        nc.scalar.wait_ge(D5["gy_done"], 3 * (n - 1) + m + 1)
                        k = 3 * (n - 1) + m
                        if m == 2:
                            nc.scalar.wait_ge(D5["act_ready"], k - 1)
                        elif k >= 1:
                            nc.scalar.wait_ge(D5["act_ready"], 3 * (n - 1))
                        nc.scalar.activation(arena[0:w, 3 + m % 2, :], bank[(5, 7, 5)[m]][0:w, :],
                                             ACT.Silu).then_inc(D5["sg_ready"], 1)

        def delta_pe():
            def project(n):
                lay, j = divmod(n, JT)
                if n >= 1:
                    nc.tensor.wait_ge(D5["ht_ready"], n)
                for t in range(C):
                    nc.tensor.wait_ge(D5["xh_ready"], C * n + t + 1)
                    ins = nc.tensor.transpose(bank[0][:, t * P:(t + 1) * P], XH4[:, t, j, :], ident[:])
                ins.then_inc(D5["t1_done"], 1)
                nc.tensor.wait_ge(D5["ht_ready"], n + 1)
                for t in range(C):
                    k = C * n + t
                    if k >= 2:
                        nc.tensor.wait_ge(D5["qkv_ready"], k - 1)
                    nc.tensor.matmul(bank[1 + t % 2][:, 0:3 * P + H], hT[:, t * P:(t + 1) * P], qkvb[:, lay, :],
                                     start=True, stop=True).then_inc(D5["qkv_done"], 1)

            nc.tensor.wait_ge(s_w1, 16 * W1_LOADS)
            project(0)
            for n in range(N5 + 1):
                if n + 1 < N5:
                    project(n + 1)
                if n == 0:
                    continue
                i = n - 1
                lay, j = divmod(i, JT)
                nc.tensor.wait_ge(D5["o_ready"], i + 1)
                if i >= 1:
                    nc.tensor.wait_ge(D5["h2_ready"], i)
                for t in range(C):
                    ins = nc.tensor.transpose(bank[3][:, t * P:(t + 1) * P],
                                              O5[:, t].rearrange("p h k -> p (h k)"), ident[:])
                ins.then_inc(D5["ot_turned"], 1)
                nc.tensor.wait_ge(D5["ot_ready"], i + 1)
                if i >= 1:
                    nc.tensor.wait_ge(D5["act_ready"], 3 * i)
                for t in range(C):
                    ins = nc.tensor.matmul(bank[4][:, t * P:(t + 1) * P], oT[:, t * P:(t + 1) * P], wo[:, lay, :],
                                           start=True, stop=True)
                ins.then_inc(D5["wo_done"], 1)
                for t in range(C):
                    nc.tensor.wait_ge(D5["xh2_ready"], C * i + t + 1)
                    ins = nc.tensor.transpose(bank[3][:, t * P:(t + 1) * P], XH4[:, t, j, :], ident[:])
                ins.then_inc(D5["t2_done"], 1)
                nc.tensor.wait_ge(D5["h2_ready"], i + 1)
                for m, (at_, w) in enumerate(FB):
                    k = 3 * i + m
                    gb, yb = (5, 7, 5)[m], (6, 4, 6)[m]
                    if m == 2:
                        nc.tensor.wait_ge(D5["act_ready"], k - 1)
                    if m == 1 and i >= 1:
                        nc.tensor.wait_ge(D5["u_ready"], i)
                    nc.tensor.matmul(bank[gb][0:w, :], wg[:, lay, at_:at_ + w], h2T, start=True, stop=True)
                    nc.tensor.matmul(bank[yb][0:w, :], wg[:, lay, FF + at_:FF + at_ + w], h2T, start=True,
                                     stop=True).then_inc(D5["gy_done"], 1)
                nc.tensor.wait_ge(D5["act_ready"], 3 * i + 3)
                for t in range(C):
                    for m, (_, w) in enumerate(FB):
                        ins = nc.tensor.matmul(bank[7][:, t * P:(t + 1) * P], gact[0:w, m, t * P:(t + 1) * P],
                                               wd[0:w, lay, m, :], start=(m == 0), stop=(m == len(FB) - 1))
                ins.then_inc(D5["wd_done"], 1)

        W1_LOADS = LAYERS * 8 + 1

        def delta_sp():
            for k in range(LAYERS):
                for n, name in enumerate(("Wq", "Wk", "Wv")):
                    nc.sync.dma_start(qkvb[:, k, n * P:(n + 1) * P], A["L1_attn_" + name][k]).then_inc(s_w1, 16)
                nc.sync.dma_start(qkvb[:, k, 3 * P:], A["L1_attn_Wb"][k]).then_inc(s_w1, 16)
                nc.sync.dma_start(wo[:, k, :], A["L1_attn_Wo"][k]).then_inc(s_w1, 16)
                nc.sync.dma_start(wg[:, k, :], A["L1_attn_Wg"][k]).then_inc(s_w1, 16)
                nc.sync.dma_start(wd[:, k, 0:2, :], A["L1_attn_Wd"][k, 0:256, :].rearrange("(m h) d -> h m d", h=P)
                                  ).then_inc(s_w1, 16)
                nc.sync.dma_start(wd[0:96, k, 2, :], A["L1_attn_Wd"][k, 256:FF, :]).then_inc(s_w1, 16)
            nc.sync.dma_start(final_row[:], A["L1_attn_final_norm_w"].unsqueeze(0).to_broadcast([P, P])).then_inc(s_w1, 16)

        block = ctx.enter_context(nc.Block())

        @block.sync
        def _(sp):
            xin = A["L0_attn_x"].rearrange("b (j p) d -> b p j d", p=P)
            sp.dma_start(U[:, 0:JT, :], A["L1_ffn_slot_embeds"].rearrange("(t u) s d -> (u s) t d", u=2)).then_inc(slots_ld, 16)
            for c in range(C):
                sp.dma_start(X[:, JT * c:JT * c + JT, :], xin[c]).then_inc(s_x, 16)
            sp.dma_start(gwraw[:], A["L0_ffn_gate_w"]).then_inc(s_small, 16)
            sp.dma_start(gb_row[:], A["L0_ffn_gate_b"].unsqueeze(0).to_broadcast([P, E])).then_inc(s_small, 16)
            for name, (at, k, ref) in COLS.items():
                if name == "onorm":
                    for h in range(H):
                        sp.dma_start(vrows[at:at + k, h * DK:(h + 1) * DK], A["L1_attn_onorm_w"]).then_inc(s_small, 16)
                    continue
                src = A[ref]
                if len(src.shape) == 2:
                    src = src.rearrange("a b -> (a b)")
                sp.dma_start(vrows[at:at + k, :], src.rearrange("(k d) -> k d", d=P)).then_inc(s_small, 16)
            moe_sp(M[0], 0)
            sp.dma_start(gate_w[:], A["L0_attn_gate_w"]).then_inc(s_w0, 16)
            sp.dma_start(state_w[:], A["L0_attn_state_w"]).then_inc(s_w0, 16)
            sp.dma_start(out_w[:], A["L0_attn_out_w"]).then_inc(s_w0, 16)
            sp.dma_start(outb_row[:], A["L0_attn_out_b"].unsqueeze(0).to_broadcast([P, P])).then_inc(s_w0, 16)
            sp.dma_start(stateb_row[:], A["L0_attn_state_b"].unsqueeze(0).to_broadcast([P, P])).then_inc(s_w0, 16)
            sp.dma_start(mlp_w1[:], A["L0_attn_mlp_w1"]).then_inc(s_w0, 16)
            sp.dma_start(mlp_w2[:], A["L0_attn_mlp_w2"].rearrange("(m h) d -> h m d", h=P)).then_inc(s_w0, 16)
            delta_sp()
            moe_sp(M[1], 1)
            nc.sync.wait_ge(M[1]["w_split"], 2 * E)
            soft_sp(F[0])
            nc.sync.wait_ge(F[0]["y_done"], E)
            soft_sp(F[1])
            oout = out.rearrange("b (j p) d -> b p j d", p=P)
            for c in range(C):
                sp.wait_ge(x_ready, STAGES * C - C + c + 1)
                sp.dma_start(oout[c], X[:, JT * c:JT * c + JT, :]).then_inc(s_out, 16)
            sp.wait_ge(s_out, 16 * C)

        @block.gpsimd
        def _(pool):
            nc.gpsimd.memset(ident[:], 0.0).then_inc(s_zero, 1)
            pool.wait_ge(s_zero, 1)
            nc.gpsimd.affine_select(out=ident[:], in_=ident[:], compare_op=ALU.not_equal, fill=1.0, base=0,
                                    pattern=[[-1, P]], channel_multiplier=1).then_inc(s_const, 1)
            nc.gpsimd.memset(tri[:], 1.0).then_inc(s_zero, 1)
            pool.wait_ge(s_zero, 2)
            nc.gpsimd.affine_select(out=tri[:], in_=tri[:], compare_op=ALU.is_gt, fill=0.0, base=0,
                                    pattern=[[1, E], [-1, E]], channel_multiplier=0).then_inc(s_const, 1)
            moe_pool(M[0], 0)
            ssm_pool()
            moe_pool(M[1], 1)

        @block.vector
        def _(dve):
            dve.wait_ge(b_turned, 1)
            dve.tensor_copy(vcols[:], bank[7][:, E:E + n_cols]).then_inc(b_copied, 1)
            dve.tensor_copy(gwh[:], bank[7][:, 0:E]).then_inc(b_copied, 1)
            dve.wait_ge(b_copied, 2)
            dve.tensor_tensor(gwl[:], bank[7][:, 0:E], gwh[:].bitcast(F32), ALU.subtract).then_inc(b_copied, 1)
            slots_dve()
            dve.wait_ge(s_const, 2)
            moe_dve(M[0], 0)
            ssm_dve()
            moe_dve(M[1], 1)
            soft_dve(F[0], 2 * C, False)
            delta_dve(3 * C)
            soft_dve(F[1], 4 * C, True)

        @block.scalar
        def _(act):
            slots_act()
            moe_act(M[0], 0)
            ssm_act()
            moe_act(M[1], 1)
            soft_act(F[0])
            delta_act()
            soft_act(F[1])

        @block.tensor
        def _(pe):
            pe.wait_ge(s_const, 1)
            pe.wait_ge(s_small, 16 * (1 + len(COLS) + H))
            pe.transpose(bank[7][:, E:E + n_cols], vrows[:], ident[0:n_cols, 0:n_cols])
            pe.transpose(bank[7][:, 0:E], gwraw[:], ident[0:E, 0:E]).then_inc(b_turned, 1)
            pe.wait_ge(b_copied, 3)
            slots_pe()
            moe_pe(M[0], 0)
            ssm_pe()
            moe_pe(M[1], 1)
            soft_pe(F[0])
            delta_pe()
            soft_pe(F[1])


def kernel(**inputs):
    import numpy as _np
    import concourse.bacc as _bacc
    from concourse import mybir as _mybir
    from concourse.bass_utils import run_bass_kernel_spmd as _run

    nc = _bacc.Bacc("TRN2", target_bir_lowering=False, num_devices=1)
    arrays, aps = {}, {}
    for name in inputs:
        a = _np.ascontiguousarray(inputs[name])
        arrays[f"in_{name}_dram"] = a
        aps[name] = nc.dram_tensor(f"in_{name}_dram", a.shape, _mybir.dt.from_np(a.dtype), kind="ExternalInput").ap()
    out = nc.dram_tensor("out_0_dram", (4, 512, 128), _mybir.dt.float32, kind="ExternalOutput").ap()
    program(nc, aps, out)
    r = _run(nc, [arrays], core_ids=[0])
    return r.results[0]["out_0_dram"]
```

```python
from contextlib import ExitStack

import concourse.bass as bass
from concourse import mybir

STAGES = 6
P = 128
T = 16
C = 4
JT = 4
CH = JT * P
E = 8
S_PER = 64
NB = C * S_PER
SCALE = float(P) ** 0.5
H = 8
DK = P // H
LAYERS = 2
FF = 352
FB = [(0, 128), (128, 128), (256, 96)]
HK = 4

F32 = mybir.dt.float32
F32R = mybir.dt.float32r
I32 = mybir.dt.int32
ALU = mybir.AluOpType
ACT = mybir.ActivationFunctionType
AX_X = mybir.AxisListType.X
RSQRT_MAGIC = float(0x5F3759DF)


def program(nc, A, out):
    with ExitStack() as ctx:
        def sb(name, shape, dt=F32):
            return ctx.enter_context(nc.sbuf_tensor(name, shape, dt))

        def sem(name):
            return ctx.enter_context(nc.semaphore(name))

        bank = [ctx.enter_context(nc.psum_tensor(f"bank{i}", [P, CH], F32)) for i in range(8)]
        ident = sb("ident", [P, P])
        X = sb("X", [P, T, P])
        XH = sb("XH", [P, T, P])
        stats = sb("stats", [P, T, 6])
        mv = sb("mv", [P, T, 2])
        rs = sb("rs", [P, 8, T])
        xTh = sb("xTh", [P, C, CH], F32R)
        xTl = sb("xTl", [P, C, CH], F32R)
        arena = sb("arena", [P, 40, CH])
        hh = sb("hh", [P, 2, HK, CH], F32R)
        hl = sb("hl", [P, 2, HK, CH], F32R)
        wraw = [sb(f"wraw{p}", [P, 2, CH]) for p in range(2)]
        wh = [sb(f"wh{p}", [P, 2, CH], F32R) for p in range(2)]
        wl = [sb(f"wl{p}", [P, 2, CH], F32R) for p in range(2)]

        U = sb("U", [P, T, P])

        COLS = {}
        n_cols = 0
        for name, ref, k in (
            ("n1w", "L0_attn_norm1_w", 1), ("n1b", "L0_attn_norm1_b", 1), ("gate_b", "L0_attn_gate_b", 2),
            ("state_b", "L0_attn_state_b", 1), ("n2w", "L0_attn_norm2_w", 1), ("n2b", "L0_attn_norm2_b", 1),
            ("mlp_b1", "L0_attn_mlp_b1", HK), ("mlp_b2", "L0_attn_mlp_b2", 1), ("gamma", "L1_ffn_norm_gamma", 1),
            ("slot_gamma", "L1_ffn_slot_norm_gamma", 1), ("r1w", "L1_attn_norm1_w", 2), ("r2w", "L1_attn_norm2_w", 2),
            ("b1_0", "L0_ffn_b1", E * HK), ("b2_0", "L0_ffn_b2", E), ("b1_1", "L1_ffn_b1", E * HK),
            ("b2_1", "L1_ffn_b2", E), ("onorm", None, 2),
        ):
            COLS[name] = (n_cols, k, ref)
            n_cols += k
        vrows = sb("vrows", [n_cols, P])
        vcols = sb("vcols", [P, n_cols])

        def col(name, k=0):
            at = COLS[name][0] + k
            return vcols[:, at:at + 1]

        def cols_of(name):
            at, k, _ = COLS[name]
            return vcols[:, at:at + k]

        gate_w = sb("gate_w", [P, 2 * P])
        state_w = sb("state_w", [P, P])
        out_w = sb("out_w", [P, P])
        outb_row = sb("outb_row", [P, P])
        stateb_row = sb("stateb_row", [P, P])
        mlp_w1 = sb("mlp_w1", [P, CH])
        mlp_w2 = sb("mlp_w2", [P, HK, P])
        sbar = sb("sbar", [P, 2])

        qkvb = sb("qkvb", [P, LAYERS, 3 * P + H])
        wo = sb("wo", [P, LAYERS, P])
        wg = sb("wg", [P, LAYERS, 2 * FF])
        wd = sb("wd", [P, LAYERS, 3, P])
        final_row = sb("final_row", [P, P])

        snT = sb("snT", [P, CH])
        slotsT = U[:].rearrange("p t d -> p (t d)").rearrange("p (e b s) -> p e b s", e=E, b=C)
        nmax = sb("nmax", [P, C, 8])
        sums = sb("sums", [P, C, 8])

        tri = sb("tri", [P, E, E])
        gwraw = sb("gwraw", [E, P])
        gwh = sb("gwh", [P, E], F32R)
        gwl = sb("gwl", [P, E], F32R)
        gb_row = sb("gb_row", [P, E])
        b1col = sb("b1col", [P, 2, HK])
        G = sb("G", [P, T, E])
        WE = sb("WE", [P, E, T])
        gsm = sb("gsm", [P, 4, T, E])
        wcol = sb("wcol", [P, 2, T])

        ybank = (bank[5], bank[7])
        acc = arena[:, 0:4, :]
        hf = arena[:, 4:12, :]
        wbs = arena[:, 12:14, :]
        tmp = arena[:, 14:16, :]

        b1T, b2T = cols_of("b1_0"), cols_of("b2_0")

        s_x = sem("s_x")
        s_w0 = sem("s_w0")
        s_const = sem("s_const")
        s_zero = sem("s_zero")
        s_small = sem("s_small")
        s_out = sem("s_out")
        x_ready = sem("x_ready")
        dve_chain = sem("dve_chain")
        pool_chain = sem("pool_chain")
        b_turned = sem("b_turned")
        b_copied = sem("b_copied")

        chain_at = {"dve": 0, "pool": 0}

        def link(ins):
            chain_at["dve"] += 1
            ins.then_inc(dve_chain, 1)
            nc.vector.wait_ge(dve_chain, chain_at["dve"])

        def moe_sems(n):
            names = ("xh_ready xt_turned xt_hi xt_lo gates_done logits_ready exp_ready wcol_ready w_split g1_done "
                     "hf_ready hh_ready hl_dve hl_pool wb_done wb_copied g2_done y_ready acc_done "
                     "w_hi acc_turned wload0 wload1 b1_ready").split()
            return {k: sem(f"{k}_{n}") for k in names}

        M = [moe_sems("moe0"), moe_sems("moe1")]
        B = {k: sem(k + "_ssm") for k in (
            "xh_ready xt_turned xt_ready z_done z_abs z_exp z_ln delta_ready decay_ready bc_done bc_copied g_done silu_ready "
            "xg_ready ub_done scan_ready u_b_ready ssm_done x1_ready xh2_ready x2_turned x2_ready g1_done hf_ready y_done "
            "y_copied yt_done xu_ready").split()}

        def dve_rsqrt(y, v, t):
            link(nc.vector.tensor_scalar(t.bitcast(I32), v.bitcast(I32), 1, None, ALU.logical_shift_right))
            link(nc.vector.tensor_scalar(y.bitcast(I32), t.bitcast(I32), -1.0, RSQRT_MAGIC, ALU.mult, ALU.add))
            for _ in range(3):
                link(nc.vector.scalar_tensor_tensor(out=t, in0=y, scalar=-0.5, in1=y, op0=ALU.mult, op1=ALU.mult))
                link(nc.vector.tensor_tensor(t, t, v, ALU.mult))
                link(nc.vector.scalar_tensor_tensor(out=y, in0=t, scalar=1.5, in1=y, op0=ALU.add, op1=ALU.mult))

        def dve_stats(src, done, at):
            for t in range(T):
                if t % JT == 0 and at is not None:
                    nc.vector.wait_ge(done, at + t // JT + 1)
                last = nc.vector.bn_stats(stats[:, t, :], src[:, t, :])
            link(last)
            for t in range(T):
                last = nc.vector.bn_aggr(mv[:, t, :], stats[:, t, :])
            link(last)

        def row(k):
            return rs[:, k, :]

        def moe_dve(S, k):
            if k == 0:
                nc.vector.wait_ge(s_x, 16 * C)
            dve_stats(X, x_ready, None if k == 0 else C)
            link(nc.vector.tensor_scalar(row(1), mv[:, :, 1], 1e-5, None, ALU.add))
            dve_rsqrt(row(0), row(1), row(2))
            for t in range(T):
                nc.vector.tensor_scalar(XH[:, t, :], X[:, t, :], mv[:, t, 0:1], rs[:, 0, t:t + 1],
                                        ALU.subtract, ALU.mult).then_inc(S["xh_ready"], 1)
            nc.vector.tensor_copy(b1col[:, 0, :], b1T[:, 0:HK]).then_inc(S["b1_ready"], 1)
            nc.vector.wait_ge(S["wload0"], 32)
            for which in range(2):
                nc.vector.tensor_copy(wh[0][:, which, :], wraw[0][:, which, :]).then_inc(S["w_hi"], 1)
            for c in range(C):
                nc.vector.wait_ge(S["xt_hi"], c + 1)
                nc.vector.tensor_tensor(xTl[:, c, :], bank[c][:], xTh[:, c, :].bitcast(F32),
                                        ALU.subtract).then_inc(S["xt_lo"], 1)
            nc.vector.wait_ge(S["gates_done"], 1)
            glog = bank[6][:, 0:T * E].rearrange("p (t e) -> p t e", e=E)
            link(nc.vector.tensor_tensor(G[:], glog, gb_row[:].unsqueeze(1).to_broadcast([P, T, E]), ALU.add))
            link(nc.vector.tensor_reduce(row(3), G[:], AX_X, ALU.max))
            nc.vector.tensor_tensor(gsm[:, 0], G[:], row(3).unsqueeze(2).to_broadcast([P, T, E]),
                                    ALU.subtract).then_inc(S["logits_ready"], 1)
            for t0 in range(0, T, JT):
                g = G[:, t0:t0 + JT, :]
                gj = g.unsqueeze(2).to_broadcast([P, JT, E, E])
                ge_ = g.unsqueeze(3).to_broadcast([P, JT, E, E])
                before = arena[:, 16, 0:JT * E * E].rearrange("p (t e j) -> p t e j", e=E, j=E)
                equal = arena[:, 17, 0:JT * E * E].rearrange("p (t e j) -> p t e j", e=E, j=E)
                nc.vector.tensor_tensor(before, gj, ge_, ALU.is_gt)
                link(nc.vector.tensor_tensor(equal, gj, ge_, ALU.is_equal))
                link(nc.vector.tensor_tensor(equal, equal, tri[:].unsqueeze(1).to_broadcast([P, JT, E, E]), ALU.mult))
                link(nc.vector.tensor_tensor(before, before, equal, ALU.add))
                link(nc.vector.tensor_reduce(gsm[:, 1, t0:t0 + JT, :], before, AX_X, ALU.add))
            link(nc.vector.tensor_scalar(gsm[:, 1], gsm[:, 1], 2.0, None, ALU.is_lt))
            nc.vector.wait_ge(S["exp_ready"], 1)
            link(nc.vector.tensor_tensor(gsm[:, 1], gsm[:, 1], gsm[:, 2], ALU.mult))
            link(nc.vector.tensor_reduce(row(4), gsm[:, 1], AX_X, ALU.add))
            link(nc.vector.reciprocal(row(5), row(4)))
            link(nc.vector.tensor_tensor(WE[:].rearrange("p e t -> p t e"), gsm[:, 1],
                                         row(5).unsqueeze(2).to_broadcast([P, T, E]), ALU.mult))
            nc.vector.tensor_copy(wcol[:, 0, :], WE[:, 0, :]).then_inc(S["wcol_ready"], 1)

            nc.vector.sem_inc(S["hh_ready"], 5)
            nc.vector.sem_inc(S["hl_dve"], 4)
            nc.vector.sem_inc(S["y_ready"], 2)

            def split_hidden(s, q):
                nc.vector.wait_ge(S["g2_done"], s + 1)
                for m in range(HK):
                    nc.vector.wait_ge(S["hf_ready"], s * 4 + (m + 1))
                    nc.vector.tensor_copy(hh[:, q, m, :], hf[:, q * 4 + m, :]).then_inc(S["hh_ready"], 1)
                    if m < 3:
                        nc.vector.wait_ge(S["hh_ready"], s * 4 + (m + 6))
                        nc.vector.tensor_tensor(hl[:, q, m, :], hf[:, q * 4 + m, :], hh[:, q, m, :].bitcast(F32),
                                                ALU.subtract).then_inc(S["hl_dve"], 1)

            def body(i, last):
                for p in range(2):
                    for c in range(C):
                        q = c % 2
                        s = i * 8 + (4 * p + c)
                        more = not (last and p == 1)
                        if more or c < C - 1:
                            split_hidden(s + 1, 1 - q)
                        if c == 0 and more:
                            nc.vector.wait_ge(S["wload0"] if p else S["wload1"], i * 32 + (64 if p else 32))
                            nc.vector.wait_ge(S["g2_done"], i * 8 + (4 * p + 2))
                            for which in range(2):
                                nc.vector.tensor_copy(wh[1 - p][:, which, :], wraw[1 - p][:, which, :]
                                                      ).then_inc(S["w_hi"], 1)
                        if c == 2 and more:
                            n = i * 2 + (p + 1)
                            nc.vector.wait_ge(S["hf_ready"], i * 32 + (16 * p + 1))
                            nc.vector.tensor_scalar(wcol[:, 1 - p, :], WE[:, bass.ds(n, 1), :].squeeze(1), 1.0, None,
                                                    ALU.mult).then_inc(S["wcol_ready"], 1)
                            nc.vector.tensor_scalar(b1col[:, 1 - p, :], b1T[:, bass.ds(n * HK, HK)], 1.0, None,
                                                    ALU.mult).then_inc(S["b1_ready"], 1)
                        nc.vector.wait_ge(S["g2_done"], s + 3)
                        nc.vector.wait_ge(S["wb_copied"], s + 2)
                        nc.vector.wait_ge(S["acc_done"], s + 1)
                        nc.vector.scalar_tensor_tensor(
                            out=tmp[:, q, :], in0=ybank[q][:], scalar=b2T[:, bass.ds(i * 2 + p, 1)],
                            in1=wbs[:, q, :], op0=ALU.add, op1=ALU.mult).then_inc(S["y_ready"], 1)

            split_hidden(0, 0)
            with nc.vector.Fori(0, E // 2 - 1) as i:
                body(i, False)
            body(E // 2 - 1, True)
            for c in range(C):
                nc.vector.wait_ge(S["acc_turned"], c + 1)
                nc.vector.scalar_tensor_tensor(
                    out=X[:, JT * c:JT * c + JT, :], in0=bank[c][:].rearrange("p (t d) -> p t d", d=P),
                    scalar=0.5, in1=X[:, JT * c:JT * c + JT, :], op0=ALU.mult, op1=ALU.add).then_inc(x_ready, 1)

        def moe_act(S, k):
            for c in range(C):
                nc.scalar.wait_ge(S["xt_turned"], c + 1)
                nc.scalar.activation(xTh[:, c, :], bank[c][:], ACT.Copy).then_inc(S["xt_hi"], 1)
            nc.scalar.wait_ge(S["logits_ready"], 1)
            nc.scalar.activation(gsm[:, 2], gsm[:, 0], ACT.Exp).then_inc(S["exp_ready"], 1)
            nc.scalar.sem_inc(S["wb_copied"], 1)
            with nc.scalar.Fori(0, E // 2) as i:
                for p in range(2):
                    nc.scalar.wait_ge(S["b1_ready"], i * 2 + (p + 1))
                    for c in range(C):
                        q = c % 2
                        s = i * 8 + (4 * p + c)
                        nc.scalar.wait_ge(S["hh_ready"], s * 4 + 1)
                        nc.scalar.wait_ge(S["hl_dve"], s * 3 + 1)
                        nc.scalar.wait_ge(S["hl_pool"], s + 1)
                        for m in range(HK):
                            nc.scalar.wait_ge(S["g1_done"], s * 4 + (m + 1))
                            nc.scalar.activation(hf[:, q * 4 + m, :], bank[m][:], ACT.Gelu,
                                                 bias=b1col[:, p, m:m + 1]).then_inc(S["hf_ready"], 1)
                        nc.scalar.wait_ge(S["wb_done"], s + 1)
                        nc.scalar.wait_ge(S["y_ready"], s + 1)
                        nc.scalar.activation(wbs[:, q, :], bank[4][:], ACT.Copy).then_inc(S["wb_copied"], 1)

        def moe_pool(S, k):
            if k:
                nc.gpsimd.wait_ge(x_ready, 2 * C)
            nc.gpsimd.memset(acc, 0.0).then_inc(S["acc_done"], 2)
            nc.gpsimd.sem_inc(S["hl_pool"], 2)

            def split(p, which, e):
                src = wraw[p][:, which, :]
                nc.gpsimd.wait_ge(S["w_hi"], e * 2 + (which + 1))
                nc.gpsimd.tensor_tensor(wl[p][:, which, :], src, wh[p][:, which, :].bitcast(F32),
                                        ALU.subtract).then_inc(S["w_split"], 1)

            split(0, 0, 0)
            split(0, 1, 0)

            def low_hidden(s, q):
                for m in (3,):
                    if m == 3:
                        nc.gpsimd.wait_ge(S["g2_done"], s + 1)
                    nc.gpsimd.wait_ge(S["hh_ready"], s * 4 + (m + 6))
                    nc.gpsimd.tensor_tensor(hl[:, q, m, :], hf[:, q * 4 + m, :], hh[:, q, m, :].bitcast(F32),
                                            ALU.subtract).then_inc(S["hl_pool"], 1)

            def body(i, last):
                for p in range(2):
                    for c in range(C):
                        q = c % 2
                        s = i * 8 + (4 * p + c)
                        more = not (last and p == 1)
                        if more or c < C - 1:
                            low_hidden(s + 1, 1 - q)
                        if more and c < 2:
                            split(1 - p, c, i * 2 + (p + 1))
                        nc.gpsimd.wait_ge(S["y_ready"], s + 3)
                        nc.gpsimd.wait_ge(S["acc_done"], s + 2)
                        nc.gpsimd.tensor_tensor(acc[:, c, :], acc[:, c, :], tmp[:, q, :], ALU.add
                                                ).then_inc(S["acc_done"], 1)

            low_hidden(0, 0)
            with nc.gpsimd.Fori(0, E // 2 - 1) as i:
                body(i, False)
            body(E // 2 - 1, True)

        def mm3(o, ah, al, bh, bl, start, stop):
            nc.tensor.matmul(o, ah, bh, start=start, stop=False)
            nc.tensor.matmul(o, ah, bl, start=False, stop=False)
            return nc.tensor.matmul(o, al, bh, start=False, stop=stop)

        def moe_pe(S, k):
            nc.tensor.sem_inc(S["g2_done"], 2)
            for c in range(C):
                for j in range(JT):
                    t = JT * c + j
                    nc.tensor.wait_ge(S["xh_ready"], t + 1)
                    if t == 0 and k == 0:
                        nc.tensor.wait_ge(s_const, 1)
                    ins = nc.tensor.transpose(bank[c][:, j * P:(j + 1) * P], XH[:, t, :], ident[:])
                ins.then_inc(S["xt_turned"], 1)
            if k == 0:
                nc.tensor.wait_ge(b_copied, 3)
            nc.tensor.wait_ge(S["xt_hi"], C)
            nc.tensor.wait_ge(S["xt_lo"], C)
            for t in range(T):
                c, j = divmod(t, JT)
                ins = mm3(bank[6][:, t * E:(t + 1) * E], xTh[:, c, j * P:(j + 1) * P], xTl[:, c, j * P:(j + 1) * P],
                          gwh[:], gwl[:], True, True)
            ins.then_inc(S["gates_done"], 1)

            def g1(p, c, s, at_s):
                nc.tensor.wait_ge(S["w_split"], at_s)
                for m in range(HK):
                    nc.tensor.wait_ge(S["hf_ready"], s * 4 + (m - 3))
                    cols = slice(m * P, (m + 1) * P)
                    mm3(bank[m][:], wh[p][:, 0, cols], wl[p][:, 0, cols], xTh[:, c, :], xTl[:, c, :],
                        True, True).then_inc(S["g1_done"], 1)

            def step(i, p, c, more):
                q = c % 2
                s = i * 8 + (4 * p + c)
                nc.tensor.wait_ge(S["wcol_ready"], i * 2 + (p + 1))
                nc.tensor.wait_ge(S["wb_copied"], s + 1)
                for j in range(JT):
                    ins = nc.tensor.transpose(bank[4][:, j * P:(j + 1) * P],
                                              wcol[:, p, JT * c + j:JT * c + j + 1].to_broadcast([P, P]), ident[:])
                ins.then_inc(S["wb_done"], 1)
                if more:
                    p2, c2 = (p, c + 1) if c < C - 1 else (1 - p, 0)
                    e2 = i * 2 + (p + (1 if c == C - 1 else 0))
                    g1(p2, c2, s + 1, e2 * 2 + 1)
                nc.tensor.wait_ge(S["y_ready"], s + 1)
                if c == 0:
                    nc.tensor.wait_ge(S["w_split"], i * 4 + (2 * p + 2))
                for m in range(HK):
                    nc.tensor.wait_ge(S["hh_ready"], s * 4 + (m + 6))
                    if m < 3:
                        nc.tensor.wait_ge(S["hl_dve"], s * 3 + (m + 5))
                    else:
                        nc.tensor.wait_ge(S["hl_pool"], s + 3)
                    cols = slice(m * P, (m + 1) * P)
                    ins = mm3(ybank[q][:], wh[p][:, 1, cols], wl[p][:, 1, cols], hh[:, q, m, :], hl[:, q, m, :],
                              m == 0, m == HK - 1)
                ins.then_inc(S["g2_done"], 1)

            nc.tensor.wait_ge(S["w_split"], 2)
            for m in range(HK):
                cols = slice(m * P, (m + 1) * P)
                mm3(bank[m][:], wh[0][:, 0, cols], wl[0][:, 0, cols], xTh[:, 0, :], xTl[:, 0, :],
                    True, True).then_inc(S["g1_done"], 1)
            with nc.tensor.Fori(0, E // 2 - 1) as i:
                for p in range(2):
                    for c in range(C):
                        step(i, p, c, True)
            for p in range(2):
                for c in range(C):
                    step(E // 2 - 1, p, c, not (p == 1 and c == C - 1))
            for c in range(C):
                nc.tensor.wait_ge(S["acc_done"], 2 + 4 * (E - 1) + c + 1)
                for j in range(JT):
                    ins = nc.tensor.transpose(bank[c][:, j * P:(j + 1) * P], acc[:, c, j * P:(j + 1) * P], ident[:])
                ins.then_inc(S["acc_turned"], 1)

        def moe_sp(S, k):
            w1, w2 = A["L0_ffn_w1"], A["L0_ffn_w2"].rearrange("e (m h) d -> e h m d", h=P)

            def load(e, p, wl_sem):
                nc.sync.dma_start(wraw[p][:, 0, :], w1[e, :, :] if isinstance(e, int) else
                                  w1[bass.ds(e, 1), :, :].squeeze(0)).then_inc(wl_sem, 16)
                dst = wraw[p][:, 1, :].rearrange("p (m d) -> p m d", d=P)
                nc.sync.dma_start(dst, w2[e, :, :, :] if isinstance(e, int) else
                                  w2[bass.ds(e, 1), :, :, :].squeeze(0)).then_inc(wl_sem, 16)

            if k:
                nc.sync.wait_ge(M[0]["w_split"], 2 * E)
            load(0, 0, S["wload0"])
            load(1, 1, S["wload1"])
            with nc.sync.Fori(0, E // 2 - 1) as i:
                nc.sync.wait_ge(S["w_split"], i * 4 + 2)
                load(i * 2 + 2, 0, S["wload0"])
                nc.sync.wait_ge(S["w_split"], i * 4 + 4)
                load(i * 2 + 3, 1, S["wload1"])

        xT = arena[:, 0:4, :]
        gate = arena[:, 4:8, :]
        gate2 = arena[:, 8:12, :]
        delta_b = arena[:, 12:16, :]
        decay_b = arena[:, 16:20, :]
        states = arena[:, 20:24, :]
        hid = arena[:, 24:32, :]
        yfm = arena[:, 32:34, :]
        dBu = arena[:, 34:36, :]
        zs = rs[:, 3:8, :]

        def ssm_dve():
            dve_stats(X, x_ready, 0)
            link(nc.vector.tensor_scalar(row(1), mv[:, :, 1], 1e-5, None, ALU.add))
            dve_rsqrt(row(0), row(1), row(2))
            for t in range(T):
                last = nc.vector.tensor_scalar(U[:, t, :], X[:, t, :], mv[:, t, 0:1], rs[:, 0, t:t + 1],
                                               ALU.subtract, ALU.mult)
            link(nc.vector.tensor_tensor(row(1), row(0), row(0), ALU.mult))
            link(nc.vector.tensor_tensor(row(1), row(1), mv[:, :, 1], ALU.mult))
            link(nc.vector.tensor_scalar(row(1), row(1), 1e-5, None, ALU.add))
            dve_rsqrt(row(0), row(1), row(2))
            for t in range(T):
                nc.vector.tensor_scalar(XH[:, t, :], U[:, t, :], rs[:, 0, t:t + 1], None,
                                        ALU.mult).then_inc(B["xh_ready"], 1)
            nc.vector.wait_ge(s_w0, 16 * 7)
            nc.vector.reduce_sum(sbar[:, 0:1], state_w[:], AX_X)
            link(nc.vector.reduce_sum(sbar[:, 1:2], stateb_row[:], AX_X))
            nc.vector.tensor_scalar(sbar[:, 1:2], sbar[:, 1:2], 1.0 / P, None, ALU.mult).then_inc(B["z_done"], 1)
            nc.vector.wait_ge(B["z_done"], 2)
            link(nc.vector.tensor_scalar(zs[:, 0], bank[7][:, 0:T], 1.0 / P, sbar[:, 1:2], ALU.mult, ALU.add))
            link(nc.vector.tensor_scalar(zs[:, 1], zs[:, 0], -1.0, None, ALU.mult))
            nc.vector.tensor_tensor(zs[:, 1], zs[:, 1], zs[:, 0], ALU.max).then_inc(B["z_abs"], 1)
            nc.vector.wait_ge(B["z_exp"], 1)
            w_, one = row(0), row(1)
            link(nc.vector.tensor_scalar(w_, zs[:, 2], 1.0, None, ALU.add))
            link(nc.vector.tensor_scalar(one, w_, 1.0, None, ALU.is_equal))
            link(nc.vector.scalar_tensor_tensor(out=w_, in0=w_, scalar=-1.0, in1=one, op0=ALU.add, op1=ALU.add))
            link(nc.vector.reciprocal(w_, w_))
            link(nc.vector.tensor_tensor(w_, w_, zs[:, 2], ALU.mult))
            nc.vector.wait_ge(B["z_ln"], 1)
            link(nc.vector.tensor_tensor(one, one, zs[:, 3], ALU.add))
            link(nc.vector.tensor_tensor(one, one, w_, ALU.mult))
            nc.vector.scalar_tensor_tensor(out=zs[:, 3], in0=zs[:, 0], scalar=0.0, in1=one, op0=ALU.max,
                                           op1=ALU.add).then_inc(B["delta_ready"], 1)
            for c in range(C):
                nc.vector.wait_ge(B["silu_ready"], 2 * c + 2)
                nc.vector.tensor_tensor(gate[:, c, :], gate[:, c, :], xT[:, c, :], ALU.mult).then_inc(B["xg_ready"], 1)
            for c in range(C):
                nc.vector.wait_ge(B["ub_done"], c + 1)
                nc.vector.wait_ge(B["bc_copied"], 2 * c + 2)
                link(nc.vector.scalar_tensor_tensor(out=dBu[:, 0, :], in0=bank[7][:], scalar=col("state_b"),
                                                    in1=delta_b[:, c, :], op0=ALU.add, op1=ALU.mult))
                link(nc.vector.scalar_tensor_tensor(out=dBu[:, 1, :], in0=bank[3][:], scalar=col("state_b"),
                                                    in1=dBu[:, 0, :], op0=ALU.add, op1=ALU.mult))
                nc.vector.tensor_tensor_scan(states[:, c, :], decay_b[:, c, :], dBu[:, 1, :], 0.0, ALU.mult,
                                             ALU.add).then_inc(B["scan_ready"], 1)
            for c in range(C):
                nc.vector.wait_ge(B["ssm_done"], c + 1)
                nc.vector.wait_ge(B["u_b_ready"], c + 1)
                sl = slice(JT * c, JT * c + JT)
                link(nc.vector.tensor_tensor(U[:, sl, :], U[:, sl, :],
                                             bank[4 + c % 2][:].rearrange("p (t d) -> p t d", d=P), ALU.add))
                for t in range(JT * c, JT * c + JT):
                    last = nc.vector.bn_stats(stats[:, t, :], U[:, t, :])
                last.then_inc(B["x1_ready"], 1)
            nc.vector.wait_ge(B["x1_ready"], C)
            for t in range(T):
                last = nc.vector.bn_aggr(mv[:, t, :], stats[:, t, :])
            link(last)
            link(nc.vector.tensor_scalar(row(1), mv[:, :, 1], 1e-5, None, ALU.add))
            dve_rsqrt(row(0), row(1), row(2))
            for t in range(T):
                nc.vector.tensor_scalar(XH[:, t, :], U[:, t, :], mv[:, t, 0:1], rs[:, 0, t:t + 1],
                                        ALU.subtract, ALU.mult).then_inc(B["xh2_ready"], 1)
            for c in range(C):
                sl = slice(JT * c, JT * c + JT)
                nc.vector.wait_ge(B["yt_done"], c + 1)
                nc.vector.wait_ge(B["xu_ready"], c + 1)
                nc.vector.tensor_tensor(X[:, sl, :], X[:, sl, :], bank[7][:].rearrange("p (t d) -> p t d", d=P),
                                        ALU.add).then_inc(x_ready, 1)

        def ssm_act():
            for c in range(C):
                nc.scalar.wait_ge(B["xt_turned"], c + 1)
                nc.scalar.activation(xT[:, c, :], bank[c][:], ACT.Identity, bias=col("n1b"),
                                     scale=col("n1w")).then_inc(B["xt_ready"], 1)
            nc.scalar.wait_ge(B["z_abs"], 1)
            nc.scalar.activation(zs[:, 2], zs[:, 1], ACT.Exp, scale=-1.0).then_inc(B["z_exp"], 1)
            nc.scalar.wait_ge(B["z_exp"], 1)
            nc.scalar.activation(zs[:, 3], zs[:, 2], ACT.Ln, bias=1.0).then_inc(B["z_ln"], 1)
            nc.scalar.wait_ge(B["delta_ready"], 1)
            nc.scalar.activation(zs[:, 4], zs[:, 3], ACT.Exp, scale=-1.0).then_inc(B["decay_ready"], 1)
            for c in range(C):
                pair = (4, 5) if c % 2 == 0 else (6, 0)
                for g, dst in ((0, gate), (1, gate2)):
                    nc.scalar.wait_ge(B["g_done"], 2 * c + g + 1)
                    nc.scalar.activation(dst[:, c, :], bank[pair[g]][:], ACT.Silu,
                                         bias=col("gate_b", g)).then_inc(B["silu_ready"], 1)
            for c in range(C):
                for g, dst in ((0, delta_b), (1, decay_b)):
                    nc.scalar.wait_ge(B["bc_done"], 2 * c + g + 1)
                    nc.scalar.activation(dst[:, c, :], bank[1 + g][:], ACT.Copy).then_inc(B["bc_copied"], 1)
            for c in range(C):
                nc.scalar.wait_ge(B["x2_turned"], c + 1)
                nc.scalar.activation(xT[:, c, :], bank[6][:] if c % 2 == 0 else bank[0][:], ACT.Identity,
                                     bias=col("n2b"), scale=col("n2w")).then_inc(B["x2_ready"], 1)
            for c in range(C + 1):
                if c < C:
                    if c >= 2:
                        nc.scalar.wait_ge(B["y_done"], c - 1)
                    for m in range(HK):
                        nc.scalar.wait_ge(B["g1_done"], HK * c + m + 1)
                        nc.scalar.activation(hid[:, (c % 2) * HK + m, :], bank[1 + m][:], ACT.Gelu,
                                             bias=col("mlp_b1", m)).then_inc(B["hf_ready"], 1)
                if c >= 1:
                    nc.scalar.wait_ge(B["y_done"], c)
                    if c >= 3:
                        nc.scalar.wait_ge(B["yt_done"], c - 2)
                    nc.scalar.activation(yfm[:, (c - 1) % 2, :], bank[5 + (c - 1) % 2][:], ACT.Identity,
                                         bias=col("mlp_b2")).then_inc(B["y_copied"], 1)

        def ssm_pool():
            nc.gpsimd.wait_ge(s_w0, 16 * 7)
            for c in range(C):
                sl = slice(JT * c, JT * c + JT)
                nc.gpsimd.wait_ge(B["xh_ready"], JT * c + JT)
                nc.gpsimd.tensor_tensor(U[:, sl, :], U[:, sl, :], outb_row[:].unsqueeze(1).to_broadcast([P, JT, P]),
                                        ALU.add).then_inc(B["u_b_ready"], 1)
            for c in range(C):
                sl = slice(JT * c, JT * c + JT)
                nc.gpsimd.wait_ge(B["x1_ready"], c + 1)
                nc.gpsimd.tensor_tensor(X[:, sl, :], X[:, sl, :], U[:, sl, :], ALU.add).then_inc(B["xu_ready"], 1)

        def ssm_pe():
            for c in range(C):
                for j in range(JT):
                    nc.tensor.wait_ge(B["xh_ready"], JT * c + j + 1)
                    ins = nc.tensor.transpose(bank[c][:, j * P:(j + 1) * P], XH[:, JT * c + j, :], ident[:])
                ins.then_inc(B["xt_turned"], 1)
            nc.tensor.wait_ge(B["z_done"], 1)
            for t in range(T):
                c, j = divmod(t, JT)
                nc.tensor.wait_ge(B["xt_ready"], c + 1)
                ins = nc.tensor.matmul(bank[7][:, t:t + 1], xT[:, c, j * P:(j + 1) * P], sbar[:, 0:1],
                                       start=True, stop=True)
            ins.then_inc(B["z_done"], 1)
            for c in range(C):
                pair = (4, 5) if c % 2 == 0 else (6, 0)
                if c >= 2:
                    nc.tensor.wait_ge(B["silu_ready"], 2 * (c - 1))
                for g in range(2):
                    nc.tensor.matmul(bank[pair[g]][:], gate_w[:, g * P:(g + 1) * P], xT[:, c, :], start=True,
                                     stop=True).then_inc(B["g_done"], 1)
            nc.tensor.wait_ge(B["decay_ready"], 1)
            for c in range(C):
                for g, k in ((0, 3), (1, 4)):
                    if c >= 1:
                        nc.tensor.wait_ge(B["bc_copied"], 2 * c - 1 + g)
                    for j in range(JT):
                        t = JT * c + j
                        ins = nc.tensor.transpose(bank[1 + g][:, j * P:(j + 1) * P],
                                                  zs[:, k, t:t + 1].to_broadcast([P, P]), ident[:])
                    ins.then_inc(B["bc_done"], 1)
                nc.tensor.wait_ge(B["xg_ready"], c + 1)
                if c >= 1:
                    nc.tensor.wait_ge(B["scan_ready"], c)
                nc.tensor.matmul(bank[7][:], state_w[:], gate2[:, c, :], start=True, stop=True)
                nc.tensor.matmul(bank[3][:], state_w[:], gate[:, c, :], start=True, stop=True).then_inc(B["ub_done"], 1)
            for c in range(C):
                nc.tensor.wait_ge(B["scan_ready"], c + 1)
                if c >= 2:
                    nc.tensor.wait_ge(B["x1_ready"], c - 1)
                for j in range(JT):
                    ins = nc.tensor.matmul(bank[4 + c % 2][:, j * P:(j + 1) * P], states[:, c, j * P:(j + 1) * P],
                                           out_w[:], start=True, stop=True)
                ins.then_inc(B["ssm_done"], 1)
            for c in range(C):
                if c >= 2:
                    nc.tensor.wait_ge(B["x2_ready"], c - 1)
                for j in range(JT):
                    nc.tensor.wait_ge(B["xh2_ready"], JT * c + j + 1)
                    ins = nc.tensor.transpose((bank[6] if c % 2 == 0 else bank[0])[:, j * P:(j + 1) * P],
                                              XH[:, JT * c + j, :], ident[:])
                ins.then_inc(B["x2_turned"], 1)
            for c in range(C + 2):
                if c < C:
                    nc.tensor.wait_ge(B["x2_ready"], C if c else 1)
                    for m in range(HK):
                        if c >= 1:
                            nc.tensor.wait_ge(B["hf_ready"], HK * (c - 1) + m + 1)
                        nc.tensor.matmul(bank[1 + m][:], mlp_w1[:, m * P:(m + 1) * P], xT[:, c, :], start=True,
                                         stop=True).then_inc(B["g1_done"], 1)
                if 1 <= c <= C:
                    if c >= 3:
                        nc.tensor.wait_ge(B["y_copied"], c - 2)
                    for m in range(HK):
                        nc.tensor.wait_ge(B["hf_ready"], HK * (c - 1) + m + 1)
                        ins = nc.tensor.matmul(bank[5 + (c - 1) % 2][:], mlp_w2[:, m, :],
                                               hid[:, ((c - 1) % 2) * HK + m, :], start=(m == 0), stop=(m == HK - 1))
                    ins.then_inc(B["y_done"], 1)
                if c >= 2:
                    nc.tensor.wait_ge(B["y_copied"], c - 1)
                    if c >= 3:
                        nc.tensor.wait_ge(x_ready, C + c - 2)
                    for j in range(JT):
                        ins = nc.tensor.transpose(bank[7][:, j * P:(j + 1) * P],
                                                  yfm[:, (c - 2) % 2, j * P:(j + 1) * P], ident[:])
                    ins.then_inc(B["yt_done"], 1)

        comb = arena[:, 4:12, :]
        disp = arena[:, 12:20, :]
        dispT = arena[:, 20:24, :]
        combT = arena[:, 24:40, :]
        hid_s = arena[:, 4:8, :].rearrange("p (q h) (b n) -> p q (h b) n", q=2, b=2)
        eoT = arena[:, 8:12, :]
        eo = arena[:, 12:16, :].rearrange("p c (s d) -> p c s d", d=P)

        def soft_sems(n):
            names = ("xh_ready xt_turned xt_ready lg_done nm_ready exp_done dt_ready tr_done ct_ready d_ready "
                     "slots_done slots_ready wload0 wload1 g1_done hf_ready y_done eot_ready eo_turned eo_ready out_done").split()
            return {k: sem(f"{k}_{n}") for k in names}

        F = [soft_sems("soft0"), soft_sems("soft1")]
        slots_ld = sem("slots_ld")
        sn_ready = sem("sn_ready")
        sn_turned = sem("sn_turned")
        sn_copied = sem("sn_copied")

        def slots_dve():
            se = U[:, 0:JT, :]
            nc.vector.wait_ge(slots_ld, 16)
            for t in range(JT):
                last = nc.vector.bn_stats(stats[:, t, :], se[:, t, :])
            link(last)
            for t in range(JT):
                last = nc.vector.bn_aggr(mv[:, t, :], stats[:, t, :])
            link(last)
            r = [rs[:, k, 0:JT] for k in range(3)]
            link(nc.vector.tensor_tensor(r[1], mv[:, 0:JT, 0], mv[:, 0:JT, 0], ALU.mult))
            link(nc.vector.tensor_tensor(r[1], r[1], mv[:, 0:JT, 1], ALU.add))
            link(nc.vector.tensor_scalar(r[1], r[1], float(P), 1e-30, ALU.mult, ALU.max))
            dve_rsqrt(r[0], r[1], r[2])
            link(nc.vector.tensor_scalar(r[0], r[0], 1e12, SCALE, ALU.min, ALU.mult))
            for t in range(JT):
                nc.vector.tensor_scalar(U[:, JT + t, :], se[:, t, :], rs[:, 0, t:t + 1], None,
                                        ALU.mult).then_inc(sn_ready, 1)

        def slots_pe():
            nc.tensor.wait_ge(sn_ready, JT)
            for t in range(JT):
                ins = nc.tensor.transpose(bank[7][:, t * P:(t + 1) * P], U[:, JT + t, :], ident[:])
            ins.then_inc(sn_turned, 1)

        def slots_act():
            nc.scalar.wait_ge(b_copied, 1)
            nc.scalar.wait_ge(sn_turned, 1)
            nc.scalar.activation(snT[:], bank[7][:], ACT.Copy, scale=col("slot_gamma")).then_inc(sn_copied, 1)

        def soft_dve(S, at, whole):
            if whole:
                nc.vector.wait_ge(x_ready, at + C)
            dve_stats(X, x_ready, None if whole else at)
            link(nc.vector.tensor_scalar(row(1), mv[:, :, 1], 1e-5, None, ALU.add))
            dve_rsqrt(row(0), row(1), row(2))
            link(nc.vector.tensor_tensor(row(3), row(0), row(0), ALU.mult))
            link(nc.vector.tensor_tensor(row(3), row(3), mv[:, :, 1], ALU.mult))
            link(nc.vector.tensor_scalar(row(3), row(3), float(P), 1e-30, ALU.mult, ALU.max))
            dve_rsqrt(row(1), row(3), row(2))
            link(nc.vector.tensor_scalar(row(1), row(1), 1e12, SCALE, ALU.min, ALU.mult))
            link(nc.vector.tensor_tensor(row(0), row(0), row(1), ALU.mult))
            for t in range(T):
                nc.vector.tensor_scalar(XH[:, t, :], X[:, t, :], mv[:, t, 0:1], rs[:, 0, t:t + 1],
                                        ALU.subtract, ALU.mult).then_inc(S["xh_ready"], 1)

            def maxima(b):
                for k in range(8):
                    nc.vector.wait_ge(S["lg_done"], 8 * b + k + 1)
                    nc.vector.tensor_reduce(nmax[:, b, k:k + 1], bank[k % 4][:], AX_X, ALU.max,
                                            negate=True).then_inc(S["nm_ready"], 1)

            def scale_dispatch(b):
                nc.vector.wait_ge(S["exp_done"], 8 * b + 8)
                link(nc.vector.reciprocal(sums[:, b, 4:8], sums[:, b, 4:8]))
                for st in range(4):
                    d = disp[:, 4 * (b % 2) + st, :]
                    nc.vector.tensor_scalar(d, d, sums[:, b, 4 + st:5 + st], None, ALU.mult).then_inc(S["dt_ready"], 1)

            maxima(0)
            scale_dispatch(0)
            for b in range(C):
                if b < C - 1:
                    maxima(b + 1)
                for st in range(4):
                    nc.vector.wait_ge(S["tr_done"], 8 * b + st + 1)
                    nc.vector.tensor_copy(combT[:, 4 * b + st, :], bank[4 + st % 2][:]).then_inc(S["ct_ready"], 1)
                if b < C - 1:
                    scale_dispatch(b + 1)
            link(nc.vector.reciprocal(sums[:, :, 0:4], sums[:, :, 0:4]))
            link(nc.vector.tensor_scalar(sums[:, :, 0:4], sums[:, :, 0:4], 0.5, None, ALU.mult))
            for e in range(E):
                nc.vector.wait_ge(S["y_done"], e + 1)
                dst = eoT[:, :, e * S_PER:(e + 1) * S_PER]
                nc.vector.tensor_scalar(dst, bank[4 + e % 2][:, 0:NB].rearrange("p (b s) -> p b s", b=C),
                                        cols_of("b2_1")[:, e:e + 1], None, ALU.add).then_inc(S["eot_ready"], 1)
            for c in range(C):
                nc.vector.wait_ge(S["out_done"], c + 1)
                for j in range(JT):
                    t = JT * c + j
                    ins = nc.vector.scalar_tensor_tensor(
                        out=X[:, t, :], in0=bank[c][:, j * P:(j + 1) * P], scalar=sums[:, c, j:j + 1],
                        in1=X[:, t, :], op0=ALU.mult, op1=ALU.add)
                ins.then_inc(x_ready, 1)

        def soft_act(S):
            for c in range(C):
                nc.scalar.wait_ge(S["xt_turned"], c + 1)
                nc.scalar.activation(xT[:, c, :], bank[c][:], ACT.Copy, scale=col("gamma")).then_inc(S["xt_ready"], 1)

            def exps(b):
                for k in range(8):
                    nc.scalar.wait_ge(S["nm_ready"], 8 * b + k + 1)
                    if b >= 2:
                        nc.scalar.wait_ge(S["tr_done"], 8 * (b - 2) + (4 if k < 4 else 8))
                    dst = (comb if k < 4 else disp)[:, 4 * (b % 2) + k % 4, :]
                    nc.scalar.activation(dst, bank[k % 4][:], ACT.Exp, bias=nmax[:, b, k:k + 1],
                                         accum_out=sums[:, b, k:k + 1]).then_inc(S["exp_done"], 1)

            exps(0)
            for b in range(C):
                if b < C - 1:
                    exps(b + 1)
                for nt in range(JT):
                    nc.scalar.wait_ge(S["tr_done"], 8 * b + 4 + nt + 1)
                    if b >= 1:
                        nc.scalar.wait_ge(S["slots_done"], b)
                    nc.scalar.activation(dispT[:, nt, :], bank[4 + nt % 2][:], ACT.Copy).then_inc(S["d_ready"], 1)
                nc.scalar.wait_ge(S["slots_done"], b + 1)
                nc.scalar.activation(slotsT[:, :, b, :], bank[6][:].rearrange("p (e s) -> p e s", e=E), ACT.Copy,
                                     scale=col("gamma")).then_inc(S["slots_ready"], 1)
            for e in range(E):
                if e >= 2:
                    nc.scalar.wait_ge(S["y_done"], e - 1)
                for m in range(HK):
                    nc.scalar.wait_ge(S["g1_done"], HK * e + m + 1)
                    nc.scalar.activation(hid_s[:, e % 2, m, :], bank[m][:, 0:NB],
                                         ACT.Gelu, bias=cols_of("b1_1")[:, HK * e + m:HK * e + m + 1]).then_inc(S["hf_ready"], 1)
            for c in range(C):
                nc.scalar.wait_ge(S["eo_turned"], c + 1)
                nc.scalar.activation(eo[:, c, :, :], bank[6 + c % 2][:].rearrange("p (s d) -> p s d", d=P),
                                     ACT.Copy).then_inc(S["eo_ready"], 1)

        def soft_pe(S):
            for c in range(C):
                for j in range(JT):
                    nc.tensor.wait_ge(S["xh_ready"], JT * c + j + 1)
                    ins = nc.tensor.transpose(bank[c][:, j * P:(j + 1) * P], XH[:, JT * c + j, :], ident[:])
                ins.then_inc(S["xt_turned"], 1)
            nc.tensor.wait_ge(sn_copied, 1)

            def logits(b):
                nc.tensor.wait_ge(S["xt_ready"], C)
                for k in range(8):
                    n = 8 * b + k
                    if n >= 4:
                        nc.tensor.wait_ge(S["exp_done"], n - 3)
                    blk = slice((k % 4) * P, (k % 4 + 1) * P)
                    if k < 4:
                        ins = nc.tensor.matmul(bank[k][:], xT[:, b, blk], snT[:], start=True, stop=True)
                    else:
                        ins = nc.tensor.matmul(bank[k - 4][:], snT[:, blk], xT[:, b, :], start=True, stop=True)
                    ins.then_inc(S["lg_done"], 1)

            logits(0)
            for b in range(C):
                if b < C - 1:
                    logits(b + 1)
                for j in range(8):
                    if j < 2 and b >= 1:
                        nc.tensor.wait_ge(S["d_ready"], 4 * (b - 1) + 3 + j)
                    elif 2 <= j < 6:
                        nc.tensor.wait_ge(S["ct_ready"], 4 * b + j - 1)
                    elif j >= 6:
                        nc.tensor.wait_ge(S["d_ready"], 4 * b + j - 5)
                    if j < 4:
                        nc.tensor.wait_ge(S["exp_done"], 8 * b + 4)
                    else:
                        nc.tensor.wait_ge(S["dt_ready"], 4 * b + 4)
                    src = comb if j < 4 else disp
                    for k in range(4):
                        ins = nc.tensor.transpose(bank[4 + j % 2][:, k * P:(k + 1) * P],
                                                  src[:, 4 * (b % 2) + k, (j % 4) * P:(j % 4 + 1) * P], ident[:])
                    ins.then_inc(S["tr_done"], 1)
                if b >= 1:
                    nc.tensor.wait_ge(S["slots_ready"], b)
                for nt in range(JT):
                    nc.tensor.wait_ge(S["d_ready"], 4 * b + nt + 1)
                    ins = nc.tensor.matmul(bank[6][:], XH[:, JT * b + nt, :], dispT[:, nt, :], start=(nt == 0),
                                           stop=(nt == JT - 1))
                ins.then_inc(S["slots_done"], 1)

            def g1(e):
                nc.tensor.wait_ge(S["wload1"] if e % 2 else S["wload0"], 32 * (e // 2 + 1))
                for m in range(HK):
                    if e >= 1:
                        nc.tensor.wait_ge(S["hf_ready"], HK * (e - 1) + m + 1)
                    nc.tensor.matmul(bank[m][:, 0:NB],
                                     wraw[e % 2][:, 0, m * P:(m + 1) * P],
                                     slotsT[:, e, :, :], start=True, stop=True).then_inc(S["g1_done"], 1)

            nc.tensor.wait_ge(S["slots_ready"], C)
            nc.tensor.wait_ge(S["exp_done"], 8 * C)
            nc.tensor.wait_ge(S["ct_ready"], 4 * C)
            g1(0)
            for e in range(E):
                if e < E - 1:
                    g1(e + 1)
                if e >= 2:
                    nc.tensor.wait_ge(S["eot_ready"], e - 1)
                for m in range(HK):
                    nc.tensor.wait_ge(S["hf_ready"], HK * e + m + 1)
                    ins = nc.tensor.matmul(bank[4 + e % 2][:, 0:NB], wraw[e % 2][:, 1, m * P:(m + 1) * P],
                                           hid_s[:, e % 2, m, :], start=(m == 0), stop=(m == HK - 1))
                ins.then_inc(S["y_done"], 1)
            nc.tensor.wait_ge(S["eot_ready"], E)
            for c in range(C):
                if c >= 2:
                    nc.tensor.wait_ge(S["eo_ready"], c - 1)
                for k in range(4):
                    ins = nc.tensor.transpose(bank[6 + c % 2][:, k * P:(k + 1) * P], eoT[:, c, k * P:(k + 1) * P], ident[:])
                ins.then_inc(S["eo_turned"], 1)
            for c in range(C):
                nc.tensor.wait_ge(S["eo_ready"], c + 1)
                for nt in range(JT):
                    for k in range(4):
                        ins = nc.tensor.matmul(bank[c][:, nt * P:(nt + 1) * P], combT[:, 4 * c + k, nt * P:(nt + 1) * P],
                                               eo[:, c, k, :], start=(k == 0), stop=(k == 3))
                ins.then_inc(S["out_done"], 1)

        def soft_sp(S):
            w1, w2 = A["L1_ffn_w1"], A["L1_ffn_w2"].rearrange("e (m h) d -> e h m d", h=P)
            for e in range(E):
                wl_sem = S["wload1"] if e % 2 else S["wload0"]
                if e >= 2:
                    nc.sync.wait_ge(S["y_done"], e - 1)
                nc.sync.dma_start(wraw[e % 2][:, 0, :], w1[e]).then_inc(wl_sem, 16)
                nc.sync.dma_start(wraw[e % 2][:, 1, :].rearrange("p (m d) -> p m d", d=P), w2[e]).then_inc(wl_sem, 16)

        N5 = LAYERS * 2
        A5 = 8
        W5 = 2 * P
        G5 = 2 * H
        flat = "p a n -> p (a n)"
        hT = arena[:, 0:2, :].rearrange(flat)
        oT = arena[:, 2:4, :].rearrange(flat)
        h2T = arena[:, 4:6, :].rearrange(flat)
        sgate = arena[:, 6:8, :]
        gact = arena[:, 8:14, :].rearrange("p (m a) n -> p m (a n)", m=3)
        qkv = [arena[:, a:a + 6, :].rearrange(flat).rearrange("p (a r) -> p a r", a=A5) for a in (14, 20)]
        sq = arena[:, 26:30, :].rearrange(flat)
        prod = arena[:, 30:38, :].rearrange(flat).rearrange("p (x n) -> p x n", n=W5)
        u5 = arena[:, 38:40, :].rearrange(flat).rearrange("p (t n) -> p t n", n=W5)
        th = sb("th", [P, 2, A5, H])
        coef = sb("coef", [P, 16, G5])
        small5 = gsm[:].rearrange("p z t e -> p (z t e)")[:, 0:3 * A5 * G5].rearrange("p (z n) -> p z n", z=3)
        junk = [z[:].rearrange("p a b -> p (a b)") for z in (G, WE)]
        ssq = sb("ssq", [P, 2, A5])
        nhalf = sb("nhalf", [P, T])
        grouped = "p (t g i) d -> p t g (i d)"
        X5, U5, XH5 = (z[:].rearrange(grouped, g=2, i=2) for z in (X, U, XH))
        KK_AT = [0, 3, 5]
        KQ_AT = [6, 10, 13, 15]
        D5 = {k: sem(k + "_delta") for k in (
            "u_ready squared rms_ready xh_ready xh2_ready turned cols_ready qkv_done qkv_ready sq_ready qk_scaled "
            "vb_ready kq_ready coef_ready step_ready o_raw o_ready wo_done gy_done sg_ready act_ready wd_done "
            "beta_ready").split()}
        TURNS = [("h", 0), ("h", 1), ("o", 0), ("x", 0), ("h", 2), ("o", 1), ("x", 1), ("h", 3), ("o", 2), ("x", 2),
                 ("o", 3), ("x", 3)]
        NORMS = [("h", 0), ("h", 1), ("x", 0), ("h", 2), ("x", 1), ("h", 3), ("x", 2), ("f", 2), ("x", 3), ("f", 3)]

        def turns(what, n, half):
            return 2 * TURNS.index((what, n)) + half + 1

        def norms(what, n):
            return NORMS.index((what, n)) + 1

        def u_at(n, halves):
            return T + 4 * n + halves

        s_w1 = sem("s_w1")

        def plink(ins):
            chain_at["pool"] += 1
            ins.then_inc(pool_chain, 1)
            nc.gpsimd.wait_ge(pool_chain, chain_at["pool"])

        def tile5(z, n, a):
            t = JT * (a // 2) + 2 * (n % 2) + a % 2
            return z[:, t, :]

        def hk(ap):
            return ap.rearrange("p m (g k) -> p m g k", k=DK)

        def spread(at_, m):
            return coef[:, at_:at_ + m].unsqueeze(3).to_broadcast([P, m, G5, DK])

        def delta_dve(at):
            dve_stats(X, x_ready, at)
            link(nc.vector.tensor_scalar(row(1), mv[:, :, 1], 1e-5, None, ALU.add))
            dve_rsqrt(row(0), row(1), row(2))
            for t in range(T):
                nc.vector.tensor_scalar(U[:, t, :], X[:, t, :], mv[:, t, 0:1], rs[:, 0, t:t + 1],
                                        ALU.subtract, ALU.mult).then_inc(D5["u_ready"], 1)
            nc.vector.wait_ge(D5["u_ready"], T)

            def norm_qk(n):
                nc.vector.wait_ge(D5["sq_ready"], n + 1)
                ss, r, t_ = small5[:, 0, :], small5[:, 1, :], small5[:, 2, :]
                link(nc.vector.tensor_reduce(ss, sq.rearrange("p (g k) -> p g k", k=DK), AX_X, ALU.add))
                link(nc.vector.tensor_scalar(ss, ss, 1e-6, None, ALU.add))
                dve_rsqrt(r, ss, t_)
                qk = qkv[n % 2][:, :, 0:W5].rearrange("p a (g k) -> p a g k", k=DK)
                nc.vector.tensor_tensor(qk, qk, r.rearrange("p (a g) -> p a g", a=A5).unsqueeze(3).to_broadcast(
                    [P, A5, G5, DK]), ALU.mult).then_inc(D5["qk_scaled"], 1)
                nc.vector.wait_ge(D5["qk_scaled"], n + 1)

            def solve(n):
                k = qkv[n % 2][:, :, P:W5].rearrange("p (t i) n -> p t i n", i=2)
                pr = prod.rearrange("p x (i n) -> p x i n", i=2)
                for s_ in range(C - 1):
                    m = C - 1 - s_
                    last = nc.vector.tensor_tensor(pr[:, KK_AT[s_]:KK_AT[s_] + m], k[:, s_ + 1:],
                                                   k[:, s_:s_ + 1].to_broadcast([P, m, 2, P]), ALU.mult)
                link(last)
                link(nc.vector.tensor_reduce(coef[:, 0:6], hk(prod[:, 0:6]), AX_X, ALU.add))
                nc.vector.wait_ge(D5["beta_ready"], n + 1)
                b = th[:, n % 2].rearrange("p (t i) h -> p t (i h)", i=2)
                for s_ in range(C - 1):
                    a = coef[:, KK_AT[s_]:KK_AT[s_] + C - 1 - s_]
                    last = nc.vector.tensor_tensor(a, a, b[:, s_ + 1:], ALU.mult)
                link(last)
                nc.vector.wait_ge(D5["vb_ready"], n + 1)
                tmp5 = hk(prod[:, 0:3])
                u = hk(u5)
                for s_ in range(C - 1):
                    m = C - 1 - s_
                    link(nc.vector.tensor_tensor(tmp5[:, 0:m], spread(KK_AT[s_], m),
                                                 u[:, s_:s_ + 1].to_broadcast([P, m, G5, DK]), ALU.mult))
                    nc.vector.tensor_tensor(u[:, s_ + 1:], u[:, s_ + 1:], tmp5[:, 0:m],
                                            ALU.subtract).then_inc(D5["step_ready"], 1)
                    nc.vector.wait_ge(D5["step_ready"], (C - 1) * n + s_ + 1)

            def query_coefs(n):
                nc.vector.wait_ge(D5["kq_ready"], n + 1)
                nc.vector.tensor_reduce(coef[:, 6:16], hk(prod[:, 6:16]), AX_X, ALU.add).then_inc(D5["coef_ready"], 1)

            def norm_o(n):
                nc.vector.wait_ge(D5["o_raw"], n + 1)
                o = hk(XH5[:, :, n % 2, :])
                sqo = hk(prod[:, 0:4])
                link(nc.vector.tensor_tensor(sqo, o, o, ALU.mult))
                ss, r, t_ = (small5[:, k, 0:C * G5] for k in range(3))
                link(nc.vector.tensor_reduce(ss.rearrange("p (t h) -> p t h", t=C), sqo, AX_X, ALU.add))
                link(nc.vector.tensor_scalar(ss, ss, 1.0 / DK, 1e-6, ALU.mult, ALU.add))
                dve_rsqrt(r, ss, t_)
                nc.vector.tensor_tensor(o, o, r.rearrange("p (t h) -> p t h", t=C).unsqueeze(3).to_broadcast(
                    [P, C, G5, DK]), ALU.mult).then_inc(D5["o_ready"], 1)

            def add_psum(n, b0, b1):
                for half, b in enumerate((b0, b1)):
                    u = U5[:, 2 * half:2 * half + 2, n % 2, :]
                    nc.vector.tensor_tensor(u, u, bank[b][:].rearrange("p (t n) -> p t n", t=2), ALU.add).then_inc(D5["u_ready"], 1)

            def xh2(n):
                nc.vector.wait_ge(D5["rms_ready"], norms("x", n))
                for a in range(A5):
                    nc.vector.tensor_scalar(tile5(XH, n, a), tile5(U, n, a), ssq[:, 1, a:a + 1], None,
                                            ALU.mult).then_inc(D5["xh2_ready"], 1)

            def gated(n):
                for k in range(6):
                    m, half = divmod(k, 2)
                    w = FB[m][1]
                    nc.vector.wait_ge(D5["sg_ready"], 6 * n + k + 1)
                    if k == 0 and n >= 1:
                        nc.vector.wait_ge(D5["wd_done"], n)
                    nc.vector.tensor_tensor(gact[0:w, m, half * CH:(half + 1) * CH], bank[4 + k % 2][0:w, :],
                                            sgate[0:w, k % 2, :], ALU.mult).then_inc(D5["act_ready"], 1)

            def finish(n):
                nc.vector.wait_ge(D5["rms_ready"], norms("f", n))
                for a in range(A5):
                    last = nc.vector.scalar_tensor_tensor(out=tile5(XH, n, a), in0=tile5(U, n, a),
                                                          scalar=ssq[:, 0, a:a + 1], in1=final_row[:],
                                                          op0=ALU.mult, op1=ALU.mult)
                link(last)
                x = X5[:, :, n % 2, :]
                nc.vector.tensor_tensor(x, x, XH5[:, :, n % 2, :], ALU.add).then_inc(x_ready, 2)

            for n in range(N5 + 1):
                if n < N5:
                    norm_qk(n)
                if n >= 1:
                    nc.vector.wait_ge(D5["wo_done"], n)
                    add_psum(n - 1, 6, 7)
                if n < N5:
                    solve(n)
                if n >= 1:
                    xh2(n - 1)
                if n < N5:
                    query_coefs(n)
                if n >= 1:
                    gated(n - 1)
                    nc.vector.wait_ge(D5["wd_done"], n)
                    add_psum(n - 1, 0, 1)
                if n < N5:
                    norm_o(n)
                if n - 1 >= N5 - 2:
                    finish(n - 1)

        def delta_act():
            def squares(what, n, which):
                before = A5 * (norms(what, n) - 1)
                for a in range(A5):
                    if a >= 2:
                        nc.scalar.wait_ge(D5["squared"], before + a - 1)
                    ins = nc.scalar.activation(junk[a % 2], tile5(U, n, a), ACT.Square,
                                               accum_out=ssq[:, which, a:a + 1])
                    ins.then_inc(D5["squared"], 1)

            def project(n):
                nc.scalar.wait_ge(D5["u_ready"], u_at(n - 2, 4) if n >= 2 else T)
                squares("h", n, 0)
                nc.scalar.wait_ge(D5["rms_ready"], norms("h", n))
                for a in range(A5):
                    nc.scalar.activation(tile5(XH, n, a), tile5(U, n, a), ACT.Copy,
                                         scale=ssq[:, 0, a:a + 1]).then_inc(D5["xh_ready"], 1)
                for half in range(2):
                    nc.scalar.wait_ge(D5["turned"], turns("h", n, half))
                    nc.scalar.activation(hT[:, half * CH:(half + 1) * CH], bank[half][:], ACT.Copy,
                                         scale=col("r1w", n // 2)).then_inc(D5["cols_ready"], 1)
                for a in range(A5):
                    nc.scalar.wait_ge(D5["qkv_done"], A5 * n + a + 1)
                    src = bank[2 + a % 2]
                    if n >= 2 and a == 0:
                        nc.scalar.wait_ge(D5["o_ready"], n - 1)
                    nc.scalar.activation(qkv[n % 2][:, a, :], src[:, 0:3 * P], ACT.Silu)
                    nc.scalar.activation(th[:, n % 2, a, :], src[:, 3 * P:3 * P + H], ACT.Tanh,
                                         scale=0.5).then_inc(D5["qkv_ready"], 1)
                nc.scalar.wait_ge(D5["qkv_ready"], A5 * n + A5)
                if n >= 1:
                    nc.scalar.wait_ge(D5["qk_scaled"], n)
                nc.scalar.activation(sq.rearrange("p (a n) -> p a n", a=A5), qkv[n % 2][:, :, 0:W5],
                                     ACT.Square).then_inc(D5["sq_ready"], 1)

            project(0)
            for n in range(N5 + 1):
                if n == 0:
                    project(1)
                    continue
                i = n - 1
                for half in range(2):
                    nc.scalar.wait_ge(D5["turned"], turns("o", i, half))
                    nc.scalar.activation(oT[:, half * CH:(half + 1) * CH], bank[4 + half][:], ACT.Copy,
                                         scale=col("onorm", i // 2)).then_inc(D5["cols_ready"], 1)
                nc.scalar.wait_ge(D5["u_ready"], u_at(i, 2))
                squares("x", i, 1)
                for half in range(2):
                    nc.scalar.wait_ge(D5["turned"], turns("x", i, half))
                    nc.scalar.activation(h2T[:, half * CH:(half + 1) * CH], bank[4 + half][:], ACT.Copy,
                                         scale=col("r2w", i // 2)).then_inc(D5["cols_ready"], 1)
                for k in range(6):
                    w = FB[k // 2][1]
                    nc.scalar.wait_ge(D5["gy_done"], 6 * i + k + 1)
                    if 6 * i + k >= 2:
                        nc.scalar.wait_ge(D5["act_ready"], 6 * i + k - 1)
                    nc.scalar.activation(sgate[0:w, k % 2, :], bank[6 + k % 2][0:w, :],
                                         ACT.Silu).then_inc(D5["sg_ready"], 1)
                if 2 <= n + 1 < N5:
                    project(n + 1)
                elif i >= N5 - 2:
                    nc.scalar.wait_ge(D5["u_ready"], u_at(i, 4))
                    if i == N5 - 1:
                        nc.scalar.wait_ge(x_ready, 4 * C + 2)
                    squares("f", i, 0)

        def delta_pool():
            def factors(what, n, which):
                nc.gpsimd.wait_ge(D5["squared"], A5 * norms(what, n))
                v = ssq[:, which, :]
                plink(nc.gpsimd.tensor_scalar(v, v, 1.0 / P, 1e-6, ALU.mult, ALU.add))
                nc.gpsimd.tensor_tensor(v, v, nhalf[:, 0:A5], ALU.pow).then_inc(D5["rms_ready"], 1)

            def beta_v(n):
                nc.gpsimd.wait_ge(D5["sq_ready"], n + 1)
                b = th[:, n % 2]
                nc.gpsimd.tensor_scalar(b, b, 1.0, None, ALU.add).then_inc(D5["beta_ready"], 1)
                nc.gpsimd.wait_ge(D5["beta_ready"], n + 1)
                v = qkv[n % 2][:, :, W5:3 * P].rearrange("p a (h k) -> p a h k", k=DK)
                nc.gpsimd.tensor_tensor(u5.rearrange("p t (i h k) -> p (t i) h k", i=2, k=DK), v,
                                        b.unsqueeze(3).to_broadcast([P, A5, H, DK]), ALU.mult).then_inc(D5["vb_ready"], 1)

            def query_products(n):
                nc.gpsimd.wait_ge(D5["qk_scaled"], n + 1)
                q, k = (qkv[n % 2][:, :, z * P:(z + 1) * P].rearrange("p (t i) n -> p t i n", i=2) for z in (0, 1))
                pr = prod.rearrange("p x (i n) -> p x i n", i=2)
                for s_ in range(C):
                    m = C - s_
                    ins = nc.gpsimd.tensor_tensor(pr[:, KQ_AT[s_]:KQ_AT[s_] + m], q[:, s_:],
                                                  k[:, s_:s_ + 1].to_broadcast([P, m, 2, P]), ALU.mult)
                ins.then_inc(D5["kq_ready"], 1)

            def outputs(n):
                nc.gpsimd.wait_ge(D5["coef_ready"], n + 1)
                if n >= 2:
                    nc.gpsimd.wait_ge(D5["turned"], turns("x", n - 2, 1))
                u = hk(u5)
                o = hk(XH5[:, :, n % 2, :])
                part = hk(prod[:, 6:10])
                plink(nc.gpsimd.tensor_tensor(o, spread(KQ_AT[0], C), u[:, 0:1].to_broadcast([P, C, G5, DK]), ALU.mult))
                for s_ in range(1, C):
                    m = C - s_
                    nc.gpsimd.wait_ge(D5["step_ready"], (C - 1) * n + s_)
                    plink(nc.gpsimd.tensor_tensor(part[:, 0:m], spread(KQ_AT[s_], m),
                                                  u[:, s_:s_ + 1].to_broadcast([P, m, G5, DK]), ALU.mult))
                    ins = nc.gpsimd.tensor_tensor(o[:, s_:], o[:, s_:], part[:, 0:m], ALU.add)
                    if s_ < C - 1:
                        plink(ins)
                    else:
                        ins.then_inc(D5["o_raw"], 1)
                        nc.gpsimd.wait_ge(D5["o_raw"], n + 1)

            factors("h", 0, 0)
            for n in range(N5 + 1):
                if n == 0:
                    factors("h", 1, 0)
                if n < N5:
                    beta_v(n)
                    query_products(n)
                if n >= 1:
                    factors("x", n - 1, 1)
                if n < N5:
                    outputs(n)
                if n >= 1:
                    factors(*(("h", n + 1) if n + 1 < N5 else ("f", n - 1)), 0)

        def delta_pe():
            def project(n):
                lay = n // 2
                if n >= 2:
                    nc.tensor.wait_ge(D5["u_ready"], u_at(n - 2, 4))
                if n >= 1:
                    nc.tensor.wait_ge(D5["cols_ready"], turns("h", n - 1, 1))
                for a in range(A5):
                    nc.tensor.wait_ge(D5["xh_ready"], A5 * n + a + 1)
                    ins = nc.tensor.transpose(bank[a // 4][:, (a % 4) * P:(a % 4 + 1) * P], tile5(XH, n, a), ident[:])
                    if a % 4 == 3:
                        ins.then_inc(D5["turned"], 1)
                for a in range(A5):
                    nc.tensor.wait_ge(D5["cols_ready"], turns("h", n, a // 4))
                    k = A5 * n + a
                    if k >= 2:
                        nc.tensor.wait_ge(D5["qkv_ready"], k - 1)
                    nc.tensor.matmul(bank[2 + a % 2][:, 0:3 * P + H], hT[:, a * P:(a + 1) * P], qkvb[:, lay, :],
                                     start=True, stop=True).then_inc(D5["qkv_done"], 1)

            nc.tensor.wait_ge(s_w1, 16 * W1_LOADS)
            project(0)
            for n in range(N5 + 1):
                if n == 0:
                    project(1)
                    continue
                i = n - 1
                lay = i // 2
                nc.tensor.wait_ge(D5["o_ready"], i + 1)
                if i >= 1:
                    nc.tensor.wait_ge(D5["act_ready"], 6 * i)
                for a in range(A5):
                    ins = nc.tensor.transpose(bank[4 + a // 4][:, (a % 4) * P:(a % 4 + 1) * P], tile5(XH, i, a), ident[:])
                    if a % 4 == 3:
                        ins.then_inc(D5["turned"], 1)
                for a in range(A5):
                    nc.tensor.wait_ge(D5["cols_ready"], turns("o", i, a // 4))
                    ins = nc.tensor.matmul(bank[6 + a // 4][:, (a % 4) * P:(a % 4 + 1) * P], oT[:, a * P:(a + 1) * P],
                                           wo[:, lay, :], start=True, stop=True)
                ins.then_inc(D5["wo_done"], 1)
                for a in range(A5):
                    nc.tensor.wait_ge(D5["xh2_ready"], A5 * i + a + 1)
                    ins = nc.tensor.transpose(bank[4 + a // 4][:, (a % 4) * P:(a % 4 + 1) * P], tile5(XH, i, a), ident[:])
                    if a % 4 == 3:
                        ins.then_inc(D5["turned"], 1)
                for k in range(6):
                    m, half = divmod(k, 2)
                    at_, w = FB[m]
                    nc.tensor.wait_ge(D5["cols_ready"], turns("x", i, half))
                    if k >= 2:
                        nc.tensor.wait_ge(D5["act_ready"], 6 * i + k - 1)
                    h = h2T[:, half * CH:(half + 1) * CH]
                    nc.tensor.matmul(bank[6 + k % 2][0:w, :], wg[:, lay, at_:at_ + w], h, start=True, stop=True)
                    nc.tensor.matmul(bank[4 + k % 2][0:w, :], wg[:, lay, FF + at_:FF + at_ + w], h, start=True,
                                     stop=True).then_inc(D5["gy_done"], 1)
                nc.tensor.wait_ge(D5["act_ready"], 6 * n)
                for a in range(A5):
                    for m, (_, w) in enumerate(FB):
                        ins = nc.tensor.matmul(bank[a // 4][:, (a % 4) * P:(a % 4 + 1) * P],
                                               gact[0:w, m, a * P:(a + 1) * P], wd[0:w, lay, m, :],
                                               start=(m == 0), stop=(m == len(FB) - 1))
                ins.then_inc(D5["wd_done"], 1)
                if 2 <= n + 1 < N5:
                    project(n + 1)

        W1_LOADS = LAYERS * 8 + 1

        def delta_sp():
            for k in range(LAYERS):
                for n, name in enumerate(("Wq", "Wk", "Wv")):
                    nc.sync.dma_start(qkvb[:, k, n * P:(n + 1) * P], A["L1_attn_" + name][k]).then_inc(s_w1, 16)
                nc.sync.dma_start(qkvb[:, k, 3 * P:], A["L1_attn_Wb"][k]).then_inc(s_w1, 16)
                nc.sync.dma_start(wo[:, k, :], A["L1_attn_Wo"][k]).then_inc(s_w1, 16)
                nc.sync.dma_start(wg[:, k, :], A["L1_attn_Wg"][k]).then_inc(s_w1, 16)
                nc.sync.dma_start(wd[:, k, 0:2, :], A["L1_attn_Wd"][k, 0:256, :].rearrange("(m h) d -> h m d", h=P)
                                  ).then_inc(s_w1, 16)
                nc.sync.dma_start(wd[0:96, k, 2, :], A["L1_attn_Wd"][k, 256:FF, :]).then_inc(s_w1, 16)
            nc.sync.dma_start(final_row[:], A["L1_attn_final_norm_w"].unsqueeze(0).to_broadcast([P, P])).then_inc(s_w1, 16)

        block = ctx.enter_context(nc.Block())

        @block.sync
        def _(sp):
            xin = A["L0_attn_x"].rearrange("b (j p) d -> b p j d", p=P)
            sp.dma_start(U[:, 0:JT, :], A["L1_ffn_slot_embeds"].rearrange("(t u) s d -> (u s) t d", u=2)).then_inc(slots_ld, 16)
            for c in range(C):
                sp.dma_start(X[:, JT * c:JT * c + JT, :], xin[c]).then_inc(s_x, 16)
            sp.dma_start(gwraw[:], A["L0_ffn_gate_w"]).then_inc(s_small, 16)
            sp.dma_start(gb_row[:], A["L0_ffn_gate_b"].unsqueeze(0).to_broadcast([P, E])).then_inc(s_small, 16)
            for name, (at, k, ref) in COLS.items():
                if name == "onorm":
                    for h in range(H):
                        sp.dma_start(vrows[at:at + k, h * DK:(h + 1) * DK], A["L1_attn_onorm_w"]).then_inc(s_small, 16)
                    continue
                src = A[ref]
                if len(src.shape) == 2:
                    src = src.rearrange("a b -> (a b)")
                sp.dma_start(vrows[at:at + k, :], src.rearrange("(k d) -> k d", d=P)).then_inc(s_small, 16)
            moe_sp(M[0], 0)
            sp.dma_start(gate_w[:], A["L0_attn_gate_w"]).then_inc(s_w0, 16)
            sp.dma_start(state_w[:], A["L0_attn_state_w"]).then_inc(s_w0, 16)
            sp.dma_start(out_w[:], A["L0_attn_out_w"]).then_inc(s_w0, 16)
            sp.dma_start(outb_row[:], A["L0_attn_out_b"].unsqueeze(0).to_broadcast([P, P])).then_inc(s_w0, 16)
            sp.dma_start(stateb_row[:], A["L0_attn_state_b"].unsqueeze(0).to_broadcast([P, P])).then_inc(s_w0, 16)
            sp.dma_start(mlp_w1[:], A["L0_attn_mlp_w1"]).then_inc(s_w0, 16)
            sp.dma_start(mlp_w2[:], A["L0_attn_mlp_w2"].rearrange("(m h) d -> h m d", h=P)).then_inc(s_w0, 16)
            delta_sp()
            moe_sp(M[1], 1)
            nc.sync.wait_ge(M[1]["w_split"], 2 * E)
            soft_sp(F[0])
            nc.sync.wait_ge(F[0]["y_done"], E)
            soft_sp(F[1])
            oout = out.rearrange("b (j p) d -> b p j d", p=P)
            for c in range(C):
                sp.wait_ge(x_ready, STAGES * C - C + c + 1)
                sp.dma_start(oout[c], X[:, JT * c:JT * c + JT, :]).then_inc(s_out, 16)
            sp.wait_ge(s_out, 16 * C)

        @block.gpsimd
        def _(pool):
            nc.gpsimd.memset(ident[:], 0.0).then_inc(s_zero, 1)
            pool.wait_ge(s_zero, 1)
            nc.gpsimd.affine_select(out=ident[:], in_=ident[:], compare_op=ALU.not_equal, fill=1.0, base=0,
                                    pattern=[[-1, P]], channel_multiplier=1).then_inc(s_const, 1)
            nc.gpsimd.memset(nhalf[:], -0.5)
            nc.gpsimd.memset(tri[:], 1.0).then_inc(s_zero, 1)
            pool.wait_ge(s_zero, 2)
            nc.gpsimd.affine_select(out=tri[:], in_=tri[:], compare_op=ALU.is_gt, fill=0.0, base=0,
                                    pattern=[[1, E], [-1, E]], channel_multiplier=0).then_inc(s_const, 1)
            moe_pool(M[0], 0)
            ssm_pool()
            moe_pool(M[1], 1)
            delta_pool()

        @block.vector
        def _(dve):
            dve.wait_ge(b_turned, 1)
            dve.tensor_copy(vcols[:], bank[7][:, E:E + n_cols]).then_inc(b_copied, 1)
            dve.tensor_copy(gwh[:], bank[7][:, 0:E]).then_inc(b_copied, 1)
            dve.wait_ge(b_copied, 2)
            dve.tensor_tensor(gwl[:], bank[7][:, 0:E], gwh[:].bitcast(F32), ALU.subtract).then_inc(b_copied, 1)
            slots_dve()
            dve.wait_ge(s_const, 2)
            moe_dve(M[0], 0)
            ssm_dve()
            moe_dve(M[1], 1)
            soft_dve(F[0], 2 * C, False)
            delta_dve(3 * C)
            soft_dve(F[1], 4 * C, True)

        @block.scalar
        def _(act):
            slots_act()
            moe_act(M[0], 0)
            ssm_act()
            moe_act(M[1], 1)
            soft_act(F[0])
            delta_act()
            soft_act(F[1])

        @block.tensor
        def _(pe):
            pe.wait_ge(s_const, 1)
            pe.wait_ge(s_small, 16 * (1 + len(COLS) + H))
            pe.transpose(bank[7][:, E:E + n_cols], vrows[:], ident[0:n_cols, 0:n_cols])
            pe.transpose(bank[7][:, 0:E], gwraw[:], ident[0:E, 0:E]).then_inc(b_turned, 1)
            pe.wait_ge(b_copied, 3)
            slots_pe()
            moe_pe(M[0], 0)
            ssm_pe()
            moe_pe(M[1], 1)
            soft_pe(F[0])
            delta_pe()
            soft_pe(F[1])


def kernel(**inputs):
    import numpy as _np
    import concourse.bacc as _bacc
    from concourse import mybir as _mybir
    from concourse.bass_utils import run_bass_kernel_spmd as _run

    nc = _bacc.Bacc("TRN2", target_bir_lowering=False, num_devices=1)
    arrays, aps = {}, {}
    for name in inputs:
        a = _np.ascontiguousarray(inputs[name])
        arrays[f"in_{name}_dram"] = a
        aps[name] = nc.dram_tensor(f"in_{name}_dram", a.shape, _mybir.dt.from_np(a.dtype), kind="ExternalInput").ap()
    out = nc.dram_tensor("out_0_dram", (4, 512, 128), _mybir.dt.float32, kind="ExternalOutput").ap()
    program(nc, aps, out)
    r = _run(nc, [arrays], core_ids=[0])
    return r.results[0]["out_0_dram"]
```

```python
from contextlib import ExitStack

import concourse.bass as bass
from concourse import mybir

STAGES = 6
P = 128
T = 16
C = 4
JT = 4
CH = JT * P
E = 8
S_PER = 64
NB = C * S_PER
SCALE = float(P) ** 0.5
H = 8
DK = P // H
LAYERS = 2
FF = 352
FB = [(0, 128), (128, 128), (256, 96)]
HK = 4

F32 = mybir.dt.float32
F32R = mybir.dt.float32r
I32 = mybir.dt.int32
ALU = mybir.AluOpType
ACT = mybir.ActivationFunctionType
AX_X = mybir.AxisListType.X
RSQRT_MAGIC = float(0x5F3759DF)


def program(nc, A, out):
    with ExitStack() as ctx:
        def sb(name, shape, dt=F32):
            return ctx.enter_context(nc.sbuf_tensor(name, shape, dt))

        def sem(name):
            return ctx.enter_context(nc.semaphore(name))

        bank = [ctx.enter_context(nc.psum_tensor(f"bank{i}", [P, CH], F32)) for i in range(8)]
        ident = sb("ident", [P, P])
        X = sb("X", [P, T, P])
        XH = sb("XH", [P, T, P])
        stats = sb("stats", [P, T, 6])
        mv = sb("mv", [P, T, 2])
        rs = sb("rs", [P, 8, T])
        xTh = sb("xTh", [P, C, CH], F32R)
        xTl = sb("xTl", [P, C, CH], F32R)
        arena = sb("arena", [P, 40, CH])
        hh = sb("hh", [P, 2, HK, CH], F32R)
        hl = sb("hl", [P, 2, HK, CH], F32R)
        wraw = [sb(f"wraw{p}", [P, 2, CH]) for p in range(2)]
        wh = [sb(f"wh{p}", [P, 2, CH], F32R) for p in range(2)]
        wl = [sb(f"wl{p}", [P, 2, CH], F32R) for p in range(2)]

        U = sb("U", [P, T, P])

        COLS = {}
        n_cols = 0
        for name, ref, k in (
            ("n1w", "L0_attn_norm1_w", 1), ("n1b", "L0_attn_norm1_b", 1), ("gate_b", "L0_attn_gate_b", 2),
            ("state_b", "L0_attn_state_b", 1), ("n2w", "L0_attn_norm2_w", 1), ("n2b", "L0_attn_norm2_b", 1),
            ("mlp_b1", "L0_attn_mlp_b1", HK), ("mlp_b2", "L0_attn_mlp_b2", 1), ("gamma", "L1_ffn_norm_gamma", 1),
            ("slot_gamma", "L1_ffn_slot_norm_gamma", 1), ("r1w", "L1_attn_norm1_w", 2), ("r2w", "L1_attn_norm2_w", 2),
            ("b1_0", "L0_ffn_b1", E * HK), ("b2_0", "L0_ffn_b2", E), ("b1_1", "L1_ffn_b1", E * HK),
            ("b2_1", "L1_ffn_b2", E), ("onorm", None, 2),
        ):
            COLS[name] = (n_cols, k, ref)
            n_cols += k
        vrows = sb("vrows", [n_cols, P])
        vcols = sb("vcols", [P, n_cols])

        def col(name, k=0):
            at = COLS[name][0] + k
            return vcols[:, at:at + 1]

        def cols_of(name):
            at, k, _ = COLS[name]
            return vcols[:, at:at + k]

        gate_w = sb("gate_w", [P, 2 * P])
        state_w = sb("state_w", [P, P])
        out_w = sb("out_w", [P, P])
        outb_row = sb("outb_row", [P, P])
        stateb_row = sb("stateb_row", [P, P])
        mlp_w1 = sb("mlp_w1", [P, CH])
        mlp_w2 = sb("mlp_w2", [P, HK, P])
        sbar = sb("sbar", [P, 2])

        qkvb = sb("qkvb", [P, LAYERS, 3 * P + H])
        wo = sb("wo", [P, LAYERS, P])
        wg = sb("wg", [P, LAYERS, 2 * FF])
        wd = sb("wd", [P, LAYERS, 3, P])
        final_row = sb("final_row", [P, P])

        snT = sb("snT", [P, CH])
        slotsT = U[:].rearrange("p t d -> p (t d)").rearrange("p (e b s) -> p e b s", e=E, b=C)
        nmax = sb("nmax", [P, C, 8])
        sums = sb("sums", [P, C, 8])

        falling = sb("falling", [P, E])
        gwraw = sb("gwraw", [E, P])
        gw = sb("gw", [P, 2 * E], F32R)
        gb_row = sb("gb_row", [P, E])
        b1col = sb("b1col", [P, 2, HK])
        G = sb("G", [P, T, E])
        WE = sb("WE", [P, E, T])
        gsm = sb("gsm", [P, 4, T, E])

        ybank = (bank[5], bank[7])
        acc = arena[:, 0:4, :]
        hf = arena[:, 4:12, :]
        WT = arena[:, 12, 0:P]
        wb = [arena[:, a:a + C, :] for a in (16, 20)]
        wt_dram = [nc.dram_tensor(f"token_weights{k}", (E, T * P), F32, kind="Internal").ap() for k in range(2)]
        tmp = arena[:, 14:16, :]

        b1T, b2T = cols_of("b1_0"), cols_of("b2_0")

        s_x = [sem("s_x0"), sem("s_x1")]
        mv_ready = sem("mv_ready")
        rs_ready = sem("rs_ready")
        attn_w = sem("attn_w")
        W0_LOADS = 7
        s_const = sem("s_const")
        s_zero = sem("s_zero")
        s_small = sem("s_small")
        s_out = sem("s_out")
        x_ready = sem("x_ready")
        dve_chain = sem("dve_chain")
        pool_chain = sem("pool_chain")
        bias_step = sem("bias_step")

        chain_at = {"dve": 0, "pool": 0}

        def link(ins):
            chain_at["dve"] += 1
            ins.then_inc(dve_chain, 1)
            nc.vector.wait_ge(dve_chain, chain_at["dve"])

        def moe_sems(n):
            names = ("xh_ready xt_turned xt_hi xt_lo gates_done logits_ready exp_ready we_step w_split g1_done "
                     "hf_ready hh_ready hl_dve hl_pool wb0 wb1 g2_done y_ready acc_done "
                     "w_hi acc_turned wload0 wload1 b1_ready").split()
            return {k: sem(f"{k}_{n}") for k in names}

        M = [moe_sems("moe0"), moe_sems("moe1")]
        B = {k: sem(k + "_ssm") for k in (
            "xh_ready xt_turned xt_ready z_done z_step bc_done bc_copied g_done silu_ready "
            "xg_ready ub_done scan_ready u_b_ready ssm_done x1_ready xh2_ready x2_turned x2_ready g1_done hf_ready y_done "
            "y_copied yt_done xu_ready mlp_w x2_split mlp_hi mlp_lo").split()}


        def dve_rsqrt(y, v, t):
            link(nc.vector.tensor_scalar(t.bitcast(I32), v.bitcast(I32), 1, None, ALU.logical_shift_right))
            link(nc.vector.tensor_scalar(y.bitcast(I32), t.bitcast(I32), -1.0, RSQRT_MAGIC, ALU.mult, ALU.add))
            for _ in range(3):
                link(nc.vector.scalar_tensor_tensor(out=t, in0=y, scalar=-0.5, in1=y, op0=ALU.mult, op1=ALU.mult))
                link(nc.vector.tensor_tensor(t, t, v, ALU.mult))
                link(nc.vector.scalar_tensor_tensor(out=y, in0=t, scalar=1.5, in1=y, op0=ALU.add, op1=ALU.mult))

        LN_MOE0, LN_SSM, LN_MLP, LN_MOE1, LN_SOFT0, LN_DELTA, LN_SOFT1 = range(7)

        def tiles(c):
            return slice(JT * c, JT * c + JT)

        def plink(ins):
            chain_at["pool"] += 1
            ins.then_inc(pool_chain, 1)
            nc.gpsimd.wait_ge(pool_chain, chain_at["pool"])

        def norm_aggr(c):
            for t in range(JT * c, JT * c + JT):
                last = nc.vector.bn_aggr(mv[:, t, :], stats[:, t, :])
            last.then_inc(mv_ready, 1)

        def norm_stats(src, c):
            for t in range(JT * c, JT * c + JT):
                last = nc.vector.bn_stats(stats[:, t, :], src[:, t, :])
            link(last)
            norm_aggr(c)

        def norm_factors(ln, c):
            nc.gpsimd.wait_ge(mv_ready, C * ln + c + 1)
            var = mv[:, tiles(c), 1]
            r0, r1 = rs[:, 0, tiles(c)], rs[:, 1, tiles(c)]
            half = nhalf[:, 0:JT]
            plink(nc.gpsimd.tensor_scalar(r1, var, 1e-5, None, ALU.add))
            last = nc.gpsimd.tensor_tensor(r0, r1, half, ALU.pow)
            if ln == LN_SSM or ln in (LN_SOFT0, LN_SOFT1):
                plink(last)
                plink(nc.gpsimd.tensor_tensor(r1, r0, r0, ALU.mult))
                plink(nc.gpsimd.tensor_tensor(r1, r1, var, ALU.mult))
            if ln == LN_SSM:
                plink(nc.gpsimd.tensor_scalar(r1, r1, 1e-5, None, ALU.add))
                last = nc.gpsimd.tensor_tensor(r1, r1, half, ALU.pow)
            if ln in (LN_SOFT0, LN_SOFT1):
                plink(nc.gpsimd.tensor_scalar(r1, r1, float(P), 1e-30, ALU.mult, ALU.max))
                plink(nc.gpsimd.tensor_tensor(r1, r1, half, ALU.pow))
                plink(nc.gpsimd.tensor_scalar(r1, r1, 1e12, SCALE, ALU.min, ALU.mult))
                last = nc.gpsimd.tensor_tensor(r0, r0, r1, ALU.mult)
            last.then_inc(rs_ready, 1)

        def norm_rows(ln, c):
            src, dst, done = {
                LN_MOE0: (X, XH, M[0]["xh_ready"]), LN_SSM: (X, U, dve_chain), LN_MLP: (U, XH, B["xh2_ready"]),
                LN_MOE1: (X, XH, M[1]["xh_ready"]), LN_SOFT0: (X, XH, F[0]["xh_ready"]),
                LN_DELTA: (X, U, D5["u_ready"]), LN_SOFT1: (X, XH, F[1]["xh_ready"])}[ln]
            nc.vector.wait_ge(rs_ready, C * ln + c + 1)
            for t in range(JT * c, JT * c + JT):
                last = nc.vector.tensor_scalar(dst[:, t, :], src[:, t, :], mv[:, t, 0:1], rs[:, 0, t:t + 1],
                                               ALU.subtract, ALU.mult)
                if ln != LN_SSM:
                    last.then_inc(done, 1)
            if ln == LN_SSM:
                link(last)
                for t in range(JT * c, JT * c + JT):
                    nc.vector.tensor_scalar(XH[:, t, :], U[:, t, :], rs[:, 1, t:t + 1], None,
                                            ALU.mult).then_inc(B["xh_ready"], 1)

        def x_done(c, n, ln):
            nc.vector.wait_ge(x_ready, n)
            norm_stats(X, c)
            if c >= 1:
                norm_rows(ln, c - 1)

        def row(k):
            return rs[:, k, :]

        def moe_dve(S, k):
            nc.vector.sem_inc(S["hh_ready"], 5)
            nc.vector.sem_inc(S["hl_dve"], 4)
            nc.vector.sem_inc(S["y_ready"], 2)

            def first_weights():
                nc.vector.tensor_copy(b1col[:, 0, :], b1T[:, 0:HK]).then_inc(S["b1_ready"], 1)
                nc.vector.wait_ge(S["wload0"], 32)
                for which in range(2):
                    nc.vector.tensor_copy(wh[0][:, which, :], wraw[0][:, which, :]).then_inc(S["w_hi"], 1)

            def low_part(c):
                nc.vector.wait_ge(S["xt_hi"], c + 1)
                nc.vector.tensor_tensor(xTl[:, c, :], bank[c][:], xTh[:, c, :].bitcast(F32),
                                        ALU.subtract).then_inc(S["xt_lo"], 1)

            for c in range(C):
                low_part(c)
                if k and c == 0:
                    norm_rows(LN_MOE1, C - 1)
            if k:
                first_weights()
            if k == 0:
                biases_dve()
                first_weights()
                slots_dve()
            nc.vector.wait_ge(S["gates_done"], 1)
            glog = bank[4][:, 0:T * 2 * E].rearrange("p (t z e) -> p t z e", z=2, e=E)
            link(nc.vector.tensor_tensor(G[:], glog[:, :, 0], gb_row[:].unsqueeze(1).to_broadcast([P, T, E]), ALU.add))
            link(nc.vector.tensor_tensor(G[:], G[:], glog[:, :, 1], ALU.add))
            link(nc.vector.tensor_reduce(row(3), G[:], AX_X, ALU.max))
            nc.vector.tensor_tensor(gsm[:, 0], G[:], row(3).unsqueeze(2).to_broadcast([P, T, E]),
                                    ALU.subtract).then_inc(S["logits_ready"], 1)
            g, one, pick = G[:], gsm[:, 1], gsm[:, 3]
            for n in range(2):
                if n:
                    link(nc.vector.tensor_reduce(row(3), g, AX_X, ALU.max))
                link(nc.vector.tensor_tensor(pick, g, row(3).unsqueeze(2).to_broadcast([P, T, E]), ALU.is_equal))
                link(nc.vector.tensor_tensor(pick, pick, falling[:].unsqueeze(1).to_broadcast([P, T, E]), ALU.mult))
                link(nc.vector.tensor_reduce(row(4), pick, AX_X, ALU.max))
                link(nc.vector.tensor_tensor(pick, pick, row(4).unsqueeze(2).to_broadcast([P, T, E]), ALU.is_equal))
                if n == 0:
                    nc.vector.tensor_copy(one, pick)
                    link(nc.vector.scalar_tensor_tensor(out=g, in0=pick, scalar=-3e38, in1=g, op0=ALU.mult,
                                                        op1=ALU.add))
                else:
                    link(nc.vector.tensor_tensor(one, one, pick, ALU.add))
            nc.vector.wait_ge(S["exp_ready"], 1)
            link(nc.vector.tensor_tensor(gsm[:, 1], gsm[:, 1], gsm[:, 2], ALU.mult))
            link(nc.vector.tensor_reduce(row(4), gsm[:, 1], AX_X, ALU.add))
            link(nc.vector.reciprocal(row(5), row(4)))
            nc.vector.tensor_tensor(WE[:].rearrange("p e t -> p t e"), gsm[:, 1],
                                    row(5).unsqueeze(2).to_broadcast([P, T, E]), ALU.mult).then_inc(S["we_step"], 1)

            def add_moe(c):
                nc.vector.wait_ge(S["acc_turned"], c + 1)
                nc.vector.scalar_tensor_tensor(
                    out=X[:, tiles(c), :], in0=bank[6][:].rearrange("p (t d) -> p t d", d=P),
                    scalar=0.5, in1=X[:, tiles(c), :], op0=ALU.mult, op1=ALU.add).then_inc(x_ready, 1)
                x_done(c, (2 * C if k else 0) + c + 1, LN_SOFT0 if k else LN_SSM)

            def split_hidden(s, q):
                nc.vector.wait_ge(S["g2_done"], s + 1)
                for m in range(HK):
                    nc.vector.wait_ge(S["hf_ready"], s * 4 + (m + 1))
                    nc.vector.tensor_copy(hh[:, q, m, :], hf[:, q * 4 + m, :]).then_inc(S["hh_ready"], 1)
                    if m < 3:
                        nc.vector.wait_ge(S["hh_ready"], s * 4 + (m + 6))
                        nc.vector.tensor_tensor(hl[:, q, m, :], hf[:, q * 4 + m, :], hh[:, q, m, :].bitcast(F32),
                                                ALU.subtract).then_inc(S["hl_dve"], 1)

            def body(i, last):
                for p in range(2):
                    for c in range(C):
                        q = c % 2
                        s = i * 8 + (4 * p + c)
                        more = not (last and p == 1)
                        if more or c < C - 1:
                            split_hidden(s + 1, 1 - q)
                        if c == 0 and more:
                            nc.vector.wait_ge(S["wload0"] if p else S["wload1"], i * 32 + (64 if p else 32))
                            nc.vector.wait_ge(S["g2_done"], i * 8 + (4 * p + 2))
                            for which in range(2):
                                nc.vector.tensor_copy(wh[1 - p][:, which, :], wraw[1 - p][:, which, :]
                                                      ).then_inc(S["w_hi"], 1)
                        if c == 2 and more:
                            n = i * 2 + (p + 1)
                            nc.vector.wait_ge(S["hf_ready"], i * 32 + (16 * p + 1))
                            nc.vector.tensor_scalar(b1col[:, 1 - p, :], b1T[:, bass.ds(n * HK, HK)], 1.0, None,
                                                    ALU.mult).then_inc(S["b1_ready"], 1)
                        nc.vector.wait_ge(S["g2_done"], s + 3)
                        if c == 0:
                            nc.vector.wait_ge(S["wb1"] if p else S["wb0"], i * 16 + (16 if p else 32))
                        nc.vector.wait_ge(S["acc_done"], s + 1)
                        nc.vector.scalar_tensor_tensor(
                            out=tmp[:, q, :], in0=ybank[q][:], scalar=b2T[:, bass.ds(i * 2 + p, 1)],
                            in1=wb[p][:, c, :], op0=ALU.add, op1=ALU.mult).then_inc(S["y_ready"], 1)
                        if not more and c >= 1:
                            add_moe(c - 1)

            split_hidden(0, 0)
            nc.vector.wait_ge(S["we_step"], 2)
            nc.vector.tensor_copy(WT, bank[6][:, 0:P]).then_inc(S["we_step"], 1)
            with nc.vector.Fori(0, E // 2 - 1) as i:
                body(i, False)
            body(E // 2 - 1, True)
            add_moe(C - 1)

        def moe_act(S, k):
            for c in range(C):
                nc.scalar.wait_ge(S["xt_turned"], c + 1)
                nc.scalar.activation(xTh[:, c, :], bank[c][:], ACT.Copy).then_inc(S["xt_hi"], 1)
            if k == 0:
                slots_act()
            nc.scalar.wait_ge(S["logits_ready"], 1)
            nc.scalar.activation(gsm[:, 2], gsm[:, 0], ACT.Exp).then_inc(S["exp_ready"], 1)
            with nc.scalar.Fori(0, E // 2) as i:
                for p in range(2):
                    nc.scalar.wait_ge(S["b1_ready"], i * 2 + (p + 1))
                    for c in range(C):
                        q = c % 2
                        s = i * 8 + (4 * p + c)
                        nc.scalar.wait_ge(S["hh_ready"], s * 4 + 1)
                        nc.scalar.wait_ge(S["hl_dve"], s * 3 + 1)
                        nc.scalar.wait_ge(S["hl_pool"], s + 1)
                        for m in range(HK):
                            nc.scalar.wait_ge(S["g1_done"], s * 4 + (m + 1))
                            nc.scalar.activation(hf[:, q * 4 + m, :], bank[m][:], ACT.Gelu,
                                                 bias=b1col[:, p, m:m + 1]).then_inc(S["hf_ready"], 1)

        def moe_pool(S, k):
            if k == 0:
                for c in range(C):
                    norm_factors(LN_MOE0, c)
            else:
                nc.gpsimd.wait_ge(x_ready, 2 * C)
            nc.gpsimd.memset(acc, 0.0).then_inc(S["acc_done"], 2)
            nc.gpsimd.sem_inc(S["hl_pool"], 2)

            def split(p, which, e):
                src = wraw[p][:, which, :]
                nc.gpsimd.wait_ge(S["w_hi"], e * 2 + (which + 1))
                nc.gpsimd.tensor_tensor(wl[p][:, which, :], src, wh[p][:, which, :].bitcast(F32),
                                        ALU.subtract).then_inc(S["w_split"], 1)

            split(0, 0, 0)
            split(0, 1, 0)

            def low_hidden(s, q):
                for m in (3,):
                    if m == 3:
                        nc.gpsimd.wait_ge(S["g2_done"], s + 1)
                    nc.gpsimd.wait_ge(S["hh_ready"], s * 4 + (m + 6))
                    nc.gpsimd.tensor_tensor(hl[:, q, m, :], hf[:, q * 4 + m, :], hh[:, q, m, :].bitcast(F32),
                                            ALU.subtract).then_inc(S["hl_pool"], 1)

            def body(i, last):
                for p in range(2):
                    for c in range(C):
                        q = c % 2
                        s = i * 8 + (4 * p + c)
                        more = not (last and p == 1)
                        if more or c < C - 1:
                            low_hidden(s + 1, 1 - q)
                        if more and c < 2:
                            split(1 - p, c, i * 2 + (p + 1))
                        nc.gpsimd.wait_ge(S["y_ready"], s + 3)
                        nc.gpsimd.wait_ge(S["acc_done"], s + 2)
                        nc.gpsimd.tensor_tensor(acc[:, c, :], acc[:, c, :], tmp[:, q, :], ALU.add
                                                ).then_inc(S["acc_done"], 1)
                        if not more and c >= 1:
                            norm_factors(LN_SOFT0 if k else LN_SSM, c - 1)

            low_hidden(0, 0)
            with nc.gpsimd.Fori(0, E // 2 - 1) as i:
                body(i, False)
            body(E // 2 - 1, True)
            norm_factors(LN_SOFT0 if k else LN_SSM, C - 1)

        def mm3(o, ah, al, bh, bl, start, stop):
            nc.tensor.matmul(o, ah, bh, start=start, stop=False)
            nc.tensor.matmul(o, ah, bl, start=False, stop=False)
            return nc.tensor.matmul(o, al, bh, start=False, stop=stop)

        def moe_pe(S, k):
            nc.tensor.sem_inc(S["g2_done"], 2)

            def turn(c):
                for j in range(JT):
                    t = JT * c + j
                    nc.tensor.wait_ge(S["xh_ready"], t + 1)
                    ins = nc.tensor.transpose(bank[c][:, j * P:(j + 1) * P], XH[:, t, :], ident[:])
                ins.then_inc(S["xt_turned"], 1)

            def gates(c):
                nc.tensor.wait_ge(S["xt_lo"], c + 1)
                for j in range(JT):
                    t = JT * c + j
                    at_, cols = t * 2 * E, slice(j * P, (j + 1) * P)
                    nc.tensor.matmul(bank[4][:, at_:at_ + 2 * E], xTh[:, c, cols], gw[:], start=True, stop=False)
                    ins = nc.tensor.matmul(bank[4][:, at_:at_ + E], xTl[:, c, cols], gw[:, 0:E], start=False, stop=True)
                return ins

            for c in range(C - 1):
                turn(c)
            if k == 0:
                turn(C - 1)
                biases_pe()
                nc.tensor.wait_ge(bias_step, 4)
            else:
                gates(0)
                turn(C - 1)
            for c in range(1 if k else 0, C):
                ins = gates(c)
            ins.then_inc(S["gates_done"], 1)
            if k == 0:
                slots_pe()

            def g1(p, c, s, at_s):
                nc.tensor.wait_ge(S["w_split"], at_s)
                for m in range(HK):
                    nc.tensor.wait_ge(S["hf_ready"], s * 4 + (m - 3))
                    cols = slice(m * P, (m + 1) * P)
                    mm3(bank[m][:], wh[p][:, 0, cols], wl[p][:, 0, cols], xTh[:, c, :], xTl[:, c, :],
                        True, True).then_inc(S["g1_done"], 1)

            def step(i, p, c, more):
                q = c % 2
                s = i * 8 + (4 * p + c)
                if more:
                    p2, c2 = (p, c + 1) if c < C - 1 else (1 - p, 0)
                    e2 = i * 2 + (p + (1 if c == C - 1 else 0))
                    g1(p2, c2, s + 1, e2 * 2 + 1)
                nc.tensor.wait_ge(S["y_ready"], s + 1)
                if c == 0:
                    nc.tensor.wait_ge(S["w_split"], i * 4 + (2 * p + 2))
                for m in range(HK):
                    nc.tensor.wait_ge(S["hh_ready"], s * 4 + (m + 6))
                    if m < 3:
                        nc.tensor.wait_ge(S["hl_dve"], s * 3 + (m + 5))
                    else:
                        nc.tensor.wait_ge(S["hl_pool"], s + 3)
                    cols = slice(m * P, (m + 1) * P)
                    ins = mm3(ybank[q][:], wh[p][:, 1, cols], wl[p][:, 1, cols], hh[:, q, m, :], hl[:, q, m, :],
                              m == 0, m == HK - 1)
                ins.then_inc(S["g2_done"], 1)

            def turn_sum(c):
                nc.tensor.wait_ge(S["acc_done"], 2 + 4 * (E - 1) + c + 1)
                if c >= 1:
                    nc.tensor.wait_ge(x_ready, (2 * C if k else 0) + c)
                for j in range(JT):
                    ins = nc.tensor.transpose(bank[6][:, j * P:(j + 1) * P], acc[:, c, j * P:(j + 1) * P], ident[:])
                ins.then_inc(S["acc_turned"], 1)

            nc.tensor.wait_ge(S["w_split"], 2)
            for m in range(HK):
                cols = slice(m * P, (m + 1) * P)
                mm3(bank[m][:], wh[0][:, 0, cols], wl[0][:, 0, cols], xTh[:, 0, :], xTl[:, 0, :],
                    True, True).then_inc(S["g1_done"], 1)
            nc.tensor.wait_ge(S["we_step"], 1)
            nc.tensor.transpose(bank[6][:, 0:P], WE[:].rearrange("p e t -> p (e t)"), ident[:]).then_inc(S["we_step"], 1)
            with nc.tensor.Fori(0, E // 2 - 1) as i:
                for p in range(2):
                    for c in range(C):
                        step(i, p, c, True)
            for p in range(2):
                for c in range(C):
                    step(E // 2 - 1, p, c, not (p == 1 and c == C - 1))
                    if p == 1 and c >= 1:
                        turn_sum(c - 1)
            turn_sum(C - 1)

        def moe_sp(S, k):
            w1, w2 = A["L0_ffn_w1"], A["L0_ffn_w2"].rearrange("e (m h) d -> e h m d", h=P)

            def load(e, p, wl_sem):
                nc.sync.dma_start(wraw[p][:, 0, :], w1[e, :, :] if isinstance(e, int) else
                                  w1[bass.ds(e, 1), :, :].squeeze(0)).then_inc(wl_sem, 16)
                dst = wraw[p][:, 1, :].rearrange("p (m d) -> p m d", d=P)
                nc.sync.dma_start(dst, w2[e, :, :, :] if isinstance(e, int) else
                                  w2[bass.ds(e, 1), :, :, :].squeeze(0)).then_inc(wl_sem, 16)

            if k:
                nc.sync.wait_ge(M[0]["w_split"], 2 * E)
            def spread(e, p):
                row_ = wt_dram[k][e:e + 1, :] if isinstance(e, int) else wt_dram[k][bass.ds(e, 1), :]
                nc.sync.dma_start(wb[p].rearrange("p c n -> p (c n)"), row_.to_broadcast([P, T * P])
                                  ).then_inc(S["wb1"] if p else S["wb0"], 16)

            load(0, 0, S["wload0"])
            load(1, 1, S["wload1"])
            nc.sync.wait_ge(S["we_step"], 3)
            nc.sync.dma_start(wt_dram[k].rearrange("e (t p) -> (e t) p", p=P), WT).then_inc(S["wb0"], 16)
            nc.sync.wait_ge(S["wb0"], 16)
            spread(0, 0)
            spread(1, 1)
            with nc.sync.Fori(0, E // 2 - 1) as i:
                nc.sync.wait_ge(S["w_split"], i * 4 + 2)
                load(i * 2 + 2, 0, S["wload0"])
                nc.sync.wait_ge(S["w_split"], i * 4 + 4)
                load(i * 2 + 3, 1, S["wload1"])
                nc.sync.wait_ge(S["y_ready"], i * 8 + (C + 2))
                spread(i * 2 + 2, 0)
                nc.sync.wait_ge(S["y_ready"], i * 8 + (2 * C + 2))
                spread(i * 2 + 3, 1)

        xT = arena[:, 0:4, :]
        gate = arena[:, 4:8, :]
        gate2 = arena[:, 8:12, :]
        delta_b = arena[:, 12:16, :]
        decay_b = arena[:, 16:20, :]
        states = arena[:, 20:24, :]
        hid = arena[:, 24:32, :]
        yfm = arena[:, 32:34, :]
        dBu = arena[:, 34:36, :]
        zs = rs[:, 3:8, :]

        w1h, w2h = wh[1][:, 0, :], wh[1][:, 1, :]
        w1l, w2l = wl[1][:, 0, :], wl[1][:, 1, :]
        UB = [(7, 3), (6, 0)]

        def ssm_dve():
            norm_rows(LN_SSM, C - 1)
            nc.vector.wait_ge(attn_w, 16 * W0_LOADS)
            nc.vector.reduce_sum(sbar[:, 0:1], state_w[:], AX_X)
            link(nc.vector.reduce_sum(sbar[:, 1:2], stateb_row[:], AX_X))
            nc.vector.tensor_scalar(sbar[:, 1:2], sbar[:, 1:2], 1.0 / P, None, ALU.mult).then_inc(B["z_done"], 1)
            nc.vector.tensor_copy(w1h, mlp_w1[:]).then_inc(B["mlp_w"], 1)
            nc.vector.tensor_copy(w2h, mlp_w2[:].rearrange("p m d -> p (m d)")).then_inc(B["mlp_w"], 1)
            nc.vector.wait_ge(B["z_done"], 2)
            link(nc.vector.tensor_scalar(zs[:, 0], bank[7][:, 0:T], 1.0 / P, sbar[:, 1:2], ALU.mult, ALU.add))
            link(nc.vector.tensor_scalar(zs[:, 1], zs[:, 0], -1.0, None, ALU.mult))
            nc.vector.tensor_tensor(zs[:, 1], zs[:, 1], zs[:, 0], ALU.max).then_inc(B["z_step"], 1)
            nc.vector.wait_ge(B["z_step"], 2)
            w_, one = row(0), row(1)
            link(nc.vector.tensor_scalar(w_, zs[:, 2], 1.0, None, ALU.add))
            link(nc.vector.tensor_scalar(one, w_, 1.0, None, ALU.is_equal))
            link(nc.vector.scalar_tensor_tensor(out=w_, in0=w_, scalar=-1.0, in1=one, op0=ALU.add, op1=ALU.add))
            link(nc.vector.reciprocal(w_, w_))
            link(nc.vector.tensor_tensor(w_, w_, zs[:, 2], ALU.mult))
            nc.vector.wait_ge(B["z_step"], 3)
            link(nc.vector.tensor_tensor(one, one, zs[:, 3], ALU.add))
            link(nc.vector.tensor_tensor(one, one, w_, ALU.mult))
            nc.vector.scalar_tensor_tensor(out=zs[:, 3], in0=zs[:, 0], scalar=0.0, in1=one, op0=ALU.max,
                                           op1=ALU.add).then_inc(B["z_step"], 1)
            for c in range(C):
                nc.vector.wait_ge(B["silu_ready"], 2 * c + 2)
                nc.vector.tensor_tensor(gate[:, c, :], gate[:, c, :], xT[:, c, :], ALU.mult).then_inc(B["xg_ready"], 1)
            for c in range(C):
                nc.vector.wait_ge(B["ub_done"], c + 1)
                nc.vector.wait_ge(B["bc_copied"], 2 * c + 2)
                b_x, b_g = UB[c % 2]
                link(nc.vector.scalar_tensor_tensor(out=dBu[:, 0, :], in0=bank[b_x][:], scalar=col("state_b"),
                                                    in1=delta_b[:, c, :], op0=ALU.add, op1=ALU.mult))
                link(nc.vector.scalar_tensor_tensor(out=dBu[:, 1, :], in0=bank[b_g][:], scalar=col("state_b"),
                                                    in1=dBu[:, 0, :], op0=ALU.add, op1=ALU.mult))
                nc.vector.tensor_tensor_scan(states[:, c, :], decay_b[:, c, :], dBu[:, 1, :], 0.0, ALU.mult,
                                             ALU.add).then_inc(B["scan_ready"], 1)
            for c in range(C):
                nc.vector.wait_ge(B["ssm_done"], c + 1)
                nc.vector.wait_ge(B["u_b_ready"], c + 1)
                sl = slice(JT * c, JT * c + JT)
                nc.vector.tensor_tensor(U[:, sl, :], U[:, sl, :], bank[4 + c % 2][:].rearrange("p (t d) -> p t d", d=P),
                                        ALU.add).then_inc(B["x1_ready"], 1)
                nc.vector.wait_ge(B["x1_ready"], c + 1)
                norm_stats(U, c)
                if c >= 1:
                    norm_rows(LN_MLP, c - 1)
            norm_rows(LN_MLP, C - 1)
            for c in range(C):
                nc.vector.wait_ge(B["x2_ready"], c + 1)
                nc.vector.tensor_copy(xTh[:, c, :], xT[:, c, :]).then_inc(B["x2_split"], 1)
                nc.vector.wait_ge(B["x2_split"], 2 * c + 1)
                nc.vector.tensor_tensor(xTl[:, c, :], xT[:, c, :], xTh[:, c, :].bitcast(F32),
                                        ALU.subtract).then_inc(B["x2_split"], 1)

            def split_mlp(c):
                q = c % 2
                for m in range(HK):
                    nc.vector.wait_ge(B["hf_ready"], HK * c + m + 1)
                    nc.vector.tensor_copy(hh[:, q, m, :], hid[:, q * HK + m, :]).then_inc(B["mlp_hi"], 1)
                    if m == 0:
                        nc.vector.wait_ge(B["mlp_hi"], (HK + 1) * c + 1)
                        nc.vector.tensor_tensor(hl[:, q, 0, :], hid[:, q * HK, :], hh[:, q, 0, :].bitcast(F32),
                                                ALU.subtract).then_inc(B["mlp_hi"], 1)

            for n in range(C + 2):
                if n < C:
                    split_mlp(n)
                if n >= 2:
                    c = n - 2
                    sl = tiles(c)
                    nc.vector.wait_ge(B["yt_done"], c + 1)
                    nc.vector.wait_ge(B["xu_ready"], c + 1)
                    nc.vector.tensor_tensor(X[:, sl, :], X[:, sl, :], bank[7][:].rearrange("p (t d) -> p t d", d=P),
                                            ALU.add).then_inc(x_ready, 1)
                    x_done(c, C + c + 1, LN_MOE1)

        def ssm_act():
            for c in range(C):
                nc.scalar.wait_ge(B["xt_turned"], c + 1)
                nc.scalar.activation(xT[:, c, :], bank[c][:], ACT.Identity, bias=col("n1b"),
                                     scale=col("n1w")).then_inc(B["xt_ready"], 1)
            nc.scalar.wait_ge(B["z_step"], 1)
            nc.scalar.activation(zs[:, 2], zs[:, 1], ACT.Exp, scale=-1.0).then_inc(B["z_step"], 1)
            nc.scalar.wait_ge(B["z_step"], 2)
            nc.scalar.activation(zs[:, 3], zs[:, 2], ACT.Ln, bias=1.0).then_inc(B["z_step"], 1)
            nc.scalar.wait_ge(B["z_step"], 4)
            nc.scalar.activation(zs[:, 4], zs[:, 3], ACT.Exp, scale=-1.0).then_inc(B["z_step"], 1)
            for c in range(C):
                pair = (4, 5) if c % 2 == 0 else (6, 0)
                for g, dst in ((0, gate), (1, gate2)):
                    nc.scalar.wait_ge(B["g_done"], 2 * c + g + 1)
                    nc.scalar.activation(dst[:, c, :], bank[pair[g]][:], ACT.Silu,
                                         bias=col("gate_b", g)).then_inc(B["silu_ready"], 1)
            for c in range(C):
                for g, dst in ((0, delta_b), (1, decay_b)):
                    nc.scalar.wait_ge(B["bc_done"], 2 * c + g + 1)
                    nc.scalar.activation(dst[:, c, :], bank[1 + g][:], ACT.Copy).then_inc(B["bc_copied"], 1)
            for c in range(C):
                nc.scalar.wait_ge(B["x2_turned"], c + 1)
                nc.scalar.activation(xT[:, c, :], bank[6][:] if c % 2 == 0 else bank[0][:], ACT.Identity,
                                     bias=col("n2b"), scale=col("n2w")).then_inc(B["x2_ready"], 1)
            for c in range(C + 1):
                if c < C:
                    if c >= 2:
                        nc.scalar.wait_ge(B["y_done"], c - 1)
                    for m in range(HK):
                        nc.scalar.wait_ge(B["g1_done"], HK * c + m + 1)
                        nc.scalar.activation(hid[:, (c % 2) * HK + m, :], bank[1 + m][:], ACT.Gelu,
                                             bias=col("mlp_b1", m)).then_inc(B["hf_ready"], 1)
                if c >= 1:
                    nc.scalar.wait_ge(B["y_done"], c)
                    if c >= 3:
                        nc.scalar.wait_ge(B["yt_done"], c - 2)
                    nc.scalar.activation(yfm[:, (c - 1) % 2, :], bank[5 + (c - 1) % 2][:], ACT.Identity,
                                         bias=col("mlp_b2")).then_inc(B["y_copied"], 1)

        def ssm_pool():
            nc.gpsimd.wait_ge(attn_w, 16 * W0_LOADS)
            for c in range(C):
                sl = slice(JT * c, JT * c + JT)
                nc.gpsimd.wait_ge(B["xh_ready"], JT * c + JT)
                nc.gpsimd.tensor_tensor(U[:, sl, :], U[:, sl, :], outb_row[:].unsqueeze(1).to_broadcast([P, JT, P]),
                                        ALU.add).then_inc(B["u_b_ready"], 1)
            for which, (hi, lo, w) in enumerate(((w1h, w1l, mlp_w1[:]), (w2h, w2l, mlp_w2[:].rearrange("p m d -> p (m d)")))):
                nc.gpsimd.wait_ge(B["mlp_w"], 2)
                nc.gpsimd.tensor_tensor(lo, w, hi.bitcast(F32), ALU.subtract).then_inc(B["mlp_w"], 1)
            for c in range(C):
                sl = slice(JT * c, JT * c + JT)
                norm_factors(LN_MLP, c)
                nc.gpsimd.wait_ge(B["x1_ready"], c + 1)
                nc.gpsimd.tensor_tensor(X[:, sl, :], X[:, sl, :], U[:, sl, :], ALU.add).then_inc(B["xu_ready"], 1)

            for n in range(C + 2):
                if n < C:
                    q = n % 2
                    for m in range(1, HK):
                        nc.gpsimd.wait_ge(B["mlp_hi"], (HK + 1) * n + m + 2)
                        nc.gpsimd.tensor_tensor(hl[:, q, m, :], hid[:, q * HK + m, :], hh[:, q, m, :].bitcast(F32),
                                                ALU.subtract).then_inc(B["mlp_lo"], 1)
                if n >= 2:
                    norm_factors(LN_MOE1, n - 2)

        def ssm_pe():
            for c in range(C):
                for j in range(JT):
                    nc.tensor.wait_ge(B["xh_ready"], JT * c + j + 1)
                    ins = nc.tensor.transpose(bank[c][:, j * P:(j + 1) * P], XH[:, JT * c + j, :], ident[:])
                ins.then_inc(B["xt_turned"], 1)
            nc.tensor.wait_ge(B["z_done"], 1)
            for t in range(T):
                c, j = divmod(t, JT)
                nc.tensor.wait_ge(B["xt_ready"], c + 1)
                ins = nc.tensor.matmul(bank[7][:, t:t + 1], xT[:, c, j * P:(j + 1) * P], sbar[:, 0:1],
                                       start=True, stop=True)
            ins.then_inc(B["z_done"], 1)
            for c in range(C):
                pair = (4, 5) if c % 2 == 0 else (6, 0)
                if c >= 2:
                    nc.tensor.wait_ge(B["silu_ready"], 2 * (c - 1))
                for g in range(2):
                    nc.tensor.matmul(bank[pair[g]][:], gate_w[:, g * P:(g + 1) * P], xT[:, c, :], start=True,
                                     stop=True).then_inc(B["g_done"], 1)
            nc.tensor.wait_ge(B["z_step"], 5)
            for c in range(C):
                for g, k in ((0, 3), (1, 4)):
                    if c >= 1:
                        nc.tensor.wait_ge(B["bc_copied"], 2 * c - 1 + g)
                    for j in range(JT):
                        t = JT * c + j
                        ins = nc.tensor.transpose(bank[1 + g][:, j * P:(j + 1) * P],
                                                  zs[:, k, t:t + 1].to_broadcast([P, P]), ident[:])
                    ins.then_inc(B["bc_done"], 1)
                nc.tensor.wait_ge(B["xg_ready"], c + 1)
                if c >= 2:
                    nc.tensor.wait_ge(B["scan_ready"], c - 1)
                elif c == 1:
                    nc.tensor.wait_ge(B["silu_ready"], 2 * C)
                b_x, b_g = UB[c % 2]
                nc.tensor.matmul(bank[b_x][:], state_w[:], gate2[:, c, :], start=True, stop=True)
                nc.tensor.matmul(bank[b_g][:], state_w[:], gate[:, c, :], start=True, stop=True).then_inc(B["ub_done"], 1)
            for c in range(C):
                nc.tensor.wait_ge(B["scan_ready"], c + 1)
                if c >= 2:
                    nc.tensor.wait_ge(B["x1_ready"], c - 1)
                for j in range(JT):
                    ins = nc.tensor.matmul(bank[4 + c % 2][:, j * P:(j + 1) * P], states[:, c, j * P:(j + 1) * P],
                                           out_w[:], start=True, stop=True)
                ins.then_inc(B["ssm_done"], 1)
            for c in range(C):
                if c >= 2:
                    nc.tensor.wait_ge(B["x2_ready"], c - 1)
                for j in range(JT):
                    nc.tensor.wait_ge(B["xh2_ready"], JT * c + j + 1)
                    ins = nc.tensor.transpose((bank[6] if c % 2 == 0 else bank[0])[:, j * P:(j + 1) * P],
                                              XH[:, JT * c + j, :], ident[:])
                ins.then_inc(B["x2_turned"], 1)
            for c in range(C + 2):
                if c < C:
                    if c == 0:
                        nc.tensor.wait_ge(B["mlp_w"], 4)
                    nc.tensor.wait_ge(B["x2_split"], 2 * (c + 1))
                    for m in range(HK):
                        if c >= 1:
                            nc.tensor.wait_ge(B["hf_ready"], HK * (c - 1) + m + 1)
                        cols = slice(m * P, (m + 1) * P)
                        mm3(bank[1 + m][:], w1h[:, cols], w1l[:, cols], xTh[:, c, :], xTl[:, c, :], True,
                            True).then_inc(B["g1_done"], 1)
                if 1 <= c <= C:
                    if c >= 3:
                        nc.tensor.wait_ge(B["y_copied"], c - 2)
                    for m in range(HK):
                        q, cols = (c - 1) % 2, slice(m * P, (m + 1) * P)
                        nc.tensor.wait_ge(B["mlp_hi"], (HK + 1) * (c - 1) + m + 2)
                        if m:
                            nc.tensor.wait_ge(B["mlp_lo"], (HK - 1) * (c - 1) + m)
                        ins = mm3(bank[5 + q][:], w2h[:, cols], w2l[:, cols], hh[:, q, m, :], hl[:, q, m, :],
                                  m == 0, m == HK - 1)
                    ins.then_inc(B["y_done"], 1)
                if c >= 2:
                    nc.tensor.wait_ge(B["y_copied"], c - 1)
                    if c >= 3:
                        nc.tensor.wait_ge(x_ready, C + c - 2)
                    for j in range(JT):
                        ins = nc.tensor.transpose(bank[7][:, j * P:(j + 1) * P],
                                                  yfm[:, (c - 2) % 2, j * P:(j + 1) * P], ident[:])
                    ins.then_inc(B["yt_done"], 1)

        comb = arena[:, 4:12, :]
        disp = arena[:, 12:20, :]
        dTh, dTl = hh[:, 0], hl[:, 0]
        xnh, xnl = hh[:, 1], hl[:, 1]
        combT = arena[:, 24:40, :]
        hid_s = arena[:, 8:12, :].rearrange("p (q h) (b n) -> p q (h b) n", q=2, b=2)
        eoT = arena[:, 16:20, :]
        eo = arena[:, 20:24, :].rearrange("p c (s d) -> p c s d", d=P)

        snh, snl = wh[0][:, 0, :], wl[0][:, 0, :]

        def turn_bank(b, j):
            return bank[(4, 5, 7)[(8 * b + j) % 3]]

        def soft_weights(e, which):
            if e < 2:
                return wraw[e][:, which, :]
            return arena[:, (0, 4, 12)[e // 2 - 1] + 2 * (e % 2) + which, :]

        def soft_sems(n):
            names = ("xh_ready xt_turned xt_ready lg_done nm_ready exp_done dt_ready tr_done ct_ready d_ready "
                     "slots_done slots_ready xt_lo g1_done hf_ready y_done eot_ready eo_turned eo_ready out_done").split()
            return {k: sem(f"{k}_{n}") for k in names}

        F = [soft_sems("soft0"), soft_sems("soft1")]
        soft_w = sem("soft_w")
        xn_split = sem("xn_split")
        d_split = sem("d_split")
        slots_ld = sem("slots_ld")
        sn_step = sem("sn_step")

        def slots_dve():
            se = U[:, 0:JT, :]
            nc.vector.wait_ge(slots_ld, 16)
            for t in range(JT):
                last = nc.vector.bn_stats(stats[:, t, :], se[:, t, :])
            link(last)
            for t in range(JT):
                last = nc.vector.bn_aggr(mv[:, t, :], stats[:, t, :])
            link(last)
            r = [rs[:, k, 0:JT] for k in range(3)]
            link(nc.vector.tensor_tensor(r[1], mv[:, 0:JT, 0], mv[:, 0:JT, 0], ALU.mult))
            link(nc.vector.tensor_tensor(r[1], r[1], mv[:, 0:JT, 1], ALU.add))
            link(nc.vector.tensor_scalar(r[1], r[1], float(P), 1e-30, ALU.mult, ALU.max))
            dve_rsqrt(r[0], r[1], r[2])
            link(nc.vector.tensor_scalar(r[0], r[0], 1e12, SCALE, ALU.min, ALU.mult))
            for t in range(JT):
                nc.vector.tensor_scalar(U[:, JT + t, :], se[:, t, :], rs[:, 0, t:t + 1], None,
                                        ALU.mult).then_inc(sn_step, 1)

        def slots_pe():
            nc.tensor.wait_ge(sn_step, JT)
            for t in range(JT):
                ins = nc.tensor.transpose(bank[7][:, t * P:(t + 1) * P], U[:, JT + t, :], ident[:])
            ins.then_inc(sn_step, 1)

        def biases_dve():
            nc.vector.wait_ge(bias_step, 1)
            nc.vector.tensor_copy(vcols[:], bank[7][:, E:E + n_cols]).then_inc(bias_step, 1)
            nc.vector.tensor_copy(gw[:, 0:E], bank[7][:, 0:E]).then_inc(bias_step, 1)
            nc.vector.wait_ge(bias_step, 3)
            nc.vector.tensor_tensor(gw[:, E:2 * E], bank[7][:, 0:E], gw[:, 0:E].bitcast(F32),
                                    ALU.subtract).then_inc(bias_step, 1)

        def biases_pe():
            nc.tensor.wait_ge(s_small, 16 * (2 + len(COLS)))
            nc.tensor.transpose(bank[7][:, E:E + n_cols], vrows[:], ident[0:n_cols, 0:n_cols])
            nc.tensor.transpose(bank[7][:, 0:E], gwraw[:], ident[0:E, 0:E]).then_inc(bias_step, 1)

        def slots_act():
            nc.scalar.wait_ge(bias_step, 2)
            nc.scalar.wait_ge(sn_step, JT + 1)
            nc.scalar.activation(snT[:], bank[7][:], ACT.Copy, scale=col("slot_gamma")).then_inc(sn_step, 1)

        def soft_dve(S, at, whole):
            ln = LN_SOFT1 if whole else LN_SOFT0
            if whole:
                norm_rows(ln, 0)

            def low_part(c):
                nc.vector.wait_ge(S["xt_ready"], c + 1)
                nc.vector.scalar_tensor_tensor(out=xTl[:, c, :], in0=bank[4 + c][:], scalar=col("gamma"),
                                               in1=xTh[:, c, :].bitcast(F32), op0=ALU.mult,
                                               op1=ALU.subtract).then_inc(S["xt_lo"], 1)

            low_part(0)
            norm_rows(ln, 1 if whole else C - 1)
            if not whole:
                nc.vector.wait_ge(sn_step, JT + 3)
                nc.vector.tensor_tensor(snl, snT[:], snh.bitcast(F32), ALU.subtract).then_inc(sn_step, 1)

            def maxima(b):
                for k in range(8):
                    nc.vector.wait_ge(S["lg_done"], 8 * b + k + 1)
                    nc.vector.tensor_reduce(nmax[:, b, k:k + 1], bank[k % 4][:], AX_X, ALU.max,
                                            negate=True).then_inc(S["nm_ready"], 1)

            def scale_dispatch(b):
                nc.vector.wait_ge(S["exp_done"], 8 * b + 8)
                link(nc.vector.reciprocal(sums[:, b, 4:8], sums[:, b, 4:8]))
                for st in range(4):
                    d = disp[:, 4 * (b % 2) + st, :]
                    nc.vector.tensor_scalar(d, d, sums[:, b, 4 + st:5 + st], None, ALU.mult).then_inc(S["dt_ready"], 1)

            maxima(0)
            if whole:
                norm_rows(ln, 2)
                norm_rows(ln, 3)
            for c in range(1, C):
                low_part(c)
            scale_dispatch(0)
            for b in range(C):
                if b < C - 1:
                    maxima(b + 1)
                for st in range(4):
                    nc.vector.wait_ge(S["tr_done"], 8 * b + st + 1)
                    nc.vector.tensor_copy(combT[:, 4 * b + st, :], turn_bank(b, st)[:]).then_inc(S["ct_ready"], 1)
                for nt in range(JT):
                    nc.vector.wait_ge(S["d_ready"], JT * b + nt + 1)
                    nc.vector.tensor_tensor(dTl[:, nt, :], turn_bank(b, 4 + nt)[:], dTh[:, nt, :].bitcast(F32),
                                            ALU.subtract).then_inc(d_split, 1)
                if b < C - 1:
                    scale_dispatch(b + 1)
            link(nc.vector.reciprocal(sums[:, :, 0:4], sums[:, :, 0:4]))
            link(nc.vector.tensor_scalar(sums[:, :, 0:4], sums[:, :, 0:4], 0.5, None, ALU.mult))
            for e in range(E):
                nc.vector.wait_ge(S["y_done"], e + 1)
                dst = eoT[:, :, e * S_PER:(e + 1) * S_PER]
                nc.vector.tensor_scalar(dst, bank[4 + e % 2][:, 0:NB].rearrange("p (b s) -> p b s", b=C),
                                        cols_of("b2_1")[:, e:e + 1], None, ALU.add).then_inc(S["eot_ready"], 1)
            for c in range(C):
                nc.vector.wait_ge(S["out_done"], c + 1)
                for j in range(JT):
                    t = JT * c + j
                    ins = nc.vector.scalar_tensor_tensor(
                        out=X[:, t, :], in0=bank[c][:, j * P:(j + 1) * P], scalar=sums[:, c, j:j + 1],
                        in1=X[:, t, :], op0=ALU.mult, op1=ALU.add)
                ins.then_inc(x_ready, 1)
                if not whole:
                    x_done(c, at + C + c + 1, LN_DELTA)

        def soft_act(S):
            def high_part(c):
                nc.scalar.wait_ge(S["xt_turned"], c + 1)
                nc.scalar.activation(xTh[:, c, :], bank[4 + c][:], ACT.Copy, scale=col("gamma")
                                     ).then_inc(S["xt_ready"], 1)

            high_part(0)
            if S is F[0]:
                nc.scalar.activation(snh, snT[:], ACT.Copy).then_inc(sn_step, 1)

            def exps(b):
                for k in range(8):
                    nc.scalar.wait_ge(S["nm_ready"], 8 * b + k + 1)
                    if b >= 2:
                        nc.scalar.wait_ge(S["tr_done"], 8 * (b - 2) + (4 if k < 4 else 8))
                    dst = (comb if k < 4 else disp)[:, 4 * (b % 2) + k % 4, :]
                    nc.scalar.activation(dst, bank[k % 4][:], ACT.Exp, bias=nmax[:, b, k:k + 1],
                                         accum_out=sums[:, b, k:k + 1]).then_inc(S["exp_done"], 1)

            exps(0)
            for c in range(1, C):
                high_part(c)
            for b in range(C):
                if b < C - 1:
                    exps(b + 1)
                for nt in range(JT):
                    nc.scalar.wait_ge(S["tr_done"], 8 * b + 4 + nt + 1)
                    if b >= 1:
                        nc.scalar.wait_ge(S["slots_done"], b)
                    nc.scalar.activation(dTh[:, nt, :], turn_bank(b, 4 + nt)[:], ACT.Copy).then_inc(S["d_ready"], 1)
                nc.scalar.wait_ge(S["slots_done"], b + 1)
                nc.scalar.activation(slotsT[:, :, b, :], bank[6][:].rearrange("p (e s) -> p e s", e=E), ACT.Copy,
                                     scale=col("gamma")).then_inc(S["slots_ready"], 1)
            for e in range(E):
                if e >= 2:
                    nc.scalar.wait_ge(S["y_done"], e - 1)
                for m in range(HK):
                    nc.scalar.wait_ge(S["g1_done"], HK * e + m + 1)
                    nc.scalar.activation(hid_s[:, e % 2, m, :], bank[m][:, 0:NB],
                                         ACT.Gelu, bias=cols_of("b1_1")[:, HK * e + m:HK * e + m + 1]).then_inc(S["hf_ready"], 1)
            for c in range(C):
                nc.scalar.wait_ge(S["eo_turned"], c + 1)
                nc.scalar.activation(eo[:, c, :, :], bank[6 + c % 2][:].rearrange("p (s d) -> p s d", d=P),
                                     ACT.Copy).then_inc(S["eo_ready"], 1)

        def soft_pool(S):
            at = 0 if S is F[0] else 2 * C
            for c in range(C):
                src = XH[:, tiles(c), :].rearrange("p t d -> p (t d)")
                nc.gpsimd.wait_ge(S["xh_ready"], JT * c + JT)
                nc.gpsimd.tensor_copy(xnh[:, c, :], src).then_inc(xn_split, 1)
                nc.gpsimd.wait_ge(xn_split, at + 2 * c + 1)
                nc.gpsimd.tensor_tensor(xnl[:, c, :], src, xnh[:, c, :].bitcast(F32), ALU.subtract).then_inc(xn_split, 1)

        def soft_pe(S):
            d_at = 0 if S is F[0] else JT * C

            def turn(c):
                for j in range(JT):
                    nc.tensor.wait_ge(S["xh_ready"], JT * c + j + 1)
                    ins = nc.tensor.transpose(bank[4 + c][:, j * P:(j + 1) * P], XH[:, JT * c + j, :], ident[:])
                ins.then_inc(S["xt_turned"], 1)

            turn(0)
            nc.tensor.wait_ge(sn_step, JT + 4)

            def logits(b):
                nc.tensor.wait_ge(S["xt_lo"], b + 1)
                for k in range(8):
                    n = 8 * b + k
                    if n >= 4:
                        nc.tensor.wait_ge(S["exp_done"], n - 3)
                    blk = slice((k % 4) * P, (k % 4 + 1) * P)
                    if k < 4:
                        ins = mm3(bank[k][:], xTh[:, b, blk], xTl[:, b, blk], snh, snl, True, True)
                    else:
                        ins = mm3(bank[k - 4][:], snh[:, blk], snl[:, blk], xTh[:, b, :], xTl[:, b, :], True, True)
                    ins.then_inc(S["lg_done"], 1)

            logits(0)
            for c in range(1, C):
                turn(c)
            for b in range(C):
                if b < C - 1:
                    logits(b + 1)
                if b == 0:
                    nc.tensor.wait_ge(S["xt_lo"], C)
                for j in range(8):
                    b_, j_ = divmod(8 * b + j - 3, 8)
                    if b_ >= 0 and j_ < 4:
                        nc.tensor.wait_ge(S["ct_ready"], 4 * b_ + j_ + 1)
                    elif b_ >= 0:
                        nc.tensor.wait_ge(d_split, d_at + 4 * b_ + j_ % 4 + 1)
                    if j < 4:
                        nc.tensor.wait_ge(S["exp_done"], 8 * b + 4)
                    else:
                        nc.tensor.wait_ge(S["dt_ready"], 4 * b + 4)
                    src = comb if j < 4 else disp
                    for k in range(4):
                        ins = nc.tensor.transpose(turn_bank(b, j)[:, k * P:(k + 1) * P],
                                                  src[:, 4 * (b % 2) + k, (j % 4) * P:(j % 4 + 1) * P], ident[:])
                    ins.then_inc(S["tr_done"], 1)
                if b >= 1:
                    nc.tensor.wait_ge(S["slots_ready"], b)
                nc.tensor.wait_ge(xn_split, (0 if S is F[0] else 2 * C) + 2 * b + 2)
                for nt in range(JT):
                    nc.tensor.wait_ge(d_split, d_at + JT * b + nt + 1)
                    cols = slice(nt * P, (nt + 1) * P)
                    ins = mm3(bank[6][:], xnh[:, b, cols], xnl[:, b, cols], dTh[:, nt, :], dTl[:, nt, :], nt == 0,
                              nt == JT - 1)
                ins.then_inc(S["slots_done"], 1)

            def g1(e):
                w1 = soft_weights(e, 0)
                if e in (0, 4):
                    nc.tensor.wait_ge(soft_w, soft_loads(S, e))
                for m in range(HK):
                    if e >= 1:
                        nc.tensor.wait_ge(S["hf_ready"], HK * (e - 1) + m + 1)
                    nc.tensor.matmul(bank[m][:, 0:NB], w1[:, m * P:(m + 1) * P],
                                     slotsT[:, e, :, :], start=True, stop=True).then_inc(S["g1_done"], 1)

            nc.tensor.wait_ge(S["slots_ready"], C)
            nc.tensor.wait_ge(S["exp_done"], 8 * C)
            nc.tensor.wait_ge(S["ct_ready"], 4 * C)
            g1(0)
            for e in range(E):
                if e < E - 1:
                    g1(e + 1)
                if e >= 2:
                    nc.tensor.wait_ge(S["eot_ready"], e - 1)
                w2 = soft_weights(e, 1)
                for m in range(HK):
                    nc.tensor.wait_ge(S["hf_ready"], HK * e + m + 1)
                    ins = nc.tensor.matmul(bank[4 + e % 2][:, 0:NB], w2[:, m * P:(m + 1) * P],
                                           hid_s[:, e % 2, m, :], start=(m == 0), stop=(m == HK - 1))
                ins.then_inc(S["y_done"], 1)
            nc.tensor.wait_ge(S["eot_ready"], E)
            for c in range(C):
                if c >= 2:
                    nc.tensor.wait_ge(S["eo_ready"], c - 1)
                for k in range(4):
                    ins = nc.tensor.transpose(bank[6 + c % 2][:, k * P:(k + 1) * P], eoT[:, c, k * P:(k + 1) * P], ident[:])
                ins.then_inc(S["eo_turned"], 1)
            for c in range(C):
                nc.tensor.wait_ge(S["eo_ready"], c + 1)
                for nt in range(JT):
                    for k in range(4):
                        ins = nc.tensor.matmul(bank[c][:, nt * P:(nt + 1) * P], combT[:, 4 * c + k, nt * P:(nt + 1) * P],
                                               eo[:, c, k, :], start=(k == 0), stop=(k == 3))
                ins.then_inc(S["out_done"], 1)

        def soft_loads(S, e):
            return 2 * 16 * ((4 if S is F[0] else E + 2) + (4 if e >= 4 else 0))

        def soft_sp(S):
            w1, w2 = A["L1_ffn_w1"], A["L1_ffn_w2"].rearrange("e (m h) d -> e h m d", h=P)

            def load(e):
                nc.sync.dma_start(soft_weights(e, 0), w1[e]).then_inc(soft_w, 16)
                nc.sync.dma_start(soft_weights(e, 1).rearrange("p (m d) -> p m d", d=P), w2[e]).then_inc(soft_w, 16)

            if S is F[0]:
                nc.sync.wait_ge(M[1]["w_split"], 2 * E)
                load(0)
                load(1)
            nc.sync.wait_ge(x_ready, (3 if S is F[0] else 5) * C)
            load(2)
            load(3)
            nc.sync.wait_ge(soft_w, soft_loads(S, 0))
            nc.sync.wait_ge(S["tr_done"], 8 * 3)
            for e in range(4, E):
                load(e)

        N5 = LAYERS * JT
        NK = len(FB)
        flat = "p a n -> p (a n)"
        hT, oT, h2T = (arena[:, k, :] for k in range(3))
        sgate = arena[:, 3:6, :]
        gact = arena[:, 6:9, :]
        qkv = [arena[:, a:a + 3, :].rearrange(flat).rearrange("p (t r) -> p t r", t=C) for a in (9, 12)]
        sq = arena[:, 15:17, :].rearrange(flat)
        prod = arena[:, 17:21, :].rearrange(flat).rearrange("p (x n) -> p x n", n=P)
        parts = arena[:, 21, :].rearrange("p (x n) -> p x n", n=P)
        late = arena[:, 24, :].rearrange("p (x n) -> p x n", n=P)
        u5 = [arena[:, a, :].rearrange("p (t n) -> p t n", n=P) for a in (22, 23)]
        th = sb("th", [P, 2, C, H])
        coef = sb("coef", [P, 2, 16, H])
        NQ, NO = 2 * C * H, C * H
        small5 = gsm[:].rearrange("p z t e -> p (z t e)")[:, 0:3 * (NQ + NO)].rearrange("p (z n) -> p z n", z=3)
        junk = [z[:].rearrange("p a b -> p (a b)") for z in (G, WE)]
        ssq = sb("ssq", [P, 3, C])
        nhalf = sb("nhalf", [P, T])
        X5, U5, XH5 = (z[:].rearrange("p (t j) d -> p t j d", j=JT) for z in (X, U, XH))
        KK_AT = [0, 3, 5]
        KQ_AT = [6, 10, 13, 15]
        D5 = {k: sem(k + "_delta") for k in (
            "u_ready squared rms_ready xh_ready xh2_ready turned cols_ready qkv_done qkv_ready sq_ready qk_scaled "
            "vb_ready kq_ready coef_ready step_ready o_raw o_ready wo_done gy_done sg_ready act_ready wd_done "
            "beta_ready").split()}
        ROUNDS = range(-2, N5 + 2)

        def item(n, first=0):
            return first <= n < N5

        TURNS = [z for r in ROUNDS for z in (("o", r - 1), ("h", r + 1), ("x", r - 1)) if item(z[1])]
        NORMS = [z for r in ROUNDS for z in (("x", r - 1), ("h", r + 2), ("f", r - 2))
                 if item(z[1], N5 - JT if z[0] == "f" else 0)]
        ADDS = [z for r in ROUNDS for z in (("out", r - 1), ("mlp", r - 2)) if item(z[1])]
        GY = [(6, 7), (2, 3), (6, 7)]

        def turns(what, n):
            return TURNS.index((what, n)) + 1

        def norms(what, n):
            return NORMS.index((what, n)) + 1

        def u_at(what, n):
            return T + ADDS.index((what, n)) + 1

        def tile5(z, n, t):
            return z[:, JT * t + n % JT, :]

        def hk(ap):
            return ap.rearrange("p m (g k) -> p m g k", k=DK)

        def spread(n, at_, m):
            return coef[:, n % 2, at_:at_ + m].unsqueeze(3).to_broadcast([P, m, H, DK])

        WHICH = {"h": 0, "x": 1, "f": 2}

        def delta_dve():
            norm_rows(LN_DELTA, C - 1)
            nc.vector.wait_ge(D5["u_ready"], T)

            def sum_squares(n):
                nc.vector.wait_ge(D5["sq_ready"], n + 1)
                link(nc.vector.tensor_reduce(small5[:, 0, 0:NQ], sq.rearrange("p (g k) -> p g k", k=DK), AX_X, ALU.add))

            def norm_heads(n):
                m = n - 1
                lo, hi = (0 if item(n) else NQ), (NQ + NO if item(m) else NQ)
                ss, r, t_ = (small5[:, k, lo:hi] for k in range(3))
                ss_o, r_o = (small5[:, k, NQ:NQ + NO] for k in range(2))
                r_q = small5[:, 1, 0:NQ]
                if item(m):
                    nc.vector.wait_ge(D5["o_raw"], m + 1)
                    o = hk(XH5[:, :, m % JT, :])
                    link(nc.vector.tensor_tensor(o[:, 2:], o[:, 2:], hk(late[:, 0:2]), ALU.add))
                    link(nc.vector.tensor_tensor(hk(prod[:, 0:C]), o, o, ALU.mult))
                    link(nc.vector.tensor_reduce(ss_o.rearrange("p (t h) -> p t h", t=C), hk(prod[:, 0:C]), AX_X, ALU.add))
                    link(nc.vector.tensor_scalar(ss_o, ss_o, 1.0 / DK, None, ALU.mult))
                link(nc.vector.tensor_scalar(ss, ss, 1e-6, None, ALU.add))
                dve_rsqrt(r, ss, t_)
                if item(n):
                    qk = qkv[n % 2][:, :, 0:2 * P].rearrange("p t (g k) -> p t g k", k=DK)
                    nc.vector.tensor_tensor(qk, qk, r_q.rearrange("p (t g) -> p t g", t=C).unsqueeze(3).to_broadcast(
                        [P, C, 2 * H, DK]), ALU.mult).then_inc(D5["qk_scaled"], 1)
                if item(m):
                    nc.vector.tensor_tensor(o, o, r_o.rearrange("p (t h) -> p t h", t=C).unsqueeze(3).to_broadcast(
                        [P, C, H, DK]), ALU.mult).then_inc(D5["o_ready"], 1)

            def solve(n):
                nc.vector.wait_ge(D5["qk_scaled"], n + 1)
                k = qkv[n % 2][:, :, P:2 * P]
                for s_ in range(C - 1):
                    m = C - 1 - s_
                    last = nc.vector.tensor_tensor(prod[:, KK_AT[s_]:KK_AT[s_] + m], k[:, s_ + 1:],
                                                   k[:, s_:s_ + 1].to_broadcast([P, m, P]), ALU.mult)
                link(last)
                link(nc.vector.tensor_reduce(coef[:, n % 2, 0:6], hk(prod[:, 0:6]), AX_X, ALU.add))
                if item(n - 2):
                    gated(n - 2, (0,))
                nc.vector.wait_ge(D5["beta_ready"], n + 1)
                for s_ in range(C - 1):
                    a = coef[:, n % 2, KK_AT[s_]:KK_AT[s_] + C - 1 - s_]
                    last = nc.vector.tensor_tensor(a, a, th[:, n % 2, s_ + 1:], ALU.mult)
                link(last)
                nc.vector.wait_ge(D5["vb_ready"], n + 1)
                tmp5 = hk(prod[:, 0:3])
                u = hk(u5[n % 2])
                for s_ in range(C - 1):
                    m = C - 1 - s_
                    link(nc.vector.tensor_tensor(tmp5[:, 0:m], spread(n, KK_AT[s_], m),
                                                 u[:, s_:s_ + 1].to_broadcast([P, m, H, DK]), ALU.mult))
                    nc.vector.tensor_tensor(u[:, s_ + 1:], u[:, s_ + 1:], tmp5[:, 0:m],
                                            ALU.subtract).then_inc(D5["step_ready"], 1)
                    if s_ < C - 2:
                        nc.vector.wait_ge(D5["step_ready"], (C - 1) * n + s_ + 1)

            def query_coefs(n):
                nc.vector.wait_ge(D5["kq_ready"], n + 1)
                nc.vector.tensor_reduce(coef[:, n % 2, 6:16], hk(prod[:, 6:16]), AX_X, ALU.add
                                        ).then_inc(D5["coef_ready"], 1)

            def late_outputs(n):
                nc.vector.wait_ge(D5["coef_ready"], n + 1)
                u, part = hk(u5[n % 2]), hk(late)
                nc.vector.tensor_tensor(part[:, 0:2], spread(n, KQ_AT[2], 2), u[:, 2:3].to_broadcast([P, 2, H, DK]), ALU.mult)
                link(nc.vector.tensor_tensor(part[:, 2:3], spread(n, KQ_AT[3], 1), u[:, 3:4], ALU.mult))
                link(nc.vector.tensor_tensor(part[:, 1:2], part[:, 1:2], part[:, 2:3], ALU.add))

            def add_psum(n, b):
                u = U5[:, :, n % JT, :]
                nc.vector.tensor_tensor(u, u, bank[b][:].rearrange("p (t n) -> p t n", t=C), ALU.add
                                        ).then_inc(D5["u_ready"], 1)

            def gated(n, blocks):
                for k in blocks:
                    w = FB[k][1]
                    nc.vector.wait_ge(D5["sg_ready"], NK * n + k + 1)
                    nc.vector.tensor_tensor(gact[0:w, k, :], bank[GY[k][1]][0:w, :],
                                            sgate[0:w, k, :], ALU.mult).then_inc(D5["act_ready"], 1)
            def finish(n):
                nc.vector.wait_ge(D5["rms_ready"], norms("f", n))
                for t in range(C):
                    last = nc.vector.scalar_tensor_tensor(out=tile5(XH, n, t), in0=tile5(U, n, t),
                                                          scalar=ssq[:, 2, t:t + 1], in1=final_row[:],
                                                          op0=ALU.mult, op1=ALU.mult)
                link(last)
                x = X5[:, :, n % JT, :]
                nc.vector.tensor_tensor(x, x, XH5[:, :, n % JT, :], ALU.add).then_inc(x_ready, 1)
                nc.vector.wait_ge(x_ready, 4 * C + n - (N5 - JT) + 1)
                for t in range(C):
                    tt = JT * t + n % JT
                    last = nc.vector.bn_stats(stats[:, tt, :], X[:, tt, :])
                link(last)

            for r in ROUNDS:
                if item(r) or item(r - 1):
                    norm_heads(r)
                if item(r):
                    solve(r)
                elif item(r - 2):
                    gated(r - 2, (0,))
                if item(r - 1):
                    nc.vector.wait_ge(D5["wo_done"], r)
                    add_psum(r - 1, 1)
                if item(r):
                    query_coefs(r)
                if item(r - 2):
                    gated(r - 2, (1, 2))
                if item(r):
                    late_outputs(r)
                if item(r + 1):
                    sum_squares(r + 1)
                if item(r - 2):
                    nc.vector.wait_ge(D5["wd_done"], r - 1)
                    add_psum(r - 2, 2)
                if item(r - 2, N5 - JT):
                    finish(r - 2)
            for c in range(C):
                norm_aggr(c)

        def delta_act():
            def squares(what, n):
                before = C * (norms(what, n) - 1)
                for t in range(C):
                    if before + t >= 2:
                        nc.scalar.wait_ge(D5["squared"], before + t - 1)
                    nc.scalar.activation(junk[t % 2], tile5(U, n, t), ACT.Square,
                                         accum_out=ssq[:, WHICH[what], t:t + 1]).then_inc(D5["squared"], 1)

            def copy_cols(dst, what, n, weights):
                nc.scalar.wait_ge(D5["turned"], turns(what, n))
                nc.scalar.activation(dst, bank[1 if what == "o" else 0][:], ACT.Copy,
                                     scale=col(weights, n // JT)).then_inc(D5["cols_ready"], 1)

            def project(n):
                if n >= 2:
                    nc.scalar.wait_ge(D5["coef_ready"], n - 1)
                for t in range(C):
                    nc.scalar.wait_ge(D5["qkv_done"], C * n + t + 1)
                    src = bank[4 + t % 2]
                    nc.scalar.activation(qkv[n % 2][:, t, :], src[:, 0:3 * P], ACT.Silu)
                    nc.scalar.activation(th[:, n % 2, t, :], src[:, 3 * P:3 * P + H], ACT.Tanh,
                                         scale=0.5).then_inc(D5["qkv_ready"], 1)
                nc.scalar.wait_ge(D5["qkv_ready"], C * n + C)
                if n >= 1:
                    nc.scalar.wait_ge(D5["qk_scaled"], n)
                nc.scalar.activation(sq.rearrange("p (t n) -> p t n", t=C), qkv[n % 2][:, :, 0:2 * P],
                                     ACT.Square).then_inc(D5["sq_ready"], 1)

            def scale_rows(what, n, done):
                nc.scalar.wait_ge(D5["rms_ready"], norms(what, n))
                for t in range(C):
                    nc.scalar.activation(tile5(XH, n, t), tile5(U, n, t), ACT.Copy,
                                         scale=ssq[:, WHICH[what], t:t + 1]).then_inc(done, 1)

            def silus(m, blocks):
                for k in blocks:
                    w = FB[k][1]
                    nc.scalar.wait_ge(D5["gy_done"], NK * m + k + 1)
                    if m >= 1:
                        nc.scalar.wait_ge(D5["act_ready"], NK * (m - 1) + k + 1)
                    nc.scalar.activation(sgate[0:w, k, :], bank[GY[k][0]][0:w, :],
                                         ACT.Silu).then_inc(D5["sg_ready"], 1)

            for r in ROUNDS:
                if item(r - 2):
                    silus(r - 2, (0, 1))
                if item(r - 1):
                    copy_cols(oT, "o", r - 1, "onorm")
                if item(r + 1):
                    copy_cols(hT, "h", r + 1, "r1w")
                if item(r - 2):
                    silus(r - 2, (2,))
                if item(r - 1):
                    nc.scalar.wait_ge(D5["u_ready"], u_at("out", r - 1))
                    squares("x", r - 1)
                if item(r + 1):
                    project(r + 1)
                if item(r - 1):
                    scale_rows("x", r - 1, D5["xh2_ready"])
                    copy_cols(h2T, "x", r - 1, "r2w")
                if item(r + 2):
                    nc.scalar.wait_ge(D5["u_ready"], u_at("mlp", r + 2 - JT) if r + 2 >= JT else T)
                    squares("h", r + 2)
                if item(r - 2, N5 - JT):
                    nc.scalar.wait_ge(D5["u_ready"], u_at("mlp", r - 2))
                    if item(r - 3, N5 - JT):
                        nc.scalar.wait_ge(x_ready, 4 * C + r - 2 - (N5 - JT))
                    squares("f", r - 2)
                if item(r + 2):
                    scale_rows("h", r + 2, D5["xh_ready"])

        def delta_pool():
            def factors(what, n):
                nc.gpsimd.wait_ge(D5["squared"], C * norms(what, n))
                v = ssq[:, WHICH[what], :]
                plink(nc.gpsimd.tensor_scalar(v, v, 1.0 / P, 1e-6, ALU.mult, ALU.add))
                nc.gpsimd.tensor_tensor(v, v, nhalf[:, 0:C], ALU.pow).then_inc(D5["rms_ready"], 1)

            def beta_v(n):
                nc.gpsimd.wait_ge(D5["sq_ready"], n + 1)
                b = th[:, n % 2]
                nc.gpsimd.tensor_scalar(b, b, 1.0, None, ALU.add).then_inc(D5["beta_ready"], 1)
                nc.gpsimd.wait_ge(D5["beta_ready"], n + 1)
                nc.gpsimd.tensor_tensor(hk(u5[n % 2]), hk(qkv[n % 2][:, :, 2 * P:3 * P]),
                                        b.unsqueeze(3).to_broadcast([P, C, H, DK]), ALU.mult
                                        ).then_inc(D5["vb_ready"], 1)

            def query_products(n):
                nc.gpsimd.wait_ge(D5["qk_scaled"], n + 1)
                if n >= 1:
                    nc.gpsimd.wait_ge(D5["coef_ready"], n)
                q, k = (qkv[n % 2][:, :, z * P:(z + 1) * P] for z in (0, 1))
                for s_ in range(C):
                    m = C - s_
                    ins = nc.gpsimd.tensor_tensor(prod[:, KQ_AT[s_]:KQ_AT[s_] + m], q[:, s_:],
                                                  k[:, s_:s_ + 1].to_broadcast([P, m, P]), ALU.mult)
                ins.then_inc(D5["kq_ready"], 1)

            def outputs(n):
                nc.gpsimd.wait_ge(D5["coef_ready"], n + 1)
                u = hk(u5[n % 2])
                o = hk(XH5[:, :, n % JT, :])
                part = hk(parts)
                plink(nc.gpsimd.tensor_tensor(o, spread(n, KQ_AT[0], C), u[:, 0:1].to_broadcast([P, C, H, DK]), ALU.mult))
                plink(nc.gpsimd.tensor_tensor(part[:, 0:C - 1], spread(n, KQ_AT[1], C - 1),
                                              u[:, 1:2].to_broadcast([P, C - 1, H, DK]), ALU.mult))
                nc.gpsimd.tensor_tensor(o[:, 1:], o[:, 1:], part[:, 0:C - 1], ALU.add).then_inc(D5["o_raw"], 1)

            for r in ROUNDS:
                if item(r):
                    beta_v(r)
                    query_products(r)
                if item(r - 1):
                    factors("x", r - 1)
                if item(r):
                    outputs(r)
                if item(r + 2):
                    factors("h", r + 2)
                if item(r - 2, N5 - JT):
                    factors("f", r - 2)

        def delta_pe():
            def turn(what, n, rows_ready, done):
                k = turns(what, n) - 1
                b = bank[1 if what == "o" else 0]
                if what == "o":
                    if n >= 1:
                        nc.tensor.wait_ge(D5["u_ready"], u_at("out", n - 1))
                elif k >= 1:
                    nc.tensor.wait_ge(D5["cols_ready"], max(i + 1 for i in range(k) if TURNS[i][0] != "o"))
                for t in range(C):
                    if what != "o":
                        nc.tensor.wait_ge(rows_ready, done + t + 1)
                    elif t == 0:
                        nc.tensor.wait_ge(rows_ready, done + 1)
                    ins = nc.tensor.transpose(b[:, t * P:(t + 1) * P], tile5(XH, n, t), ident[:])
                ins.then_inc(D5["turned"], 1)

            def project(n):
                nc.tensor.wait_ge(D5["cols_ready"], turns("h", n))
                for t in range(C):
                    k = C * n + t
                    if k >= 2:
                        nc.tensor.wait_ge(D5["qkv_ready"], k - 1)
                    nc.tensor.matmul(bank[4 + t % 2][:, 0:3 * P + H], hT[:, t * P:(t + 1) * P], qkvb[:, n // JT, :],
                                     start=True, stop=True).then_inc(D5["qkv_done"], 1)

            def gated(n, blocks):
                lay = n // JT
                nc.tensor.wait_ge(D5["cols_ready"], turns("x", n))
                for k in blocks:
                    at_, w = FB[k]
                    if k == 2:
                        nc.tensor.wait_ge(D5["act_ready"], NK * n + 1)
                    elif n >= 1 and k == 0:
                        nc.tensor.wait_ge(D5["act_ready"], NK * n)
                    elif n >= 1:
                        nc.tensor.wait_ge(D5["u_ready"], u_at("mlp", n - 1))
                    g, y = GY[k]
                    nc.tensor.matmul(bank[g][0:w, :], wg[:, lay, at_:at_ + w], h2T, start=True, stop=True)
                    nc.tensor.matmul(bank[y][0:w, :], wg[:, lay, FF + at_:FF + at_ + w], h2T, start=True,
                                     stop=True).then_inc(D5["gy_done"], 1)

            def down(n):
                nc.tensor.wait_ge(D5["act_ready"], NK * n + NK)
                for t in range(C):
                    for m, (_, w) in enumerate(FB):
                        ins = nc.tensor.matmul(bank[2][:, t * P:(t + 1) * P], gact[0:w, m, t * P:(t + 1) * P],
                                               wd[0:w, n // JT, m, :], start=(m == 0), stop=(m == NK - 1))
                ins.then_inc(D5["wd_done"], 1)

            nc.tensor.wait_ge(attn_w, 16 * (W0_LOADS + W1_LOADS))
            for r in ROUNDS:
                if item(r - 2):
                    gated(r - 2, (0, 1))
                if item(r - 1):
                    turn("o", r - 1, D5["o_ready"], r - 1)
                if item(r + 1):
                    turn("h", r + 1, D5["xh_ready"], C * (r + 1))
                if item(r - 1):
                    nc.tensor.wait_ge(D5["cols_ready"], turns("o", r - 1))
                    for t in range(C):
                        ins = nc.tensor.matmul(bank[1][:, t * P:(t + 1) * P], oT[:, t * P:(t + 1) * P],
                                               wo[:, (r - 1) // JT, :], start=True, stop=True)
                    ins.then_inc(D5["wo_done"], 1)
                if item(r - 2):
                    gated(r - 2, (2,))
                if item(r + 1):
                    project(r + 1)
                if item(r - 2):
                    down(r - 2)
                if item(r - 1):
                    turn("x", r - 1, D5["xh2_ready"], C * (r - 1))


        W1_LOADS = LAYERS * 8 + 1

        def delta_sp():
            nc.sync.wait_ge(attn_w, 16 * W0_LOADS)
            for k in range(LAYERS):
                for n, name in enumerate(("Wq", "Wk", "Wv")):
                    nc.sync.dma_start(qkvb[:, k, n * P:(n + 1) * P], A["L1_attn_" + name][k]).then_inc(attn_w, 16)
                nc.sync.dma_start(qkvb[:, k, 3 * P:], A["L1_attn_Wb"][k]).then_inc(attn_w, 16)
                nc.sync.dma_start(wo[:, k, :], A["L1_attn_Wo"][k]).then_inc(attn_w, 16)
                nc.sync.dma_start(wg[:, k, :], A["L1_attn_Wg"][k]).then_inc(attn_w, 16)
                nc.sync.dma_start(wd[:, k, 0:2, :], A["L1_attn_Wd"][k, 0:256, :].rearrange("(m h) d -> h m d", h=P)
                                  ).then_inc(attn_w, 16)
                nc.sync.dma_start(wd[0:96, k, 2, :], A["L1_attn_Wd"][k, 256:FF, :]).then_inc(attn_w, 16)
            nc.sync.dma_start(final_row[:], A["L1_attn_final_norm_w"].unsqueeze(0).to_broadcast([P, P])).then_inc(attn_w, 16)

        block = ctx.enter_context(nc.Block())

        @block.sync
        def _(sp):
            xin = A["L0_attn_x"].rearrange("b (j p) d -> b p j d", p=P)
            for c in range(C):
                sp.dma_start(X[:, JT * c:JT * c + JT, :], xin[c]).then_inc(s_x[c // 2], 16)
            sp.dma_start(gwraw[:], A["L0_ffn_gate_w"]).then_inc(s_small, 16)
            sp.dma_start(gb_row[:], A["L0_ffn_gate_b"].unsqueeze(0).to_broadcast([P, E])).then_inc(s_small, 16)
            for name, (at, k, ref) in COLS.items():
                if name == "onorm":
                    sp.dma_start(vrows[at:at + k, :].rearrange("k (h d) -> k h d", d=DK),
                                 A["L1_attn_onorm_w"].unsqueeze(1).to_broadcast([k, H, DK])).then_inc(s_small, 16)
                    continue
                src = A[ref]
                if len(src.shape) == 2:
                    src = src.rearrange("a b -> (a b)")
                sp.dma_start(vrows[at:at + k, :], src.rearrange("(k d) -> k d", d=P)).then_inc(s_small, 16)
            sp.dma_start(U[:, 0:JT, :], A["L1_ffn_slot_embeds"].rearrange("(t u) s d -> (u s) t d", u=2)).then_inc(slots_ld, 16)
            moe_sp(M[0], 0)
            sp.dma_start(gate_w[:], A["L0_attn_gate_w"]).then_inc(attn_w, 16)
            sp.dma_start(state_w[:], A["L0_attn_state_w"]).then_inc(attn_w, 16)
            sp.dma_start(out_w[:], A["L0_attn_out_w"]).then_inc(attn_w, 16)
            sp.dma_start(outb_row[:], A["L0_attn_out_b"].unsqueeze(0).to_broadcast([P, P])).then_inc(attn_w, 16)
            sp.dma_start(stateb_row[:], A["L0_attn_state_b"].unsqueeze(0).to_broadcast([P, P])).then_inc(attn_w, 16)
            sp.dma_start(mlp_w1[:], A["L0_attn_mlp_w1"]).then_inc(attn_w, 16)
            sp.dma_start(mlp_w2[:], A["L0_attn_mlp_w2"].rearrange("(m h) d -> h m d", h=P)).then_inc(attn_w, 16)
            delta_sp()
            moe_sp(M[1], 1)
            soft_sp(F[0])
            soft_sp(F[1])
            oout = out.rearrange("b (j p) d -> b p j d", p=P)
            for c in range(C):
                sp.wait_ge(x_ready, STAGES * C - C + c + 1)
                sp.dma_start(oout[c], X[:, JT * c:JT * c + JT, :]).then_inc(s_out, 16)
            sp.wait_ge(s_out, 16 * C)

        @block.gpsimd
        def _(pool):
            nc.gpsimd.memset(ident[:], 0.0).then_inc(s_zero, 1)
            pool.wait_ge(s_zero, 1)
            nc.gpsimd.affine_select(out=ident[:], in_=ident[:], compare_op=ALU.not_equal, fill=1.0, base=0,
                                    pattern=[[-1, P]], channel_multiplier=1).then_inc(s_const, 1)
            nc.gpsimd.memset(nhalf[:], -0.5).then_inc(s_zero, 1)
            for e in range(E):
                ins = nc.gpsimd.memset(falling[:, e:e + 1], float(E - e))
            ins.then_inc(s_const, 1)
            pool.wait_ge(s_zero, 2)
            moe_pool(M[0], 0)
            ssm_pool()
            moe_pool(M[1], 1)
            soft_pool(F[0])
            for c in range(C):
                norm_factors(LN_DELTA, c)
            delta_pool()
            for c in range(C):
                norm_factors(LN_SOFT1, c)
            soft_pool(F[1])

        @block.vector
        def _(dve):
            for c in range(C):
                dve.wait_ge(s_x[c // 2], 32)
                norm_stats(X, c)
                if c >= 1:
                    norm_rows(LN_MOE0, c - 1)
            norm_rows(LN_MOE0, C - 1)
            dve.wait_ge(s_const, 2)
            moe_dve(M[0], 0)
            ssm_dve()
            moe_dve(M[1], 1)
            soft_dve(F[0], 2 * C, False)
            delta_dve()
            soft_dve(F[1], 4 * C, True)

        @block.scalar
        def _(act):
            moe_act(M[0], 0)
            ssm_act()
            moe_act(M[1], 1)
            soft_act(F[0])
            delta_act()
            soft_act(F[1])

        @block.tensor
        def _(pe):
            pe.wait_ge(s_const, 1)
            moe_pe(M[0], 0)
            ssm_pe()
            moe_pe(M[1], 1)
            soft_pe(F[0])
            delta_pe()
            soft_pe(F[1])


def kernel(**inputs):
    import numpy as _np
    import concourse.bacc as _bacc
    from concourse import mybir as _mybir
    from concourse.bass_utils import run_bass_kernel_spmd as _run

    nc = _bacc.Bacc("TRN2", target_bir_lowering=False, num_devices=1)
    arrays, aps = {}, {}
    for name in inputs:
        a = _np.ascontiguousarray(inputs[name])
        arrays[f"in_{name}_dram"] = a
        aps[name] = nc.dram_tensor(f"in_{name}_dram", a.shape, _mybir.dt.from_np(a.dtype), kind="ExternalInput").ap()
    out = nc.dram_tensor("out_0_dram", (4, 512, 128), _mybir.dt.float32, kind="ExternalOutput").ap()
    program(nc, aps, out)
    r = _run(nc, [arrays], core_ids=[0])
    return r.results[0]["out_0_dram"]
```
